# Optimizing a Trainium2 kernel written in Bass

```python
import numpy as np
import jax
import jax.numpy as jnp

def _softmax(x, axis=-1):
    return jax.nn.softmax(x, axis=axis)

def _gelu(x):
    return jax.nn.gelu(x, approximate=True)

def _silu(x):
    return jax.nn.silu(x)

def _sigmoid(x):
    return jax.nn.sigmoid(x)

def _layernorm(x, axis=-1, eps=1e-05):
    m = jnp.mean(x, axis=axis, keepdims=True)
    v = jnp.var(x, axis=axis, keepdims=True)
    return (x - m) / jnp.sqrt(v + eps)

def _scatter_add(tgt, idx, src, axis=0):
    return tgt.at[idx].add(src)

def _segment_sum(src, seg, n):
    return jax.ops.segment_sum(src, seg, n)
kernel_name = 'mk_decoder_postln_d2_seqx_r4_a30690'

def setup_inputs(seed: int=0):
    np.random.seed(seed)
    _w = jnp.asarray

    def _rec_inputs():
        import jax
        import jax.numpy as jnp
        _rk = jax.random.key(seed)
        x = -0.0002928 + 1 * jax.random.normal(jax.random.fold_in(_rk, 1), (8, 256, 256), jnp.float32)
        _lenS = 256 - jax.random.randint(jax.random.fold_in(_rk, 7), (8,), 0, max(1, 256 // 4) + 1, jnp.int32)
        _lenS2 = 256 - jax.random.randint(jax.random.fold_in(_rk, 8), (8,), 0, max(1, 256 // 4) + 1, jnp.int32)
        _ctx_1024P = jax.random.normal(jax.random.fold_in(_rk, 11), (8, 16, 256), jnp.float32)
        _ctx_1024c = jax.random.dirichlet(jax.random.fold_in(_rk, 511), 0.3 * jnp.ones((16,), jnp.float32), (8, 256))
        _ctx_1024t = jnp.einsum('bsk,bkd->bsd', _ctx_1024c, _ctx_1024P)
        _ctx_1024t = _ctx_1024t * jax.lax.rsqrt(jnp.mean(jnp.square(_ctx_1024t)) + 1e-12) * 0.953939
        ctx_1024 = -1.39393e-06 + 0.999914 * (_ctx_1024t + 0.3 * jax.random.normal(jax.random.fold_in(_rk, 611), (8, 256, 256), jnp.float32))
        return (x, ctx_1024)
    x, ctx_1024 = _rec_inputs()

    def _L0_attn_setup():
        import jax, jax.numpy as jnp
        import numpy as np
        HEADS = 16
        NUM_LANDMARKS = 64
        PINV_ITERS = 6
        D_MODEL = 256

        def _moore_penrose_pinv(x, num_iters):
            m = x.shape[-1]
            I = jnp.eye(m, dtype=x.dtype)
            V = x
            for _ in range(num_iters):
                KV = x @ V
                V = 0.25 * V @ (13.0 * I - KV @ (15.0 * I - KV @ (7.0 * I - KV)))
            return V
        key = jax.random.key(seed)
        k1, k2, k3 = jax.random.split(key, 3)
        b, n, d = (4, 1024, D_MODEL)
        hidden_states = jax.random.normal(k1, (b, n, d), dtype=jnp.float32)
        Wqkv = jax.random.normal(k2, (d, 3 * d), dtype=jnp.float32) * 0.02
        bqkv = jnp.zeros((3 * d,), dtype=jnp.float32)
        Wout = jax.random.normal(k3, (d, d), dtype=jnp.float32) * 0.02
        bout = jnp.zeros((d,), dtype=jnp.float32)
        return {'hidden_states': hidden_states, 'Wqkv': Wqkv, 'bqkv': bqkv, 'Wout': Wout, 'bout': bout}
    _L0_attn_all = _L0_attn_setup()
    _L0_attn_in = {k: v for k, v in _L0_attn_all.items() if k in ('Wqkv', 'bqkv', 'Wout', 'bout')}
    del _L0_attn_all

    def _L0_xattn_setup():
        import jax, jax.numpy as jnp
        import numpy as np
        EMBED_DIM = 256
        NUM_HEADS = 16
        HEAD_DIM = EMBED_DIM // NUM_HEADS
        SEG_LENS = [256, 512, 1024]
        DIL_RATIOS = [1, 2, 4]
        NEG = -100000000.0

        def _branch(q, k, v, sl, dr, L):
            B = q.shape[0]
            H, D = (NUM_HEADS, HEAD_DIM)
            sl = min(sl, L)
            pad = -L % sl
            if pad:
                pw = ((0, 0), (0, pad), (0, 0), (0, 0))
                q, k, v = (jnp.pad(q, pw), jnp.pad(k, pw), jnp.pad(v, pw))
            n = (L + pad) // sl
            qs = q.reshape(B * n, sl, H, D)
            ks = k.reshape(B * n, sl, H, D)
            vs = v.reshape(B * n, sl, H, D)
            hg = H // dr
            g = sl // dr
            grp = jnp.arange(H) // hg
            pos = jnp.arange(g)[:, None] * dr + grp[None]
            hidx = jnp.arange(H)[None, :]
            sp = lambda x: x[:, pos, hidx, :]
            qd, kd, vd = (sp(qs), sp(ks), sp(vs))
            scores = jnp.einsum('bqhd,bkhd->bhqk', qd, kd) * D ** (-0.5)
            mask = jnp.tril(jnp.ones((g, g), bool))
            scores = jnp.where(mask, scores, -jnp.inf)
            lse = jax.nn.logsumexp(scores, axis=-1)
            o = jnp.einsum('bhqk,bkhd->bqhd', jnp.exp(scores - lse[..., None]), vd)
            hcol = jnp.arange(H)[:, None]
            od = jnp.zeros((B * n, H, sl, D), o.dtype).at[:, hcol, pos.T].set(o.transpose(0, 2, 1, 3))
            ld = jnp.zeros((B * n, H, sl), lse.dtype).at[:, hcol, pos.T].set(lse)
            ld = jnp.where(ld == 0.0, NEG, ld)
            od = od.reshape(B, n, H, sl, D).transpose(0, 2, 1, 3, 4)
            od = od.reshape(B, H, n * sl, D)[:, :, :L]
            ld = ld.reshape(B, n, H, sl).transpose(0, 2, 1, 3).reshape(B, H, n * sl)[:, :, :L]
            return (od, ld)
        root = jax.random.key(seed)
        ks = jax.random.split(root, 12)
        B, L, E = (1, 1024, EMBED_DIM)
        s = 0.02
        return {'query': jax.random.normal(ks[0], (B, L, E), jnp.float32), 'key': jax.random.normal(ks[1], (B, L, E), jnp.float32), 'value': jax.random.normal(ks[2], (B, L, E), jnp.float32), 'Wq': jax.random.normal(ks[3], (E, E), jnp.float32) * s, 'bq': jnp.zeros((E,), jnp.float32), 'Wk': jax.random.normal(ks[4], (E, E), jnp.float32) * s, 'bk': jnp.zeros((E,), jnp.float32), 'Wv': jax.random.normal(ks[5], (E, E), jnp.float32) * s, 'bv': jnp.zeros((E,), jnp.float32), 'Wo': jax.random.normal(ks[6], (E, E), jnp.float32) * s, 'bo': jnp.zeros((E,), jnp.float32)}
    _L0_xattn_all = _L0_xattn_setup()
    _L0_xattn_in = {k: v for k, v in _L0_xattn_all.items() if k in ('Wq', 'bq', 'Wk', 'bk', 'Wv', 'bv', 'Wo', 'bo')}
    del _L0_xattn_all

    def _L0_ffn_setup():
        import jax, jax.numpy as jnp
        import numpy as np
        EMB = 256
        FF = 4 * EMB

        def _ternary(w):
            scale = jnp.maximum(jnp.mean(jnp.abs(w)), 1e-08)
            w_t = jnp.clip(jnp.round(w / scale), -1.0, 1.0)
            return w + jax.lax.stop_gradient(w_t - w)
        key = jax.random.key(seed)
        kx, k1, k2, kb1, kb2 = jax.random.split(key, 5)
        x = jax.random.normal(kx, (4, 512, EMB), dtype=jnp.float32)
        lim1 = 1.0 / np.sqrt(EMB)
        lim2 = 1.0 / np.sqrt(FF)
        W1 = jax.random.uniform(k1, (FF, EMB), jnp.float32, -lim1, lim1)
        b1 = jax.random.uniform(kb1, (FF,), jnp.float32, -lim1, lim1)
        W2 = jax.random.uniform(k2, (EMB, FF), jnp.float32, -lim2, lim2)
        b2 = jax.random.uniform(kb2, (EMB,), jnp.float32, -lim2, lim2)
        return {'x': x, 'W1': W1, 'b1': b1, 'W2': W2, 'b2': b2}
    _L0_ffn_all = _L0_ffn_setup()
    _L0_ffn_in = {k: v for k, v in _L0_ffn_all.items() if k in ('W1', 'b1', 'W2', 'b2')}
    del _L0_ffn_all

    def _L1_attn_setup():
        import jax, jax.numpy as jnp
        import numpy as np
        B, T, D = (4, 1024, 256)
        HD = 64
        H = D // HD
        C = 64
        key = jax.random.key(seed)
        k1, k2, k3 = jax.random.split(key, 3)
        out = jax.random.normal(k1, (B, T, D), jnp.float32)
        W_write = jax.random.normal(k2, (D, D), jnp.float32) * 0.03
        W_read = jax.random.normal(k3, (D, D), jnp.float32) * 0.03
        decay = jnp.full((H,), 4.6, jnp.float32)
        log_alpha = jnp.log(jnp.full((H,), 0.03, jnp.float32))
        return {'out': out, 'W_write': W_write, 'W_read': W_read, 'decay': decay, 'log_alpha': log_alpha}
    _L1_attn_all = _L1_attn_setup()
    _L1_attn_in = {k: v for k, v in _L1_attn_all.items() if k in ('W_write', 'W_read', 'decay', 'log_alpha')}
    del _L1_attn_all

    def _L1_xattn_setup():
        import jax, jax.numpy as jnp
        import numpy as np
        DIM = 256
        NH = 8
        HD = DIM // NH
        E = 8
        EPS = 1e-05

        def rope_cos_sin(L, hd):
            inv_freq = 1.0 / 10000.0 ** (jnp.arange(0, hd, 2, dtype=jnp.float32) / hd)
            freqs = jnp.arange(L, dtype=jnp.float32)[:, None] * inv_freq[None, :]
            emb = jnp.concatenate([freqs, freqs], axis=-1)
            return (jnp.cos(emb), jnp.sin(emb))

        def rotate_half(x):
            x1 = x[..., 0::2]
            x2 = x[..., 1::2]
            return jnp.stack((-x2, x1), axis=-1).reshape(x.shape)

        def rope(t, cos, sin):
            return t * cos[None, None] + rotate_half(t) * sin[None, None]

        def heads(t):
            B, L, C = t.shape
            return t.reshape(B, L, NH, HD).transpose(0, 2, 1, 3)
        key = jax.random.key(seed)
        ks = jax.random.split(key, 32)
        std = 0.02
        d = {}
        d['x'] = jax.random.normal(ks[0], (16, 128, DIM), jnp.float32)
        d['h_a'] = jax.random.normal(ks[1], (16, 64, DIM), jnp.float32)
        d['h_t'] = jax.random.normal(ks[2], (16, 64, DIM), jnp.float32)
        names = ['qa', 'ka', 'va', 'qt', 'kt', 'vt', 'o', 'ffn']
        for i, n in enumerate(names):
            d['W_' + n] = jax.random.normal(ks[3 + 2 * i], (E, DIM, DIM), jnp.float32) * std
            d['b_' + n] = jax.random.normal(ks[4 + 2 * i], (E, DIM), jnp.float32) * std
        d['gamma'] = jnp.ones((E, DIM), jnp.float32)
        d['beta'] = jnp.zeros((E, DIM), jnp.float32)
        d['gating_factor'] = jnp.zeros((E,), jnp.float32)
        d['expert_idx'] = 3
        return d
    _L1_xattn_all = _L1_xattn_setup()
    _L1_xattn_in = {k: v for k, v in _L1_xattn_all.items() if k in ('W_qa', 'b_qa', 'W_ka', 'b_ka', 'W_va', 'b_va', 'W_qt', 'b_qt', 'W_kt', 'b_kt', 'W_vt', 'b_vt', 'W_o', 'b_o', 'W_ffn', 'b_ffn', 'gamma', 'beta', 'gating_factor')}
    del _L1_xattn_all

    def _L1_ffn_setup():
        import jax, jax.numpy as jnp
        import numpy as np
        B, T, D = (1, 256, 256)
        E, S, H = (8, 2, 1024)
        key = jax.random.key(seed)
        kx, kg, k1, k2, k3 = jax.random.split(key, 5)
        X = jax.random.normal(kx, (B, T, D), jnp.float32)
        Wg = jax.random.normal(kg, (D, E), jnp.float32) * 0.02
        bg = jnp.zeros((E,), jnp.float32)
        W1 = jax.random.normal(k1, (E, D, H), jnp.float32) * 0.02
        W3 = jax.random.normal(k3, (E, D, H), jnp.float32) * 0.02
        W2 = jax.random.normal(k2, (E, H, D), jnp.float32) * 0.02
        return {'X': X, 'Wg': Wg, 'bg': bg, 'W1': W1, 'W2': W2, 'W3': W3}
    _L1_ffn_all = _L1_ffn_setup()
    _L1_ffn_in = {k: v for k, v in _L1_ffn_all.items() if k in ('Wg', 'bg', 'W1', 'W2', 'W3')}
    del _L1_ffn_all
    return {'x': x, 'ctx_1024': ctx_1024, 'L0_attn_Wqkv': _L0_attn_in['Wqkv'], 'L0_attn_bqkv': _L0_attn_in['bqkv'], 'L0_attn_Wout': _L0_attn_in['Wout'], 'L0_attn_bout': _L0_attn_in['bout'], 'L0_xattn_Wq': _L0_xattn_in['Wq'], 'L0_xattn_bq': _L0_xattn_in['bq'], 'L0_xattn_Wk': _L0_xattn_in['Wk'], 'L0_xattn_bk': _L0_xattn_in['bk'], 'L0_xattn_Wv': _L0_xattn_in['Wv'], 'L0_xattn_bv': _L0_xattn_in['bv'], 'L0_xattn_Wo': _L0_xattn_in['Wo'], 'L0_xattn_bo': _L0_xattn_in['bo'], 'L0_ffn_W1': _L0_ffn_in['W1'], 'L0_ffn_b1': _L0_ffn_in['b1'], 'L0_ffn_W2': _L0_ffn_in['W2'], 'L0_ffn_b2': _L0_ffn_in['b2'], 'L1_attn_W_write': _L1_attn_in['W_write'], 'L1_attn_W_read': _L1_attn_in['W_read'], 'L1_attn_decay': _L1_attn_in['decay'], 'L1_attn_log_alpha': _L1_attn_in['log_alpha'], 'L1_xattn_W_qa': _L1_xattn_in['W_qa'], 'L1_xattn_b_qa': _L1_xattn_in['b_qa'], 'L1_xattn_W_ka': _L1_xattn_in['W_ka'], 'L1_xattn_b_ka': _L1_xattn_in['b_ka'], 'L1_xattn_W_va': _L1_xattn_in['W_va'], 'L1_xattn_b_va': _L1_xattn_in['b_va'], 'L1_xattn_W_qt': _L1_xattn_in['W_qt'], 'L1_xattn_b_qt': _L1_xattn_in['b_qt'], 'L1_xattn_W_kt': _L1_xattn_in['W_kt'], 'L1_xattn_b_kt': _L1_xattn_in['b_kt'], 'L1_xattn_W_vt': _L1_xattn_in['W_vt'], 'L1_xattn_b_vt': _L1_xattn_in['b_vt'], 'L1_xattn_W_o': _L1_xattn_in['W_o'], 'L1_xattn_b_o': _L1_xattn_in['b_o'], 'L1_xattn_W_ffn': _L1_xattn_in['W_ffn'], 'L1_xattn_b_ffn': _L1_xattn_in['b_ffn'], 'L1_xattn_gamma': _L1_xattn_in['gamma'], 'L1_xattn_beta': _L1_xattn_in['beta'], 'L1_xattn_gating_factor': _L1_xattn_in['gating_factor'], 'L1_ffn_Wg': _L1_ffn_in['Wg'], 'L1_ffn_bg': _L1_ffn_in['bg'], 'L1_ffn_W1': _L1_ffn_in['W1'], 'L1_ffn_W2': _L1_ffn_in['W2'], 'L1_ffn_W3': _L1_ffn_in['W3']}

def reference(x, ctx_1024, L0_attn_Wqkv, L0_attn_bqkv, L0_attn_Wout, L0_attn_bout, L0_xattn_Wq, L0_xattn_bq, L0_xattn_Wk, L0_xattn_bk, L0_xattn_Wv, L0_xattn_bv, L0_xattn_Wo, L0_xattn_bo, L0_ffn_W1, L0_ffn_b1, L0_ffn_W2, L0_ffn_b2, L1_attn_W_write, L1_attn_W_read, L1_attn_decay, L1_attn_log_alpha, L1_xattn_W_qa, L1_xattn_b_qa, L1_xattn_W_ka, L1_xattn_b_ka, L1_xattn_W_va, L1_xattn_b_va, L1_xattn_W_qt, L1_xattn_b_qt, L1_xattn_W_kt, L1_xattn_b_kt, L1_xattn_W_vt, L1_xattn_b_vt, L1_xattn_W_o, L1_xattn_b_o, L1_xattn_W_ffn, L1_xattn_b_ffn, L1_xattn_gamma, L1_xattn_beta, L1_xattn_gating_factor, L1_ffn_Wg, L1_ffn_bg, L1_ffn_W1, L1_ffn_W2, L1_ffn_W3):
    import jax
    import jax.numpy as jnp

    def _L0_attn_ref(hidden_states, Wqkv, bqkv, Wout, bout):
        import jax, jax.numpy as jnp
        import numpy as np
        HEADS = 16
        NUM_LANDMARKS = 64
        PINV_ITERS = 6
        D_MODEL = 256

        def _moore_penrose_pinv(x, num_iters):
            m = x.shape[-1]
            I = jnp.eye(m, dtype=x.dtype)
            V = x
            for _ in range(num_iters):
                KV = x @ V
                V = 0.25 * V @ (13.0 * I - KV @ (15.0 * I - KV @ (7.0 * I - KV)))
            return V
        b, n, d = hidden_states.shape
        h, m = (HEADS, NUM_LANDMARKS)
        dh = d // h
        scale = 1.0 / np.sqrt(dh).astype(np.float32)
        l = n // m
        qkv = hidden_states @ Wqkv + bqkv
        q, k, v = jnp.split(qkv, 3, axis=-1)

        def to_heads(t):
            return t.reshape(b, n, h, dh).transpose(0, 2, 1, 3)
        q, k, v = (to_heads(q), to_heads(k), to_heads(v))
        q = q * scale
        q_l = q.reshape(b, h, m, l, dh).mean(axis=3)
        k_l = k.reshape(b, h, m, l, dh).mean(axis=3)
        sim1 = jnp.einsum('bhid,bhjd->bhij', q, k_l)
        sim2 = jnp.einsum('bhid,bhjd->bhij', q_l, k_l)
        sim3 = jnp.einsum('bhid,bhjd->bhij', q_l, k)
        attn1 = jax.nn.softmax(sim1, axis=-1)
        attn2 = jax.nn.softmax(sim2, axis=-1)
        attn3 = jax.nn.softmax(sim3, axis=-1)
        attn2_inv = _moore_penrose_pinv(attn2, PINV_ITERS)
        out = attn1 @ (attn2_inv @ (attn3 @ v))
        out = out.transpose(0, 2, 1, 3).reshape(b, n, d)
        out = out @ Wout + bout
        return out

    def _L0_xattn_ref(query, key, value, Wq, bq, Wk, bk, Wv, bv, Wo, bo):
        import jax, jax.numpy as jnp
        import numpy as np
        EMBED_DIM = 256
        NUM_HEADS = 16
        HEAD_DIM = EMBED_DIM // NUM_HEADS
        SEG_LENS = [256, 512, 1024]
        DIL_RATIOS = [1, 2, 4]
        NEG = -100000000.0

        def _branch(q, k, v, sl, dr, L):
            B = q.shape[0]
            H, D = (NUM_HEADS, HEAD_DIM)
            sl = min(sl, L)
            pad = -L % sl
            if pad:
                pw = ((0, 0), (0, pad), (0, 0), (0, 0))
                q, k, v = (jnp.pad(q, pw), jnp.pad(k, pw), jnp.pad(v, pw))
            n = (L + pad) // sl
            qs = q.reshape(B * n, sl, H, D)
            ks = k.reshape(B * n, sl, H, D)
            vs = v.reshape(B * n, sl, H, D)
            hg = H // dr
            g = sl // dr
            grp = jnp.arange(H) // hg
            pos = jnp.arange(g)[:, None] * dr + grp[None]
            hidx = jnp.arange(H)[None, :]
            sp = lambda x: x[:, pos, hidx, :]
            qd, kd, vd = (sp(qs), sp(ks), sp(vs))
            scores = jnp.einsum('bqhd,bkhd->bhqk', qd, kd) * D ** (-0.5)
            mask = jnp.tril(jnp.ones((g, g), bool))
            scores = jnp.where(mask, scores, -jnp.inf)
            lse = jax.nn.logsumexp(scores, axis=-1)
            o = jnp.einsum('bhqk,bkhd->bqhd', jnp.exp(scores - lse[..., None]), vd)
            hcol = jnp.arange(H)[:, None]
            od = jnp.zeros((B * n, H, sl, D), o.dtype).at[:, hcol, pos.T].set(o.transpose(0, 2, 1, 3))
            ld = jnp.zeros((B * n, H, sl), lse.dtype).at[:, hcol, pos.T].set(lse)
            ld = jnp.where(ld == 0.0, NEG, ld)
            od = od.reshape(B, n, H, sl, D).transpose(0, 2, 1, 3, 4)
            od = od.reshape(B, H, n * sl, D)[:, :, :L]
            ld = ld.reshape(B, n, H, sl).transpose(0, 2, 1, 3).reshape(B, H, n * sl)[:, :, :L]
            return (od, ld)
        B, L, E = query.shape
        H, D = (NUM_HEADS, HEAD_DIM)
        q = (query @ Wq.T + bq).reshape(B, L, H, D)
        k = (key @ Wk.T + bk).reshape(B, L, H, D)
        v = (value @ Wv.T + bv).reshape(B, L, H, D)
        outs, lses = ([], [])
        for sl, dr in zip(SEG_LENS, DIL_RATIOS):
            o, l = _branch(q, k, v, sl, dr, L)
            outs.append(o)
            lses.append(l)
        lse_all = jnp.stack(lses, 0)[..., None]
        m = lse_all.max(0)
        w = jnp.exp(lse_all - m)
        w = w / w.sum(0)
        w = jax.lax.stop_gradient(w)
        out = sum((o * wi.astype(o.dtype) for o, wi in zip(outs, w)))
        out = out.transpose(0, 2, 1, 3).reshape(B, L, E)
        return out @ Wo.T + bo

    def _L0_ffn_ref(x, W1, b1, W2, b2):
        import jax, jax.numpy as jnp
        import numpy as np
        EMB = 256
        FF = 4 * EMB

        def _ternary(w):
            scale = jnp.maximum(jnp.mean(jnp.abs(w)), 1e-08)
            w_t = jnp.clip(jnp.round(w / scale), -1.0, 1.0)
            return w + jax.lax.stop_gradient(w_t - w)
        h = jnp.einsum('bsd,fd->bsf', x, _ternary(W1)) + b1
        h = jax.nn.gelu(h, approximate=False)
        out = jnp.einsum('bsf,df->bsd', h, _ternary(W2)) + b2
        return out

    def _L1_attn_ref(out, W_write, W_read, decay, log_alpha):
        import jax, jax.numpy as jnp
        import numpy as np
        B, T, D = (4, 1024, 256)
        HD = 64
        H = D // HD
        C = 64
        Bb, Tt, Dd = out.shape
        d, Hh, Cc = (HD, D // HD, C)
        out32 = out.astype(jnp.float32)
        gamma = jax.nn.sigmoid(decay)
        log_gamma = jnp.log(gamma)
        v = (out32 @ W_write.T).reshape(Bb, Tt, Hh, d).transpose(0, 2, 1, 3)
        rk = out32.reshape(Bb, Tt, Hh, d).transpose(0, 2, 1, 3)
        wk = jnp.pad(rk[:, :, :-1], ((0, 0), (0, 0), (1, 0), (0, 0)))
        BH = Bb * Hh
        gamma_bh = jnp.tile(gamma, Bb)
        log_gamma_bh = jnp.tile(log_gamma, Bb)
        nC = Tt // Cc
        v_ch = v.reshape(BH, nC, Cc, d).transpose(1, 0, 2, 3)
        rk_ch = rk.reshape(BH, nC, Cc, d).transpose(1, 0, 2, 3)
        wk_ch = wk.reshape(BH, nC, Cc, d).transpose(1, 0, 2, 3)
        p = jnp.arange(Cc)
        diffs = jnp.clip(p[:, None] - 1 - p[None, :], 0)
        causal = p[:, None] > p[None, :]
        M = jnp.exp(diffs[None].astype(jnp.float32) * log_gamma_bh[:, None, None]) * causal[None]
        g_p = gamma_bh[:, None] ** p[None, :].astype(jnp.float32)
        g_w = gamma_bh[:, None] ** (Cc - 1 - p)[None, :].astype(jnp.float32)
        g_C = gamma_bh ** Cc

        def scan_fn(W, chunk):
            rk_c, wk_c, v_c = chunk
            inter = jnp.einsum('bij,bcj->bci', W, rk_c) * g_p[:, :, None]
            S = jnp.einsum('bcd,bkd->bck', rk_c, wk_c)
            intra = jnp.einsum('bck,bkd->bcd', S * M, v_c)
            W_new = g_C[:, None, None] * W + jnp.einsum('bci,bcj->bij', v_c * g_w[:, :, None], wk_c)
            return (W_new, inter + intra)
        W0 = jnp.zeros((BH, d, d), jnp.float32)
        _, reads = jax.lax.scan(scan_fn, W0, (rk_ch, wk_ch, v_ch))
        reads = reads.transpose(1, 0, 2, 3).reshape(Bb, Hh, Tt, d)
        alpha = jnp.exp(log_alpha)[None, :, None, None]
        reads = (alpha * reads).transpose(0, 2, 1, 3).reshape(Bb, Tt, Dd)
        return out + (reads @ W_read.T).astype(out.dtype)

    def _L1_xattn_ref(x, h_a, h_t, W_qa, b_qa, W_ka, b_ka, W_va, b_va, W_qt, b_qt, W_kt, b_kt, W_vt, b_vt, W_o, b_o, W_ffn, b_ffn, gamma, beta, gating_factor, expert_idx):
        import jax, jax.numpy as jnp
        import numpy as np
        DIM = 256
        NH = 8
        HD = DIM // NH
        E = 8
        EPS = 1e-05

        def rope_cos_sin(L, hd):
            inv_freq = 1.0 / 10000.0 ** (jnp.arange(0, hd, 2, dtype=jnp.float32) / hd)
            freqs = jnp.arange(L, dtype=jnp.float32)[:, None] * inv_freq[None, :]
            emb = jnp.concatenate([freqs, freqs], axis=-1)
            return (jnp.cos(emb), jnp.sin(emb))

        def rotate_half(x):
            x1 = x[..., 0::2]
            x2 = x[..., 1::2]
            return jnp.stack((-x2, x1), axis=-1).reshape(x.shape)

        def rope(t, cos, sin):
            return t * cos[None, None] + rotate_half(t) * sin[None, None]

        def heads(t):
            B, L, C = t.shape
            return t.reshape(B, L, NH, HD).transpose(0, 2, 1, 3)
        e = expert_idx

        def lin(t, W, b):
            return t @ W[e].T + b[e]
        B, T, C = x.shape
        Ka = h_a.shape[1]
        Kt = h_t.shape[1]
        q_a = heads(lin(x, W_qa, b_qa))
        q_t = heads(lin(x, W_qt, b_qt))
        k_a = heads(lin(h_a, W_ka, b_ka))
        v_a = heads(lin(h_a, W_va, b_va))
        k_t = heads(lin(h_t, W_kt, b_kt))
        v_t = heads(lin(h_t, W_vt, b_vt))
        cos_m, sin_m = rope_cos_sin(T, HD)
        q_a = rope(q_a, cos_m, sin_m)
        q_t = rope(q_t, cos_m, sin_m)
        cos_a, sin_a = rope_cos_sin(Ka, HD)
        k_a = rope(k_a, cos_a, sin_a)
        cos_t, sin_t = rope_cos_sin(Kt, HD)
        k_t = rope(k_t, cos_t, sin_t)
        ratio_g = jax.nn.sigmoid(gating_factor[e])
        s_a = jnp.einsum('bhtd,bhkd->bhtk', q_a, k_a)
        s_t = jnp.einsum('bhtd,bhkd->bhtk', q_t, k_t) * ratio_g
        scores = jnp.concatenate([s_a, s_t], axis=-1) / np.sqrt(HD)
        w = jax.nn.softmax(scores, axis=-1)
        v = jnp.concatenate([v_a, v_t], axis=2)
        out = jnp.einsum('bhtk,bhkd->bhtd', w, v)
        out = out.transpose(0, 2, 1, 3).reshape(B, T, C)
        out = lin(out, W_o, b_o)
        x = out + x
        mu = jnp.mean(x, axis=-1, keepdims=True)
        var = jnp.var(x, axis=-1, keepdims=True)
        xn = (x - mu) / jnp.sqrt(var + EPS) * gamma[e] + beta[e]
        x = jax.nn.relu(lin(xn, W_ffn, b_ffn))
        return x

    def _L1_ffn_ref(X, Wg, bg, W1, W2, W3):
        import jax, jax.numpy as jnp
        import numpy as np
        B, T, D = (1, 256, 256)
        E, S, H = (8, 2, 1024)
        logits = jnp.einsum('btd,de->bte', X, Wg) + bg
        topv, topi = jax.lax.top_k(logits, S)
        w = jax.nn.softmax(topv, axis=-1)
        xs = X[:, :, None, :] * w[..., None]
        out = X
        for e in range(E):
            h = jax.nn.silu(jnp.einsum('btsd,dh->btsh', xs, W1[e])) * jnp.einsum('btsd,dh->btsh', xs, W3[e])
            y = jnp.einsum('btsh,hd->btsd', h, W2[e])
            mask = (topi == e)[..., None]
            out = out + jnp.where(mask, y, 0.0).sum(axis=2)
        return out
    x = _layernorm(x + _L0_attn_ref(x, L0_attn_Wqkv, L0_attn_bqkv, L0_attn_Wout, L0_attn_bout), axis=-1)
    x = _layernorm(x + _L0_xattn_ref(x, ctx_1024, ctx_1024, L0_xattn_Wq, L0_xattn_bq, L0_xattn_Wk, L0_xattn_bk, L0_xattn_Wv, L0_xattn_bv, L0_xattn_Wo, L0_xattn_bo), axis=-1)
    x = _layernorm(x + _L0_ffn_ref(x, L0_ffn_W1, L0_ffn_b1, L0_ffn_W2, L0_ffn_b2), axis=-1)
    x = _layernorm(x + _L1_attn_ref(x, L1_attn_W_write, L1_attn_W_read, L1_attn_decay, L1_attn_log_alpha), axis=-1)
    x = _layernorm(x + _L1_xattn_ref(x, ctx_1024, ctx_1024, L1_xattn_W_qa, L1_xattn_b_qa, L1_xattn_W_ka, L1_xattn_b_ka, L1_xattn_W_va, L1_xattn_b_va, L1_xattn_W_qt, L1_xattn_b_qt, L1_xattn_W_kt, L1_xattn_b_kt, L1_xattn_W_vt, L1_xattn_b_vt, L1_xattn_W_o, L1_xattn_b_o, L1_xattn_W_ffn, L1_xattn_b_ffn, L1_xattn_gamma, L1_xattn_beta, L1_xattn_gating_factor, 3), axis=-1)
    x = _layernorm(x + _L1_ffn_ref(x, L1_ffn_Wg, L1_ffn_bg, L1_ffn_W1, L1_ffn_W2, L1_ffn_W3), axis=-1)
    return x

_drawn_inputs = setup_inputs


def setup_inputs(seed=0):
    import zlib

    import numpy as np

    out = dict(_drawn_inputs(seed))
    spreads = {'L0_attn_bqkv': (0.0, 0.1),
     'L0_attn_bout': (0.0, 0.1),
     'L0_xattn_bq': (0.0, 0.1),
     'L0_xattn_bk': (0.0, 0.1),
     'L0_xattn_bv': (0.0, 0.1),
     'L0_xattn_bo': (0.0, 0.1),
     'L1_attn_decay': (4.599999904632568, 0.2),
     'L1_attn_log_alpha': (-3.5065579414367676, 0.2),
     'L1_xattn_gamma': (1.0, 0.2),
     'L1_xattn_beta': (0.0, 0.1),
     'L1_xattn_gating_factor': (0.0, 0.1),
     'L1_ffn_bg': (0.0, 0.1)}
    factors = {}
    for name, (base, spread) in spreads.items():
        noise = np.random.default_rng([zlib.crc32(name.encode()), seed]).standard_normal(out[name].shape)
        drawn = base * np.exp(spread * noise) if base else spread * noise
        out[name] = jnp.asarray(drawn.astype(out[name].dtype))
    for name, factor in factors.items():
        out[name] = (out[name] * factor).astype(out[name].dtype)
    return out
```

```python
import numpy as np
import concourse.bass as bass
from concourse import mybir
from concourse.alu_op_type import AluOpType as ALU
from contextlib import ExitStack

F32 = mybir.dt.float32
BF16 = mybir.dt.bfloat16
ACT = mybir.ActivationFunctionType
AX = mybir.AxisListType

P = 128
BATCH = 8
T = 256
D = 256
NT = T // P
NC = D // P
STREAMS = 2
EPS = 1e-5

H0 = 16
DH0 = D // H0
HC = P // DH0
M = 64
LM = T // M
PAIRS = H0 // 2
PINV_ITERS = 6
BR = 3
VW = DH0 + 1
NEG = -100000000.0
BIG = -1e30
TINY = 2.0 ** -63
FF = 4 * D
FC = FF // P
H1 = 4
HD1 = D // H1
H2 = 8
HD2 = D // H2
VW2 = HD2 + 1
KT2 = 2 * T // P
E = 8
HF = 1024


class BankTurns:

    def __init__(self, tensors, filled, emptied, order):
        self.turn = {}
        count = [0] * len(tensors)
        for name, b in order:
            count[b] += 1
            assert name not in self.turn, name
            self.turn[name] = (tensors[b], filled[b], emptied[b], count[b])

    def claim(self, pe, name):
        tensor, _, emptied, k = self.turn[name]
        if k > 1:
            pe.wait_ge(emptied, k - 1)
        return tensor

    def await_filled(self, eng, name):
        tensor, filled, _, k = self.turn[name]
        eng.wait_ge(filled, k)
        return tensor

    await_done = await_filled

    def await_emptied(self, eng, name):
        _, _, emptied, k = self.turn[name]
        eng.wait_ge(emptied, k)

    def filled(self, name):
        return self.turn[name][1]

    def emptied(self, name):
        return self.turn[name][2]


def bank_order():
    o = [("n_q", 0), ("n_k", 1), ("n_v", 2)]
    o += [("n_sim2", 3)]
    o += [(f"n_max1_{t}{c}", (0, 1, 2, 3)[2 * t + c]) for t in range(NT) for c in range(NC)]
    o += [(f"n_max3_{i}", i) for i in range(4)]
    o += [("n_negT", 0)]
    o += [(f"n_s1_{i}", (1, 2, 3, 0)[i]) for i in range(4)]
    o += [(f"n_s3_{t}{c}", (1, 2, 3, 0)[2 * t + c]) for t in range(NT) for c in range(NC)]
    o += [("n_aT", 1), ("n_y", 2)]
    for g in range(2):
        o += [(f"n_k0_{g}", g), (f"n_kT0_{g}", 2 + g)]
    for i in range(PINV_ITERS - 1):
        for g in range(2):
            o += [(f"n_p{i}_{g}", g)]
        for g in range(2):
            o += [(f"n_t{i}_{g}", 2 + g)]
        for g in range(2):
            o += [(f"n_kT{i + 1}_{g}", 2 + g)]
            if i < PINV_ITERS - 2:
                o += [(f"n_k{i + 1}_{g}", g)]
    for j in range(4):
        o += [(f"n_w{j}", 2 + j % 2)]
    o += [(f"n_o{t}", t) for t in range(NT)]
    o += [("n_oT", 2), ("n_out", 3), ("n_xT", 0)]
    o += [("d_q", 1), ("d_k", 2), ("d_v", 3)]
    for c in range(NC):
        o += [(f"d_m{c}_{i}", i % 3 + 1) for i in range(6)]
        o += [(f"d_negT{c}", 0)]
        o += [(f"d_s{c}_{i}", i % 3 + 1) for i in range(6)]
        o += [(f"d_o{c}_{t}", (0, 1)[t]) for t in range(NT)]
    o += [("d_oT", 2), ("d_out", 3), ("d_xT", 0)]
    o += [(f"f_h{i}", (1, 2, 3, 0)[i]) for i in range(FC // 2)]
    o += [("f_out", 1), ("f_xT", 2)]
    o += [("r_v", 3), ("r_s0", 0), ("r_s1", 1), ("r_s2", 2), ("r_s3", 3), ("r_r", 2),
          ("r_out", 0), ("r_xT", 1)]
    o += [(f"g_{n}{r}", b) for n, r, b in
          (("ka", "", 2), ("ka", "r", 3), ("kt", "", 0), ("kt", "r", 1),
           ("qa", "", 2), ("qa", "r", 3), ("qt", "", 0), ("qt", "r", 1))]
    o += [("g_va", 2), ("g_vt", 3)]
    o += [(f"g_m{h}_{t}", 2 * (h % 2) + t) for h in range(H2) for t in range(NT)]
    o += [("g_negT", 0)]
    o += [(f"g_o{t}", t) for t in range(NT)]
    o += [(f"g_s{h}_{i}", 2 + i) for h in range(H2) for i in range(2)]
    o += [("g_oT", 2), ("g_out", 3), ("g_nT", 0), ("g_ffn", 1), ("g_xT", 2)]
    return o


def words(kind, shape):
    n = int(np.prod(shape))
    n = n if kind == F32 else (n + 1) // 2
    return n + n % 2


def words_of(table):
    return sum(words(kind, shape) for kind, *shape in table.values())


def carve(arena, sizes):
    at, out = 0, {}
    for name, (kind, *shape) in sizes.items():
        n = int(np.prod(shape))
        w = words(kind, shape)
        v = arena[:, at:at + w]
        if kind == BF16:
            v = v.bitcast(BF16)
        v = v[:, 0:n]
        if len(shape) == 2:
            v = v.rearrange("p (a b) -> p a b", a=shape[0])
        if len(shape) == 3:
            v = v.rearrange("p (a b c) -> p a b c", a=shape[0], b=shape[1])
        if len(shape) == 4:
            v = v.rearrange("p (a b c d) -> p a b c d", a=shape[0], b=shape[1], c=shape[2])
        out[name] = v
        at += w
    return out, at


NYSTROM = {
    "q": (F32, NC, T), "k": (F32, NC, T), "qb": (BF16, NC, T), "kb": (BF16, NC, T),
    "v": (F32, NT, H0, VW), "qs": (F32, NC, M), "ks": (F32, NC, M), "kl": (F32, NC, M),
    "qlm": (F32, NC, HC, M), "klm": (F32, NC, HC, M), "qlmb": (BF16, NC, HC, M), "klmb": (BF16, NC, HC, M),
    "mx1": (F32, NT, H0), "mx3": (F32, PAIRS), "mx2": (F32, PAIRS), "sum2": (F32, PAIRS), "rs2": (F32, PAIRS),
    "neg": (BF16, 3, P), "negT": (BF16, 3, P),
    "a": (F32, PAIRS, M), "aT": (F32, PAIRS, M),
    "ry": (F32, PAIRS), "z": (F32, PAIRS, DH0), "z2": (F32, PAIRS, DH0), "g": (F32, PAIRS, 2 * VW),
    "ro": (F32, NT, H0),
    "e1": (F32, PAIRS, T), "e3": (F32, NT, NC, HC * M),
}
PINV = {"kk": (F32, PAIRS, M), "kkT": (F32, PAIRS, M), "t1": (F32, PAIRS, M), "t2": (F32, PAIRS, M)}
DILATED = {
    "q": (F32, NC, T), "k": (F32, NC, T), "kb": (BF16, NC, T), "v": (F32, NT, H0, BR, VW),
    "qm": (F32, HC, T), "qmb": (BF16, HC, T), "p0": (F32, HC, T), "p1": (F32, HC, P),
    "mx": (F32, NT, H0), "neg": (BF16, NT, P), "negT": (BF16, NT, P),
    "s": (F32, NT, H0, BR), "ls": (F32, NT, H0, BR), "isz": (F32, NT, H0, BR), "w": (F32, NT, H0, BR),
    "rc": (F32, NT, H0, BR), "lm": (F32, NT, H0), "rz": (F32, NT, H0),
    "n": (F32, NT, H0, BR, VW),
}
FFN = {"h": (F32, FC, T)}
MEMORY = {"v": (F32, NT, D), "s0": (F32, H1, T), "s1": (F32, H1, P), "r": (F32, NC, T)}
GATED = {
    "qa": (F32, NC, T), "qt": (F32, NC, T), "ka": (F32, NC, T), "kt": (F32, NC, T),
    "qab": (BF16, NC, T), "qtb": (BF16, NC, T), "kab": (BF16, NC, T), "ktb": (BF16, NC, T),
    "ra": (F32, NC, T), "rb": (F32, NC, T), "v": (F32, KT2, H2, VW2),
    "mx": (F32, NT, H2), "neg": (BF16, NT, 4, 32), "negT": (BF16, NT, P), "p": (F32, 2, KT2, T),
    "ro": (F32, NT, H2), "o": (F32, NT, D), "oT": (F32, NC, T), "u": (F32, NT, D), "n": (F32, NT, D),
    "nT": (F32, NC, T), "f": (F32, NT, D),
}

MATRICES = {"qkv": 3 * D, "out": D, "dq": D, "dk": D, "dv": D, "do": D, "ff1": FF, "mw": D, "mr": D,
            "qa": D, "qar": D, "ka": D, "kar": D, "va": D, "qt": D, "qtr": D, "kt": D, "ktr": D, "vt": D,
            "go": D, "gf": D}
COLUMNS = {"q0": NC, "k0": NC, "dq": NC, "dk": NC, "ff1": FC, "decay": H1, "alpha": H1,
           "qa": NC, "qar": NC, "ka": NC, "kar": NC, "qt": NC, "qtr": NC, "kt": NC, "ktr": NC,
           "gamma": NC, "beta": NC, "gate": 1}
ROWS = ("v0", "o0", "dv", "do", "ff2", "va", "vt", "go", "gf")


def shape_constants():

    bf = np.dtype("bfloat16")
    p = np.arange(P)
    c = {"ident": np.eye(P, dtype=np.float32), "identb": np.eye(P).astype(bf)}
    mask = (p[:, None] // DH0 == np.arange(HC)[None]).astype(np.float32)
    c["hmask"] = np.concatenate([mask, mask / LM], 1)
    c["ones"] = np.ones((P, P), np.float32)
    c["eye"] = np.tile(np.eye(M, dtype=np.float32), (2, 1))
    c["eye325"] = 3.25 * c["eye"]
    selp = np.zeros((P, PAIRS, P), np.float32)
    sel16 = np.zeros((P, H0, P), np.float32)
    selg = np.zeros((P, H2, P), np.float32)
    for h in range(H0):
        selp[h, h // 2, (h % 2) * M:(h % 2 + 1) * M] = 1
        sel16[h, h, :] = 1
    for h in range(H2):
        selg[h::32, h, :] = 1
    c["selp"], c["sel16"], c["selg"] = (x.reshape(P, -1).astype(bf) for x in (selp, sel16, selg))
    c["above"] = np.where(p[:, None] < p[None], BIG, 0.0).astype(bf)
    c["below"] = np.where(p[:, None] > p[None], BIG, 0.0).astype(bf)
    heads = np.arange(H0)
    on = np.stack([np.ones((P, H0)), p[:, None] % 2 == heads // 8, p[:, None] % 4 == heads // 4], 2)
    c["valid"] = on.reshape(P, -1).astype(np.float32)
    freq = (1.0 / 10000.0 ** (np.arange(0, HD2, 2, dtype=np.float32) / np.float32(HD2))).astype(np.float32)
    ang = np.arange(T, dtype=np.float32)[None] * freq[(p % HD2) % (HD2 // 2)][:, None]
    sign = np.where(p % 2 == 0, -1.0, 1.0).astype(np.float32)[:, None]
    c["tri"] = (p[:, None] < p[None]).astype(bf)
    c["onesb"] = np.ones((P, P)).astype(bf)
    c["eids"] = np.tile(np.arange(E, dtype=np.float32), (P, 1))
    c["jids"] = np.tile(np.arange(TILES, dtype=np.float32), (P, 1))
    c["cosk"], c["sink"] = np.cos(ang).astype(np.float32), (np.sin(ang) * sign).astype(np.float32)
    r = np.float32(1.0 / np.sqrt(HD2))
    c["cosq"], c["sinq"] = c["cosk"] * r, c["sink"] * r
    t = np.arange(T)
    c["exponents"] = np.maximum(t[None] - 1 - p[:, None], 0).astype(np.float32)
    c["keep"] = (t[None] > p[:, None]).astype(np.float32)
    return c


def layers_kernel(nc, a, stop):
    ctx = ExitStack()
    with ctx:
        def sb(name, shape, dt=F32):
            return ctx.enter_context(nc.sbuf_tensor(name, shape, dt))

        sems = {}

        def sem(name):
            if name not in sems:
                sems[name] = ctx.enter_context(nc.semaphore(name))
            return sems[name]

        W = {n: sb("w_" + n, [P, NC, cols]) for n, cols in MATRICES.items()}
        w2 = sb("w_ff2", [P, FC, D])
        bias = {n: sb("b_" + n, [P, cols]) for n, cols in COLUMNS.items()}
        rows = {n: sb("r_" + n, [P, D]) for n in ROWS}
        ident = sb("ident", [P, P])
        identb = sb("identb", [P, P], BF16)
        width = max(words_of(table) for table in (NYSTROM, DILATED, FFN, MEMORY, GATED))
        arenas = [sb(f"arena{s}", [P, width]) for s in range(STREAMS)]
        scratch, exponents, keep = arenas[0][:, 0:1024], arenas[0][:, 1024:1024 + T], arenas[0][:, 1280:1280 + T]
        consts = {n: sb("c_" + n, [P, c.shape[1]], BF16 if c.dtype != np.float32 else F32)
                  for n, c in shape_constants().items() if n not in ("ident", "identb", "exponents", "keep", "tri", "onesb", "eids", "jids")}
        hmask = consts["hmask"]
        selp = consts["selp"][:].rearrange("p (a b) -> p a b", b=P)
        sel16 = consts["sel16"][:].rearrange("p (a b) -> p a b", b=P)
        selg = consts["selg"][:].rearrange("p (a b) -> p a b", b=P)
        cosg = sb("cosg", [P, T])
        sing = sb("sing", [P, T])
        dec0 = sb("dec0", [P, H1, T])
        dec1 = sb("dec1", [P, H1, P])
        small = sb("small", [P, 64])

        st = []
        psum = [ctx.enter_context(nc.psum_tensor(f"bank{i}", [P, 512], F32)) for i in range(8)]
        for s in range(STREAMS):
            arena = arenas[s]
            v = {"x": sb(f"x{s}", [P, NT, D]), "y": sb(f"y{s}", [P, NT, D]), "res": sb(f"res{s}", [P, NT, D]),
                 "xz": sb(f"xz{s}", [P, NC, T + 1]), "ctx": sb(f"ctx{s}", [P, NC, T]),
                 "st": sb(f"st{s}", [P, NT, 6]), "mv": sb(f"mv{s}", [P, NT, 2]),
                 "ve": sb(f"ve{s}", [P, NT]), "rstd": sb(f"rstd{s}", [P, NT])}
            for key, table in (("n", NYSTROM), ("d", DILATED), ("f", FFN), ("r", MEMORY), ("g", GATED)):
                v[key], _ = carve(arena[:], table)
            v["n"].update(carve(v["n"]["e3"].rearrange("p a b c -> p (a b c)"), PINV)[0])
            for key in "nd":
                v[key]["o"], v[key]["oT"] = v[key]["q"], v[key]["k"]
            v["n"]["t3"] = v["n"]["qlmb"].rearrange("p c h m -> p (c h m)").bitcast(F32)\
                .rearrange("p (a m) -> p a m", m=M)
            v["bk"] = BankTurns([psum[4 * s + i] for i in range(4)],
                            [sem(f"bank_filled{s}_{i}") for i in range(4)],
                            [sem(f"bank_emptied{s}_{i}") for i in range(4)], bank_order())
            st.append(v)

        NEGH = sb("neghalf", [P, NT])

        with nc.Block() as block:
            loaded = {n: sem("load_" + n) for n in ("sp", "act")}
            order = [(W[n][:], a["W_" + n].rearrange("(c p) n -> p c n", p=P)) for n in MATRICES]
            order += [(w2[:], a["W_ff2"].rearrange("(c p) n -> p c n", p=P))]
            order2 = [(bias[n][:], a["B_" + n]) for n in COLUMNS] + [(rows[n][:], a["R_" + n]) for n in ROWS]
            order2 += [(ident[:], a["C_ident"]), (identb[:], a["C_identb"])]
            order2 += [(consts[n][:], a["C_" + n]) for n in consts]
            order2 += [(exponents, a["C_exponents"]), (keep, a["C_keep"])]
            n_sp, n_act = 16 * len(order), 16 * len(order2)
            step = sem("setup_dve")
            act_step = sem("setup_act")
            pool_step = sem("setup_pool")
            pe_step = sem("setup_pe")

            @block.sync
            def _(sp):
                for dst, src in order:
                    sp.dma_start(dst, src).then_inc(loaded["sp"], 16)

            @block.gpsimd
            def _(pool):
                for s in range(STREAMS):
                    pool.memset(st[s]["xz"][:], 0.0)
                pool.memset(NEGH[:], -0.5)
                pool.memset(small[:, 63:64], 1.0 / (FF * D)).then_inc(pool_step, 1)

            @block.scalar
            def _(act):
                for dst, src in order2:
                    act.dma_start(dst, src).then_inc(loaded["act"], 16)
                act.wait_ge(loaded["act"], n_act)
                act.activation(small[:, 0:4], bias["decay"][:], ACT.Exp, scale=-1.0).then_inc(act_step, 1)
                act.wait_ge(act_step, 1)
                act.activation(small[:, 4:8], small[:, 0:4], ACT.Ln, bias=1.0).then_inc(act_step, 1)
                act.wait_ge(step, 1)
                for h in range(H1):
                    act.activation(dec0[:, h, :], exponents, ACT.Exp, bias=bias["alpha"][:, h:h + 1],
                                   scale=small[:, 8 + h:9 + h])
                    act.activation(dec1[:, h, :], exponents[:, 0:P], ACT.Exp, bias=bias["alpha"][:, h:h + 1],
                                   scale=small[:, 8 + h:9 + h]).then_inc(act_step, 1)
                act.activation(small[:, 12:13], bias["gate"][:], ACT.Exp, scale=-1.0).then_inc(act_step, 1)

            @block.vector
            def _(dve):
                n = 0

                def link(ins):
                    nonlocal n
                    n += 1
                    ins.then_inc(step, 1)
                    dve.wait_ge(step, n)

                dve.wait_ge(act_step, 2)
                link(dve.tensor_scalar(small[:, 8:12], small[:, 4:8], -1.0, None, ALU.mult))
                dve.wait_ge(act_step, 2 + H1)
                link(dve.tensor_tensor(dec0[:], dec0[:], keep[:, None, :].to_broadcast([P, H1, T]), ALU.mult))
                link(dve.tensor_tensor(dec1[:], dec1[:], keep[:, None, 0:P].to_broadcast([P, H1, P]), ALU.mult))
                dve.wait_ge(act_step, 3 + H1)
                link(dve.tensor_scalar(small[:, 13:14], small[:, 12:13], 1.0, None, ALU.add))
                link(dve.reciprocal(small[:, 14:15], small[:, 13:14]))
                link(dve.tensor_scalar(cosg[:], consts["cosq"][:], small[:, 14:15], None, ALU.mult))
                link(dve.tensor_scalar(sing[:], consts["sinq"][:], small[:, 14:15], None, ALU.mult))
                dve.wait_ge(loaded["sp"], n_sp)
                for i, w in enumerate((W["ff1"], w2)):
                    flat = w[:].rearrange("p c n -> p (c n)")
                    link(dve.tensor_reduce(small[:, 16 + i:17 + i], flat, axis=AX.X, op=ALU.add,
                                           apply_absolute_value=True))
                dve.wait_ge(pe_step, 1)
                for i, w in enumerate((W["ff1"], w2)):
                    flat = w[:].rearrange("p c n -> p (c n)")
                    c = small[:, 20 + 4 * i:24 + 4 * i]
                    link(dve.tensor_scalar(c[:, 0:1], psum[0][:, i:i + 1], small[:, 63:64], 1e-8, ALU.mult, ALU.max))
                    link(dve.reciprocal(c[:, 1:2], c[:, 0:1]))
                    for half in range(2):
                        f = flat[:, half * 1024:(half + 1) * 1024]
                        link(dve.tensor_scalar(f, f, c[:, 1:2], None, ALU.mult))
                        link(dve.tensor_scalar(scratch, f, -0.5, -1.0, ALU.is_lt, ALU.mult))
                        link(dve.scalar_tensor_tensor(f, f, 0.5, scratch, ALU.is_gt, ALU.add))

            @block.tensor
            def _(pe):
                pe.wait_ge(loaded["act"], n_act)
                pe.wait_ge(pool_step, 1)
                pe.wait_ge(step, 9)
                pe.matmul(psum[0][:, 0:2], consts["ones"][:], small[:, 16:18], start=True, stop=True).then_inc(pe_step, 1)

        def transposed(x, t, c):
            return x[:, t, c * P:(c + 1) * P]

        x_of = lambda s: st[s]["xz"][:, :, 1:T + 1]

        def pe_transposes(pe, s, name, src):
            b = st[s]["bk"].claim(pe, name)
            for c in range(NC):
                for t in range(NT):
                    last = pe.transpose(b[:, c * T + t * P:c * T + (t + 1) * P], transposed(src, t, c), ident[:])
            last.then_inc(st[s]["bk"].filled(name), 1)

        def pe_features(pe, s, name, w, col, x):
            b = st[s]["bk"].claim(pe, name)
            for m in range(NC):
                for c in range(NC):
                    last = pe.matmul(b[:, m * T:(m + 1) * T], w[:, c, col + m * P:col + (m + 1) * P], x[:, c, :],
                                     start=c == 0, stop=c == NC - 1)
            last.then_inc(st[s]["bk"].filled(name), 1)

        def pe_tokens(pe, s, name, w, col, x, chunks=NC):
            b = st[s]["bk"].claim(pe, name)
            for t in range(NT):
                for c in range(chunks):
                    last = pe.matmul(b[:, t * D:(t + 1) * D], x[:, c, t * P:(t + 1) * P], w[:, c, col:col + D],
                                     start=c == 0, stop=c == chunks - 1)
            last.then_inc(st[s]["bk"].filled(name), 1)

        def pe_nystrom(pe, s):
            v, bk = st[s], st[s]["bk"]
            n, x = v["n"], x_of(s)
            pe.wait_ge(sem(f"inputs{s}"), 48)
            pe_features(pe, s, "n_q", W["qkv"], 0, x)
            pe_features(pe, s, "n_k", W["qkv"], D, x)
            pe_tokens(pe, s, "n_v", W["qkv"], 2 * D, x)
            yield 1
            pe.wait_ge(sem(f"n_landmarks{s}"), 1)
            b = bk.claim(pe, "n_sim2")
            for p in range(PAIRS):
                c, h = p // 4, 2 * (p % 4)
                last = pe.matmul(b[:, p * M:(p + 1) * M], n["qlm"][:, c, h:h + 2, :], n["kl"][:, c, :], start=True, stop=True)
            last.then_inc(bk.filled("n_sim2"), 1)
            pe.wait_ge(sem(f"n_half{s}"), 4)
            for t in range(NT):
                for c in range(NC):
                    b = bk.claim(pe, f"n_max1_{t}{c}")
                    pe.matmul(b[:], n["qb"][:, c, t * P:(t + 1) * P], n["klmb"][:, c, :, :], start=True, stop=True)\
                        .then_inc(bk.filled(f"n_max1_{t}{c}"), 1)
            for i in range(4):
                b = bk.claim(pe, f"n_max3_{i}")
                for j in range(2):
                    p = 2 * i + j
                    c, h = p // 4, 2 * (p % 4)
                    last = pe.matmul(b[:, j * T:(j + 1) * T], n["qlmb"][:, c, h:h + 2, :], n["kb"][:, c, :], start=True, stop=True)
                last.then_inc(bk.filled(f"n_max3_{i}"), 1)
            yield 2
            pe.wait_ge(sem(f"n_neg{s}"), 1)
            b = bk.claim(pe, "n_negT")
            bb = b[:, 0:3 * P // 2].bitcast(BF16)
            for i in range(3):
                last = pe.transpose(bb[:, i * P:(i + 1) * P], n["neg"][:, i, :], identb[:])
            last.then_inc(bk.filled("n_negT"), 1)
            yield 3
            bk.await_emptied(pe, "n_negT")
            bk.await_emptied(pe, "n_k")
            for i in range(4):
                b = bk.claim(pe, f"n_s1_{i}")
                for j in range(2):
                    p = 2 * i + j
                    c, h = p // 4, 2 * (p % 4)
                    pe.matmul(b[:, j * T:(j + 1) * T], n["klm"][:, c, h:h + 2, :], n["q"][:, c, :], start=True, stop=False)
                    last = pe.matmul(b[:, j * T:(j + 1) * T], selp[:, p, :], n["negT"][:, 0:2, :], start=False, stop=True)
                last.then_inc(bk.filled(f"n_s1_{i}"), 1)
            for t in range(NT):
                for c in range(NC):
                    name = f"n_s3_{t}{c}"
                    b = bk.claim(pe, name)
                    pe.matmul(b[:], n["k"][:, c, t * P:(t + 1) * P], n["qlm"][:, c, :, :], start=True, stop=False)
                    for j in range(4):
                        last = pe.matmul(b[:, j * P:(j + 1) * P], sel16[:, 4 * c + j, :], n["negT"][:, 2, :],
                                         start=False, stop=j == 3)
                    last.then_inc(bk.filled(name), 1)
            yield 4
            pe.wait_ge(sem(f"n_a{s}"), 1)
            b = bk.claim(pe, "n_aT")
            for p in range(PAIRS):
                for u in (0, M):
                    last = pe.matmul(b[u:u + M, p * M:(p + 1) * M], n["a"][u:u + M, p, :], ident[u:u + M, u:u + M],
                                     start=True, stop=True)
            last.then_inc(bk.filled("n_aT"), 1)
            b = bk.claim(pe, "n_y")
            bk.await_emptied(pe, "n_v")
            pe.wait_ge(sem(f"n_vones{s}"), 1)
            bk.await_emptied(pe, "n_s3_11")
            for p in range(PAIRS):
                for t in range(NT):
                    last = pe.matmul(b[:, p * 2 * VW:(p + 1) * 2 * VW], n["e3"][:, t, p // 4, (p % 4) * P:(p % 4 + 1) * P],
                                     n["v"][:, t, 2 * p:2 * p + 2, :], start=t == 0, stop=t == NT - 1)
            last.then_inc(bk.filled("n_y"), 1)
            yield 5

            def heads(b, col, width, g, lhs, rhs):
                for p in range(4 * g, 4 * g + 4):
                    for u in (0, M):
                        last = pe.matmul(b[u:u + M, col + (p - 4 * g) * width:col + (p - 4 * g + 1) * width],
                                         lhs[u:u + M, p, :], rhs[u:u + M, p, :], start=True, stop=True)
                return last

            bk.await_emptied(pe, "n_aT")
            for g in range(2):
                b = bk.claim(pe, f"n_k0_{g}")
                heads(b, 0, M, g, n["aT"], n["a"]).then_inc(bk.filled(f"n_k0_{g}"), 1)
                b = bk.claim(pe, f"n_kT0_{g}")
                heads(b, 0, M, g, n["a"], n["aT"]).then_inc(bk.filled(f"n_kT0_{g}"), 1)
            for i in range(PINV_ITERS - 1):
                yield 6 + 3 * i
                for g in range(2):
                    bk.await_emptied(pe, f"n_k{i}_{g}")
                    bk.await_emptied(pe, f"n_kT{i}_{g}")
                    b = bk.claim(pe, f"n_p{i}_{g}")
                    heads(b, 0, M, g, n["kkT"], n["t1"]).then_inc(bk.filled(f"n_p{i}_{g}"), 1)
                yield 7 + 3 * i
                for g in range(2):
                    bk.await_emptied(pe, f"n_p{i}_{g}")
                    b = bk.claim(pe, f"n_t{i}_{g}")
                    heads(b, 0, M, g, n["t2"], n["kkT"]).then_inc(bk.filled(f"n_t{i}_{g}"), 1)
                yield 8 + 3 * i
                for g in range(2):
                    bk.await_emptied(pe, f"n_t{i}_{g}")
                    if i == 0:
                        bk.await_emptied(pe, "n_y")
                    b = bk.claim(pe, f"n_kT{i + 1}_{g}")
                    heads(b, 4 * M, DH0, g, n["t3"], n["z"])
                    heads(b, 0, M, g, n["kk"], n["t3"]).then_inc(bk.filled(f"n_kT{i + 1}_{g}"), 1)
                    if i < PINV_ITERS - 2:
                        b = bk.claim(pe, f"n_k{i + 1}_{g}")
                        heads(b, 0, M, g, n["t3"], n["kk"]).then_inc(bk.filled(f"n_k{i + 1}_{g}"), 1)
            yield 21
            for g in range(2):
                bk.await_emptied(pe, f"n_kT{PINV_ITERS - 1}_{g}")
            for j in range(4):
                if j:
                    yield 21 + j
                    bk.await_emptied(pe, f"n_w{j - 1}")
                b = bk.claim(pe, f"n_w{j}")
                for g in range(2):
                    last = heads(b, g * 4 * DH0, DH0, g, n["kkT"] if j < 3 else n["aT"], n["z"] if j == 0 else n["z2"])
                last.then_inc(bk.filled(f"n_w{j}"), 1)
            yield 25
            bk.await_emptied(pe, "n_w3")
            for t in range(NT):
                b = bk.claim(pe, f"n_o{t}")
                for p in range(PAIRS):
                    last = pe.matmul(b[:, p * 2 * VW:(p + 1) * 2 * VW], n["e1"][:, p, t * P:(t + 1) * P], n["g"][:, p, :],
                                     start=True, stop=True)
                last.then_inc(bk.filled(f"n_o{t}"), 1)
            yield 26
            bk.await_emptied(pe, "n_o0")
            bk.await_emptied(pe, "n_o1")
            pe_transposes(pe, s, "n_oT", n["o"])
            yield 27
            bk.await_emptied(pe, "n_oT")
            pe_tokens(pe, s, "n_out", W["out"], 0, n["oT"])
            yield 28
            pe_norm(pe, s, "0", "n_xT")

        def dve_nystrom(dve, s, link):
            v, bk = st[s], st[s]["bk"]
            n = v["n"]
            b = bk.await_filled(dve, "n_q")
            for m in range(NC):
                last = dve.tensor_scalar(n["q"][:, m, :], b[:, m * T:(m + 1) * T], bias["q0"][:, m:m + 1],
                                         1.0 / np.sqrt(DH0), ALU.add, ALU.mult)
            last.then_inc(bk.emptied("n_q"), 1)
            bk.await_emptied(dve, "n_q")
            dve.tensor_reduce(n["qs"][:], n["q"][:].rearrange("p c (m l) -> p c m l", l=LM), axis=AX.X, op=ALU.add)
            bk.await_emptied(dve, "n_k")
            link(dve.tensor_reduce(n["ks"][:], n["k"][:].rearrange("p c (m l) -> p c m l", l=LM), axis=AX.X, op=ALU.add))
            for c in range(NC):
                m = hmask[:, HC:2 * HC, None].to_broadcast([P, HC, M])
                dve.tensor_tensor(n["qlm"][:, c], n["qs"][:, c, None, :].to_broadcast([P, HC, M]), m, ALU.mult)
                dve.tensor_tensor(n["klm"][:, c], n["ks"][:, c, None, :].to_broadcast([P, HC, M]), m, ALU.mult)
            dve.tensor_scalar(n["kl"][:], n["ks"][:], 1.0 / LM, None, ALU.mult).then_inc(sem(f"n_landmarks{s}"), 1)
            b = bk.await_filled(dve, "n_v")
            dve.tensor_tensor(n["v"][:, :, :, 0:DH0], b[:].rearrange("p (t h d) -> p t h d", t=NT, h=H0),
                              rows["v0"][:].rearrange("p (h d) -> p h d", h=H0)[:, None].to_broadcast([P, NT, H0, DH0]),
                              ALU.add).then_inc(bk.emptied("n_v"), 1)
            yield 1
            b = bk.await_filled(dve, "n_sim2")
            b3 = b[:].rearrange("p (a m) -> p a m", m=M)
            link(dve.tensor_reduce(n["mx2"][:], b3, axis=AX.X, op=ALU.max))
            dve.tensor_tensor(n["a"][:], b3, n["mx2"][:, :, None].to_broadcast([P, PAIRS, M]), ALU.subtract)\
                .then_inc(bk.emptied("n_sim2"), 1)
            for t in range(NT):
                for c in range(NC):
                    b = bk.await_filled(dve, f"n_max1_{t}{c}")
                    dve.tensor_reduce(n["mx1"][:, t, c * HC:(c + 1) * HC], b[:].rearrange("p (h m) -> p h m", m=M),
                                      axis=AX.X, op=ALU.max).then_inc(bk.emptied(f"n_max1_{t}{c}"), 1)
            for i in range(4):
                b = bk.await_filled(dve, f"n_max3_{i}")
                dve.tensor_reduce(n["mx3"][:, 2 * i:2 * i + 2], b[:].rearrange("p (a t) -> p a t", t=T),
                                  axis=AX.X, op=ALU.max).then_inc(bk.emptied(f"n_max3_{i}"), 1)
            bk.await_emptied(dve, "n_max1_11")
            bk.await_emptied(dve, "n_max3_3")
            dve.wait_ge(sem(f"n_zeros{s}"), 1)
            dve.tensor_scalar(n["neg"][:, 0:2, 0:H0], n["mx1"][:], -1.0, None, ALU.mult)
            dve.tensor_scalar(n["neg"][:, 2, 0:PAIRS], n["mx3"][:], -1.0, None, ALU.mult).then_inc(sem(f"n_neg{s}"), 1)
            yield 2
            dve.wait_ge(sem(f"n_exp2{s}"), 1)
            link(dve.tensor_reduce(n["sum2"][:], n["a"][:], axis=AX.X, op=ALU.add))
            link(dve.reciprocal(n["rs2"][:], n["sum2"][:]))
            dve.tensor_tensor(n["a"][:], n["a"][:], n["rs2"][:, :, None].to_broadcast([P, PAIRS, M]), ALU.mult)\
                .then_inc(sem(f"n_a{s}"), 1)
            yield 4
            b = bk.await_filled(dve, "n_y")
            y = b[:, 0:PAIRS * 2 * VW].rearrange("p (a w) -> p a w", w=2 * VW)
            for u in range(2):
                last = dve.reciprocal(n["ry"][u * M:(u + 1) * M, :], y[u * M:(u + 1) * M, :, u * VW + DH0])
            link(last)
            for u in range(2):
                r = slice(u * M, (u + 1) * M)
                last = dve.tensor_tensor(n["z"][r], y[r, :, u * VW:u * VW + DH0],
                                         n["ry"][r, :, None].to_broadcast([M, PAIRS, DH0]), ALU.mult)
            last.then_inc(bk.emptied("n_y"), 1)
            eye = consts["eye"][:, None, :].to_broadcast([P, 4, M])
            eye325 = consts["eye325"][:, None, :].to_broadcast([P, 4, M])

            def part(b, g):
                return b[:, 0:4 * M].rearrange("p (a m) -> p a m", m=M)

            for i in range(PINV_ITERS - 1):
                yield 5 + 3 * i
                for g in range(2):
                    q = slice(4 * g, 4 * g + 4)
                    b = bk.await_filled(dve, f"n_k{i}_{g}")
                    if i == 0:
                        bk.await_done(dve, "n_y")
                    dve.tensor_copy(n["kk"][:, q], part(b, g))
                    dve.scalar_tensor_tensor(n["t1"][:, q], eye, 7.0, part(b, g), ALU.mult, ALU.subtract)\
                        .then_inc(bk.emptied(f"n_k{i}_{g}"), 1)
                yield 6 + 3 * i
                for g in range(2):
                    q = slice(4 * g, 4 * g + 4)
                    b = bk.await_filled(dve, f"n_p{i}_{g}")
                    dve.scalar_tensor_tensor(n["t2"][:, q], eye, 15.0, part(b, g), ALU.mult, ALU.subtract)\
                        .then_inc(bk.emptied(f"n_p{i}_{g}"), 1)
                yield 7 + 3 * i
                for g in range(2):
                    q = slice(4 * g, 4 * g + 4)
                    b = bk.await_filled(dve, f"n_t{i}_{g}")
                    dve.scalar_tensor_tensor(n["t3"][:, q], part(b, g), -0.25, eye325, ALU.mult, ALU.add)\
                        .then_inc(bk.emptied(f"n_t{i}_{g}"), 1)
            for j in range(4):
                yield 21 + j
                b = bk.await_filled(dve, f"n_w{j}")
                w = b[:, 0:PAIRS * DH0].rearrange("p (a d) -> p a d", d=DH0)
                if j < 3:
                    dve.scalar_tensor_tensor(n["z2"][:], n["z"][:], (7.0, 15.0, 13.0)[j], w, ALU.mult, ALU.subtract)\
                        .then_inc(bk.emptied(f"n_w{j}"), 1)
                else:
                    dve.wait_ge(sem(f"n_vones{s}"), 1)
                    for u in range(2):
                        r = slice(u * M, (u + 1) * M)
                        last = dve.tensor_scalar(n["g"][r, :, u * VW:u * VW + DH0], w[r], 0.25, None, ALU.mult)
                    last.then_inc(bk.emptied(f"n_w{j}"), 1)
            yield 25
            for t in range(NT):
                b = bk.await_filled(dve, f"n_o{t}")
                o = b[:, 0:H0 * VW].rearrange("p (h w) -> p h w", w=VW)
                link(dve.reciprocal(n["ro"][:, t, :], o[:, :, DH0]))
                dve.tensor_tensor(n["o"][:, t].rearrange("p (h d) -> p h d", h=H0), o[:, :, 0:DH0],
                                  n["ro"][:, t, :, None].to_broadcast([P, H0, DH0]), ALU.mult)\
                    .then_inc(bk.emptied(f"n_o{t}"), 1)
            yield 27
            dve_residual_norm(dve, s, link, "n_out", "0")

        def act_nystrom(act, s):
            v, bk = st[s], st[s]["bk"]
            n = v["n"]
            b = bk.await_filled(act, "n_k")
            for m in range(NC):
                last = act.activation(n["k"][:, m, :], b[:, m * T:(m + 1) * T], ACT.Identity, bias=bias["k0"][:, m:m + 1])
            last.then_inc(bk.emptied("n_k"), 1)
            yield 1
            bk.await_emptied(act, "n_sim2")
            act.activation(n["a"][:], n["a"][:], ACT.Exp).then_inc(sem(f"n_exp2{s}"), 1)
            yield 2
            b = bk.await_filled(act, "n_negT")
            act.copy(n["negT"][:].rearrange("p a b -> p (a b)"), b[:, 0:3 * P // 2].bitcast(BF16))\
                .then_inc(bk.emptied("n_negT"), 1)
            yield 3
            for i in range(4):
                b = bk.await_filled(act, f"n_s1_{i}")
                act.activation(n["e1"][:, 2 * i:2 * i + 2, :], b[:].rearrange("p (a t) -> p a t", t=T), ACT.Exp)\
                    .then_inc(bk.emptied(f"n_s1_{i}"), 1)
            for t in range(NT):
                for c in range(NC):
                    b = bk.await_filled(act, f"n_s3_{t}{c}")
                    act.activation(n["e3"][:, t, c, :], b[:], ACT.Exp).then_inc(bk.emptied(f"n_s3_{t}{c}"), 1)
            yield 4
            b = bk.await_filled(act, "n_aT")
            act.copy(n["aT"][:], b[:].rearrange("p (a m) -> p a m", m=M)).then_inc(bk.emptied("n_aT"), 1)
            for i in range(PINV_ITERS):
                yield 5 + 3 * i
                for g in range(2):
                    q = slice(4 * g, 4 * g + 4)
                    b = bk.await_filled(act, f"n_kT{i}_{g}")
                    if i:
                        act.copy(n["z"][:, q], b[:, 4 * M:4 * M + 4 * DH0].rearrange("p (a d) -> p a d", d=DH0))
                    act.copy(n["kkT"][:, q], b[:, 0:4 * M].rearrange("p (a m) -> p a m", m=M))\
                        .then_inc(bk.emptied(f"n_kT{i}_{g}"), 1)
            yield 26
            b = bk.await_filled(act, "n_oT")
            act.copy(n["oT"][:].rearrange("p c t -> p (c t)"), b[:]).then_inc(bk.emptied("n_oT"), 1)
            yield 28
            act_norm(act, s, "n_xT")

        def pool_nystrom(pool, s):
            v, bk = st[s], st[s]["bk"]
            n = v["n"]
            pool.wait_ge(sem(f"inputs{s}"), 48)
            pool.memset(n["neg"][:], 0.0).then_inc(sem(f"n_zeros{s}"), 1)
            pool.tensor_tensor(out=v["res"][:], in0=v["x"][:], in1=rows["o0"][:, None, :].to_broadcast([P, NT, D]),
                               op=ALU.add).then_inc(sem(f"res{s}"), 1)
            pool.memset(n["v"][:, :, :, DH0], 1.0)
            pool.memset(n["g"][:], 0.0).then_inc(sem(f"n_gz{s}"), 1)
            pool.wait_ge(sem(f"n_gz{s}"), 1)
            pool.memset(n["g"][0:M, :, DH0], 1.0)
            pool.memset(n["g"][M:P, :, VW + DH0], 1.0).then_inc(sem(f"n_vones{s}"), 1)
            pool.wait_ge(sem(f"n_vones{s}"), 1)
            bk.await_emptied(pool, "n_q")
            pool.tensor_copy(n["qb"][:], n["q"][:]).then_inc(sem(f"n_half{s}"), 1)
            bk.await_emptied(pool, "n_k")
            pool.tensor_copy(n["kb"][:], n["k"][:]).then_inc(sem(f"n_half{s}"), 1)
            pool.wait_ge(sem(f"n_landmarks{s}"), 1)
            pool.tensor_copy(n["klmb"][:], n["klm"][:]).then_inc(sem(f"n_half{s}"), 1)
            pool.tensor_copy(n["qlmb"][:], n["qlm"][:]).then_inc(sem(f"n_half{s}"), 1)
            yield 27
            pool_norm(pool, s, "0")

        def dve_norm(dve, s, link, key, src, dst):
            v = st[s]
            for t in range(NT):
                last = dve.bn_stats(v["st"][:, t, :], src[:, t, :])
            link(last)
            for t in range(NT):
                last = dve.bn_aggr(v["mv"][:, t, :], v["st"][:, t, :])
            link(last)
            dve.tensor_scalar(v["ve"][:], v["mv"][:, :, 1], EPS, None, ALU.add).then_inc(sem(f"variance{key}_{s}"), 1)
            dve.wait_ge(sem(f"rstd{key}_{s}"), 1)
            for t in range(NT):
                last = dve.tensor_scalar(dst[:, t, :], src[:, t, :], v["mv"][:, t, 0:1], v["rstd"][:, t:t + 1],
                                         ALU.subtract, ALU.mult)
            last.then_inc(sem(f"x{key}_{s}"), 1)

        def dve_residual_norm(dve, s, link, name, key):
            v, bk = st[s], st[s]["bk"]
            b = bk.await_filled(dve, name)
            dve.wait_ge(sem(f"res{s}"), 1 + int(key))
            dve.tensor_tensor(v["y"][:].rearrange("p t d -> p (t d)"), b[:], v["res"][:].rearrange("p t d -> p (t d)"),
                              ALU.add).then_inc(bk.emptied(name), 1)
            bk.await_emptied(dve, name)
            dve_norm(dve, s, link, key, v["y"], v["x"])

        def pool_norm(pool, s, key):
            v = st[s]
            pool.wait_ge(sem(f"variance{key}_{s}"), 1)
            pool.tensor_tensor(out=v["rstd"][:], in0=v["ve"][:], in1=NEGH[:], op=ALU.pow)\
                .then_inc(sem(f"rstd{key}_{s}"), 1)

        def pe_norm(pe, s, key, name):
            pe.wait_ge(sem(f"x{key}_{s}"), 1)
            pe_transposes(pe, s, name, st[s]["x"])

        def act_norm(act, s, name):
            v, bk = st[s], st[s]["bk"]
            b = bk.await_filled(act, name)
            act.copy(x_of(s), b[:].rearrange("p (c t) -> p c t", c=NC)).then_inc(bk.emptied(name), 1)

        def pe_dilated(pe, s):
            v, bk = st[s], st[s]["bk"]
            n, x = v["d"], x_of(s)
            yield 100
            bk.await_emptied(pe, "n_xT")
            pe_features(pe, s, "d_q", W["dq"], 0, x)
            pe_features(pe, s, "d_k", W["dk"], 0, v["ctx"])
            pe_tokens(pe, s, "d_v", W["dv"], 0, v["ctx"])
            for c in range(NC):
                yield 110 + 10 * c
                pe.wait_ge(sem(f"d_half{s}"), 2 + c)
                for i in range(6):
                    t, heads, keys = (0, range(4 * i, 4 * i + 4), P) if i < 2 else (1, range(2 * i - 4, 2 * i - 2), T)
                    b = bk.claim(pe, f"d_m{c}_{i}")
                    for j, h in enumerate(heads):
                        pe.matmul(b[:, j * keys:(j + 1) * keys], n["qmb"][:, h, t * P:(t + 1) * P], n["kb"][:, c, 0:keys],
                                  start=True, stop=False)
                        last = pe.matmul(b[:, (j + 1) * keys - P:(j + 1) * keys], identb[:], consts["above"][:],
                                         start=False, stop=True)
                    last.then_inc(bk.filled(f"d_m{c}_{i}"), 1)
                yield 111 + 10 * c
                pe.wait_ge(sem(f"d_neg{s}"), 1 + c)
                b = bk.claim(pe, f"d_negT{c}")
                bb = b[:, 0:P].bitcast(BF16)
                for t in range(NT):
                    last = pe.transpose(bb[:, t * P:(t + 1) * P], n["neg"][:, t, :], identb[:])
                last.then_inc(bk.filled(f"d_negT{c}"), 1)
                yield 112 + 10 * c
                pe.wait_ge(sem(f"d_qm{s}"), 1 + c)
                bk.await_emptied(pe, f"d_negT{c}")
                bk.await_emptied(pe, "d_k")
                for i in range(6):
                    b = bk.claim(pe, f"d_s{c}_{i}")
                    if i < 4:
                        pe.matmul(b[:], n["k"][:, c, 0:P], n["qm"][:, 2 * i:2 * i + 2, :], start=True, stop=False)
                        for j in range(2):
                            pe.matmul(b[:, j * T:(j + 1) * T], sel16[:, c * HC + 2 * i + j, :], n["negT"][:, 0:2, :],
                                      start=False, stop=False)
                            last = pe.matmul(b[:, j * T:j * T + P], identb[:], consts["below"][:], start=False, stop=j == 1)
                    else:
                        h = 4 * (i - 4)
                        pe.matmul(b[:], n["k"][:, c, P:T], n["qm"][:, h:h + 4, P:T], start=True, stop=False)
                        for j in range(4):
                            pe.matmul(b[:, j * P:(j + 1) * P], sel16[:, c * HC + h + j, :], n["negT"][:, 1, :],
                                      start=False, stop=False)
                            last = pe.matmul(b[:, j * P:(j + 1) * P], identb[:], consts["below"][:], start=False, stop=j == 3)
                    last.then_inc(bk.filled(f"d_s{c}_{i}"), 1)
                yield 113 + 10 * c
                pe.wait_ge(sem(f"d_v{s}"), 2)
                bk.await_emptied(pe, f"d_s{c}_5")
                for t in range(NT):
                    b = bk.claim(pe, f"d_o{c}_{t}")
                    for h in range(HC):
                        out = b[:, h * BR * VW:(h + 1) * BR * VW]
                        last = pe.matmul(out, n["p0"][:, h, t * P:(t + 1) * P], n["v"][:, 0, c * HC + h, :, :],
                                         start=True, stop=t == 0)
                        if t:
                            last = pe.matmul(out, n["p1"][:, h, :], n["v"][:, 1, c * HC + h, :, :], start=False, stop=True)
                    last.then_inc(bk.filled(f"d_o{c}_{t}"), 1)
            yield 131
            pe.wait_ge(sem(f"d_o{s}"), 1)
            pe_transposes(pe, s, "d_oT", n["o"])
            yield 132
            bk.await_emptied(pe, "d_oT")
            pe_tokens(pe, s, "d_out", W["do"], 0, n["oT"])
            yield 133
            pe_norm(pe, s, "1", "d_xT")

        def dve_dilated(dve, s, link):
            v, bk = st[s], st[s]["bk"]
            n = v["d"]
            yield 100
            b = bk.await_filled(dve, "d_q")
            for m in range(NC):
                last = dve.tensor_scalar(n["q"][:, m, :], b[:, m * T:(m + 1) * T], bias["dq"][:, m:m + 1],
                                         float(DH0) ** -0.5, ALU.add, ALU.mult)
            last.then_inc(bk.emptied("d_q"), 1)
            b = bk.await_filled(dve, "d_v")
            dve.tensor_tensor(n["v"][:, :, :, 0, 0:DH0], b[:].rearrange("p (t h d) -> p t h d", t=NT, h=H0),
                              rows["dv"][:].rearrange("p (h d) -> p h d", h=H0)[:, None].to_broadcast([P, NT, H0, DH0]),
                              ALU.add).then_inc(bk.emptied("d_v"), 1)
            for c in range(NC):
                yield 110 + 10 * c
                bk.await_emptied(dve, "d_q")
                if c:
                    bk.await_done(dve, f"d_s{c - 1}_5")
                dve.tensor_tensor(n["qm"][:], n["q"][:, c, None, :].to_broadcast([P, HC, T]),
                                  hmask[:, 0:HC, None].to_broadcast([P, HC, T]), ALU.mult).then_inc(sem(f"d_qm{s}"), 1)
                for i in range(6):
                    b = bk.await_filled(dve, f"d_m{c}_{i}")
                    t, h, k = (0, 4 * i, 4) if i < 2 else (1, 2 * i - 4, 2)
                    dve.tensor_reduce(n["mx"][:, t, c * HC + h:c * HC + h + k], b[:].rearrange("p (h k) -> p h k", h=k),
                                      axis=AX.X, op=ALU.max).then_inc(bk.emptied(f"d_m{c}_{i}"), 1)
                for i in (3, 4, 5):
                    bk.await_emptied(dve, f"d_m{c}_{i}")
                dve.wait_ge(sem(f"d_v{s}"), 1)
                if c:
                    bk.await_done(dve, f"d_negT{c - 1}")
                dve.tensor_scalar(n["neg"][:, :, c * HC:(c + 1) * HC], n["mx"][:, :, c * HC:(c + 1) * HC], -1.0, None,
                                  ALU.mult).then_inc(sem(f"d_neg{s}"), 1)
            yield 130
            for c in range(NC):
                for t in range(NT):
                    bk.await_emptied(dve, f"d_o{c}_{t}")
            dve.tensor_scalar(n["s"][:].rearrange("p t h b -> p (t h b)"),
                              n["n"][:].rearrange("p t h b w -> p (t h b) w")[:, :, DH0], TINY, None, ALU.max)\
                .then_inc(sem(f"d_sum{s}"), 1)
            valid = consts["valid"][:].rearrange("p (h b) -> p h b", b=BR)[:, None].to_broadcast([P, NT, H0, BR])
            allh = [P, NT * H0, BR]

            def flat(key):
                return n[key][:].rearrange("p t h b -> p (t h) b")

            lm = n["lm"][:].rearrange("p t h -> p (t h)")
            rz = n["rz"][:].rearrange("p t h -> p (t h)")
            dve.wait_ge(sem(f"d_sum{s}"), 2)
            for t in range(NT):
                last = dve.tensor_tensor(n["ls"][:, t], n["ls"][:, t], n["neg"][:, t, 0:H0, None].to_broadcast([P, H0, BR]),
                                         ALU.subtract)
            link(last)
            link(dve.tensor_tensor(n["ls"][:], n["ls"][:], valid, ALU.mult))
            link(dve.tensor_scalar(n["isz"][:], n["ls"][:], 0.0, NEG, ALU.is_equal, ALU.mult))
            link(dve.tensor_tensor(n["ls"][:], n["ls"][:], n["isz"][:], ALU.add))
            link(dve.tensor_reduce(lm, flat("ls"), axis=AX.X, op=ALU.max))
            dve.tensor_tensor(flat("w"), flat("ls"), lm[:, :, None].to_broadcast(allh), ALU.subtract)\
                .then_inc(sem(f"d_sum{s}"), 1)
            dve.wait_ge(sem(f"d_sum{s}"), 4)
            link(dve.tensor_reduce(lm, flat("w"), axis=AX.X, op=ALU.add))
            dve.reciprocal(rz, lm)
            link(dve.reciprocal(n["rc"][:], n["s"][:]))
            link(dve.tensor_tensor(flat("w"), flat("w"), rz[:, :, None].to_broadcast(allh), ALU.mult))
            link(dve.tensor_tensor(n["w"][:], n["w"][:], valid, ALU.mult))
            link(dve.tensor_tensor(n["w"][:], n["w"][:], n["rc"][:], ALU.mult))
            for t in range(NT):
                r = n["n"][:, t].rearrange("p h b w -> p (h b) w")[:, :, 0:DH0]
                last = dve.tensor_tensor(r, r, n["w"][:, t].rearrange("p h b -> p (h b)")[:, :, None]
                                         .to_broadcast([P, H0 * BR, DH0]), ALU.mult)
            link(last)
            for t in range(NT):
                last = dve.tensor_reduce(n["o"][:, t].rearrange("p (h d) -> p h d", h=H0),
                                         n["n"][:, t].rearrange("p h b w -> p h w b")[:, :, 0:DH0, :], axis=AX.X, op=ALU.add)
            last.then_inc(sem(f"d_o{s}"), 1)
            yield 132
            dve_residual_norm(dve, s, link, "d_out", "1")

        def act_dilated(act, s):
            v, bk = st[s], st[s]["bk"]
            n = v["d"]
            yield 100
            b = bk.await_filled(act, "d_k")
            for m in range(NC):
                last = act.activation(n["k"][:, m, :], b[:, m * T:(m + 1) * T], ACT.Identity, bias=bias["dk"][:, m:m + 1])
            last.then_inc(bk.emptied("d_k"), 1)
            for c in range(NC):
                yield 111 + 10 * c
                b = bk.await_filled(act, f"d_negT{c}")
                act.copy(n["negT"][:].rearrange("p a b -> p (a b)"), b[:, 0:P].bitcast(BF16))\
                    .then_inc(bk.emptied(f"d_negT{c}"), 1)
                yield 112 + 10 * c
                if c:
                    bk.await_done(act, f"d_o{c - 1}_1")
                for i in range(6):
                    b = bk.await_filled(act, f"d_s{c}_{i}")
                    if i < 4:
                        out = n["p0"][:, 2 * i:2 * i + 2, :].rearrange("p h t -> p (h t)")
                    else:
                        out = n["p1"][:, 4 * i - 16:4 * i - 12, :].rearrange("p h t -> p (h t)")
                    act.activation(out, b[:], ACT.Exp).then_inc(bk.emptied(f"d_s{c}_{i}"), 1)
                yield 113 + 10 * c
                for t in range(NT):
                    b = bk.await_filled(act, f"d_o{c}_{t}")
                    act.copy(n["n"][:, t, c * HC:(c + 1) * HC].rearrange("p h b w -> p (h b w)"), b[:, 0:HC * BR * VW])\
                        .then_inc(bk.emptied(f"d_o{c}_{t}"), 1)
            yield 130
            act.wait_ge(sem(f"d_sum{s}"), 1)
            act.activation(n["ls"][:], n["s"][:], ACT.Ln).then_inc(sem(f"d_sum{s}"), 1)
            act.wait_ge(sem(f"d_sum{s}"), 3)
            act.activation(n["w"][:], n["w"][:], ACT.Exp).then_inc(sem(f"d_sum{s}"), 1)
            yield 131
            b = bk.await_filled(act, "d_oT")
            act.copy(n["oT"][:].rearrange("p c t -> p (c t)"), b[:]).then_inc(bk.emptied("d_oT"), 1)
            yield 133
            act_norm(act, s, "d_xT")

        def pool_dilated(pool, s):
            v, bk = st[s], st[s]["bk"]
            n = v["d"]
            yield 100
            pool.wait_ge(sem(f"x0_{s}"), 1)
            pool.tensor_tensor(out=v["res"][:], in0=v["x"][:], in1=rows["do"][:, None, :].to_broadcast([P, NT, D]),
                               op=ALU.add).then_inc(sem(f"res{s}"), 1)
            pool.memset(n["neg"][:], 0.0).then_inc(sem(f"d_v{s}"), 1)
            bk.await_emptied(pool, "d_k")
            pool.tensor_copy(n["kb"][:], n["k"][:]).then_inc(sem(f"d_half{s}"), 1)
            for c in range(NC):
                if c:
                    yield 110 + 10 * c
                bk.await_emptied(pool, "d_q")
                if c:
                    bk.await_done(pool, f"d_m{c - 1}_5")
                pool.tensor_tensor(out=n["qmb"][:], in0=n["q"][:, c, None, :].to_broadcast([P, HC, T]),
                                   in1=hmask[:, 0:HC, None].to_broadcast([P, HC, T]), op=ALU.mult)\
                    .then_inc(sem(f"d_half{s}"), 1)
                if c == 0:
                    bk.await_emptied(pool, "d_v")
                    pool.memset(n["v"][:, :, :, 0, DH0], 1.0).then_inc(sem(f"d_ones{s}"), 1)
                    pool.wait_ge(sem(f"d_ones{s}"), 1)
                    valid = consts["valid"][:].rearrange("p (h b) -> p h b", b=BR)
                    for br in range(1, BR):
                        last = pool.tensor_tensor(out=n["v"][:, :, :, br, :], in0=n["v"][:, :, :, 0, :],
                                                  in1=valid[:, None, :, br, None].to_broadcast([P, NT, H0, VW]), op=ALU.mult)
                    last.then_inc(sem(f"d_v{s}"), 1)
            yield 132
            pool_norm(pool, s, "1")

        def pe_ffn(pe, s):
            v, bk = st[s], st[s]["bk"]
            n, x = v["f"], x_of(s)
            yield 200
            bk.await_emptied(pe, "d_xT")
            for i in range(FC // 2):
                b = bk.claim(pe, f"f_h{i}")
                for j in range(2):
                    f = 2 * i + j
                    for c in range(NC):
                        last = pe.matmul(b[:, j * T:(j + 1) * T], W["ff1"][:, c, f * P:(f + 1) * P], x[:, c, :],
                                         start=c == 0, stop=c == NC - 1)
                last.then_inc(bk.filled(f"f_h{i}"), 1)
            yield 201
            for i in range(FC // 2):
                bk.await_emptied(pe, f"f_h{i}")
            pe_tokens(pe, s, "f_out", w2, 0, n["h"], FC)
            yield 202
            pe_norm(pe, s, "2", "f_xT")

        def act_ffn(act, s):
            v, bk = st[s], st[s]["bk"]
            n = v["f"]
            yield 200
            for i in range(FC // 2):
                b = bk.await_filled(act, f"f_h{i}")
                for j in range(2):
                    f = 2 * i + j
                    last = act.activation(n["h"][:, f, :], b[:, j * T:(j + 1) * T], ACT.Gelu, bias=bias["ff1"][:, f:f + 1])
                last.then_inc(bk.emptied(f"f_h{i}"), 1)
            yield 202
            act_norm(act, s, "f_xT")

        def dve_ffn(dve, s, link):
            yield 201
            dve_residual_norm(dve, s, link, "f_out", "2")

        def pool_ffn(pool, s):
            v = st[s]
            yield 200
            pool.wait_ge(sem(f"x1_{s}"), 1)
            pool.tensor_tensor(out=v["res"][:], in0=v["x"][:], in1=rows["ff2"][:, None, :].to_broadcast([P, NT, D]),
                               op=ALU.add).then_inc(sem(f"res{s}"), 1)
            yield 201
            pool_norm(pool, s, "2")

        def pe_memory(pe, s):
            v, bk = st[s], st[s]["bk"]
            n, xz, x = v["r"], v["xz"], x_of(s)
            yield 300
            bk.await_emptied(pe, "f_xT")
            pe_tokens(pe, s, "r_v", W["mw"], 0, x)
            for i in range(4):
                r = slice(HD1 * (i % 2), HD1 * (i % 2 + 1))
                b = bk.claim(pe, f"r_s{i}")
                for c in range(NC):
                    if i < 2:
                        last = pe.matmul(b[:, c * T:(c + 1) * T], xz[r, c, 0:P], xz[r, c, 1:T + 1], start=True, stop=True)
                    else:
                        last = pe.matmul(b[:, c * P:(c + 1) * P], xz[r, c, P:T], xz[r, c, P + 1:T + 1], start=True, stop=True)
                last.then_inc(bk.filled(f"r_s{i}"), 1)
            yield 301
            for name in ("r_v", "r_s0", "r_s1", "r_s2", "r_s3"):
                bk.await_emptied(pe, name)
            b = bk.claim(pe, "r_r")
            for h in range(H1):
                r, c = slice(HD1 * (h % 2), HD1 * (h % 2 + 1)), h // 2
                pe.matmul(b[r, c * T:(c + 1) * T], n["v"][:, 0, h * HD1:(h + 1) * HD1], n["s0"][:, h, :],
                          start=True, stop=False)
                last = pe.matmul(b[r, c * T + P:(c + 1) * T], n["v"][:, 1, h * HD1:(h + 1) * HD1], n["s1"][:, h, :],
                                 start=False, stop=True)
            last.then_inc(bk.filled("r_r"), 1)
            yield 302
            bk.await_emptied(pe, "r_r")
            pe_tokens(pe, s, "r_out", W["mr"], 0, n["r"])
            yield 303
            pe_norm(pe, s, "3", "r_xT")

        def act_memory(act, s):
            v, bk = st[s], st[s]["bk"]
            n = v["r"]
            yield 300
            b = bk.await_filled(act, "r_v")
            act.copy(n["v"][:].rearrange("p t d -> p (t d)"), b[:]).then_inc(bk.emptied("r_v"), 1)
            yield 301
            b = bk.await_filled(act, "r_r")
            act.copy(n["r"][:].rearrange("p c t -> p (c t)"), b[:]).then_inc(bk.emptied("r_r"), 1)
            yield 303
            act_norm(act, s, "r_xT")

        def dve_memory(dve, s, link):
            v, bk = st[s], st[s]["bk"]
            n = v["r"]
            yield 300
            for i in range(4):
                b = bk.await_filled(dve, f"r_s{i}")
                out, table, t = (n["s0"], dec0, T) if i < 2 else (n["s1"], dec1, P)
                dve.tensor_tensor(out[:, i % 2::2, :], b[:, 0:NC * t].rearrange("p (h t) -> p h t", t=t),
                                  table[:, i % 2::2, :], ALU.mult).then_inc(bk.emptied(f"r_s{i}"), 1)
            yield 302
            dve_residual_norm(dve, s, link, "r_out", "3")

        def pool_memory(pool, s):
            v = st[s]
            yield 300
            pool.wait_ge(sem(f"x2_{s}"), 1)
            pool.tensor_tensor(out=v["res"][:], in0=v["x"][:], in1=v["x"][:], op=ALU.add).then_inc(sem(f"res{s}"), 1)
            yield 302
            pool_norm(pool, s, "3")

        ROPES = (("ka", "kar", "ctx", "cosk", "sink"), ("kt", "ktr", "ctx", "cosk", "sink"),
                 ("qa", "qar", "x", "cosq", "sinq"), ("qt", "qtr", "x", "cosg", "sing"))

        def pe_gated(pe, s):
            v, bk = st[s], st[s]["bk"]
            n, x = v["g"], x_of(s)
            yield 400
            bk.await_emptied(pe, "r_xT")
            for key, rot, src, _, _ in ROPES:
                for k in (key, rot):
                    pe_features(pe, s, "g_" + k, W[k], 0, x if src == "x" else v["ctx"])
            pe_tokens(pe, s, "g_va", W["va"], 0, v["ctx"])
            pe_tokens(pe, s, "g_vt", W["vt"], 0, v["ctx"])
            yield 401
            pe.wait_ge(sem(f"g_rope{s}"), 2 * len(ROPES))
            for h in range(H2):
                r, c = slice(HD2 * (h % 4), HD2 * (h % 4 + 1)), h // 4
                for t in range(NT):
                    b = bk.claim(pe, f"g_m{h}_{t}")
                    pe.matmul(b[:, 0:T], n["qab"][r, c, t * P:(t + 1) * P], n["kab"][r, c, :], start=True, stop=True)
                    pe.matmul(b[:, T:2 * T], n["qtb"][r, c, t * P:(t + 1) * P], n["ktb"][r, c, :], start=True, stop=True)\
                        .then_inc(bk.filled(f"g_m{h}_{t}"), 1)
            yield 402
            pe.wait_ge(sem(f"g_neg{s}"), 1)
            b = bk.claim(pe, "g_negT")
            bb = b[:, 0:P].bitcast(BF16)
            for t in range(NT):
                last = pe.transpose(bb[:, t * P:(t + 1) * P], n["neg"][:, t].rearrange("p a b -> p (a b)"), identb[:])
            last.then_inc(bk.filled("g_negT"), 1)

            def values(h):
                for i in range(2):
                    bk.await_emptied(pe, f"g_s{h}_{i}")
                for t in range(NT):
                    for k in range(KT2):
                        last = pe.matmul(o[t][:, h * VW2:(h + 1) * VW2], n["p"][:, h % 2, k, t * P:(t + 1) * P],
                                         n["v"][:, k, h, :], start=k == 0, stop=k == KT2 - 1)
                    if h == H2 - 1:
                        last.then_inc(bk.filled(f"g_o{t}"), 1)

            for h in range(H2):
                yield 410 + h
                if h == 0:
                    bk.await_emptied(pe, "g_negT")
                    bk.await_emptied(pe, "g_vt")
                    pe.wait_ge(sem(f"g_ones{s}"), 1)
                    o = [bk.claim(pe, f"g_o{t}") for t in range(NT)]
                r, c = slice(HD2 * (h % 4), HD2 * (h % 4 + 1)), h // 4
                for i, (k, q) in enumerate((("ka", "qa"), ("kt", "qt"))):
                    b = bk.claim(pe, f"g_s{h}_{i}")
                    for j in range(NT):
                        pe.matmul(b[:, j * T:(j + 1) * T], n[k][r, c, j * P:(j + 1) * P], n[q][r, c, :], start=True, stop=False)
                        last = pe.matmul(b[:, j * T:(j + 1) * T], selg[r, h, :], n["negT"][r, :, :], start=False, stop=True)
                    last.then_inc(bk.filled(f"g_s{h}_{i}"), 1)
                if h:
                    values(h - 1)
            yield 410 + H2
            values(H2 - 1)
            yield 419
            for t in range(NT):
                bk.await_emptied(pe, f"g_o{t}")
            pe_transposes(pe, s, "g_oT", n["o"])
            yield 420
            bk.await_emptied(pe, "g_oT")
            pe_tokens(pe, s, "g_out", W["go"], 0, n["oT"])
            yield 421
            pe.wait_ge(sem(f"x4_{s}"), 1)
            pe_transposes(pe, s, "g_nT", n["n"])
            yield 422
            bk.await_emptied(pe, "g_nT")
            pe_tokens(pe, s, "g_ffn", W["gf"], 0, n["nT"])

        def dve_gated(dve, s, link):
            v, bk = st[s], st[s]["bk"]
            n = v["g"]
            yield 400
            tables = {"cosg": cosg, "sing": sing, **{k: consts[k] for k in ("cosk", "sink", "cosq", "sinq")}}
            for i, (key, rot, _, cos, sin) in enumerate(ROPES):
                if i:
                    dve.wait_ge(sem(f"g_rope{s}"), 2 * i - 1)
                for k, dst, table in ((key, "ra", cos), (rot, "rb", sin)):
                    b = bk.await_filled(dve, "g_" + k)
                    for m in range(NC):
                        last = dve.scalar_tensor_tensor(n[dst][:, m, :], b[:, m * T:(m + 1) * T], bias[k][:, m:m + 1],
                                                        tables[table][:], ALU.add, ALU.mult)
                    last.then_inc(bk.emptied("g_" + k), 1)
            for i, k in enumerate(("va", "vt")):
                b = bk.await_filled(dve, "g_" + k)
                dve.tensor_tensor(n["v"][:, 2 * i:2 * i + 2, :, 0:HD2], b[:].rearrange("p (t h d) -> p t h d", t=NT, h=H2),
                                  rows[k][:].rearrange("p (h d) -> p h d", h=H2)[:, None].to_broadcast([P, NT, H2, HD2]),
                                  ALU.add).then_inc(bk.emptied("g_" + k), 1)
            yield 401
            for h in range(H2):
                for t in range(NT):
                    b = bk.await_filled(dve, f"g_m{h}_{t}")
                    dve.tensor_reduce(n["mx"][:, t, h:h + 1], b[:], axis=AX.X, op=ALU.max)\
                        .then_inc(bk.emptied(f"g_m{h}_{t}"), 1)
            for h in (H2 - 2, H2 - 1):
                for t in range(NT):
                    bk.await_emptied(dve, f"g_m{h}_{t}")
            dve.wait_ge(sem(f"g_ones{s}"), 1)
            dve.tensor_scalar(n["neg"][:, :, :, 0:H2], n["mx"][:, :, None, :].to_broadcast([P, NT, 4, H2]), -1.0, None,
                              ALU.mult).then_inc(sem(f"g_neg{s}"), 1)
            yield 418
            for t in range(NT):
                b = bk.await_filled(dve, f"g_o{t}")
                o = b[:, 0:H2 * VW2].rearrange("p (h w) -> p h w", w=VW2)
                link(dve.reciprocal(n["ro"][:, t, :], o[:, :, HD2]))
                dve.tensor_tensor(n["o"][:, t].rearrange("p (h d) -> p h d", h=H2), o[:, :, 0:HD2],
                                  n["ro"][:, t, :, None].to_broadcast([P, H2, HD2]), ALU.mult)\
                    .then_inc(bk.emptied(f"g_o{t}"), 1)
            yield 420
            b = bk.await_filled(dve, "g_out")
            dve.wait_ge(sem(f"res{s}"), 5)
            dve.tensor_tensor(n["u"][:].rearrange("p t d -> p (t d)"), b[:], v["res"][:].rearrange("p t d -> p (t d)"),
                              ALU.add).then_inc(bk.emptied("g_out"), 1)
            bk.await_emptied(dve, "g_out")
            dve_norm(dve, s, link, "4", n["u"], n["n"])
            yield 422
            b = bk.await_filled(dve, "g_ffn")
            dve.tensor_tensor(n["f"][:], b[:].rearrange("p (t d) -> p t d", t=NT),
                              rows["gf"][:, None, :].to_broadcast([P, NT, D]), ALU.add).then_inc(bk.emptied("g_ffn"), 1)
            bk.await_emptied(dve, "g_ffn")
            link(dve.scalar_tensor_tensor(v["y"][:], n["f"][:], 0.0, v["x"][:], ALU.max, ALU.add))
            dve_norm(dve, s, link, "5", v["y"], v["y"])

        def act_gated(act, s):
            v, bk = st[s], st[s]["bk"]
            n = v["g"]
            yield 402
            b = bk.await_filled(act, "g_negT")
            act.copy(n["negT"][:].rearrange("p a b -> p (a b)"), b[:, 0:P].bitcast(BF16)).then_inc(bk.emptied("g_negT"), 1)
            for h in range(H2):
                yield 410 + h
                for i in range(2):
                    b = bk.await_filled(act, f"g_s{h}_{i}")
                    act.activation(n["p"][:, h % 2, 2 * i:2 * i + 2, :], b[:].rearrange("p (k t) -> p k t", t=T), ACT.Exp)\
                        .then_inc(bk.emptied(f"g_s{h}_{i}"), 1)
            yield 419
            b = bk.await_filled(act, "g_oT")
            act.copy(n["oT"][:].rearrange("p c t -> p (c t)"), b[:]).then_inc(bk.emptied("g_oT"), 1)
            yield 421
            b = bk.await_filled(act, "g_nT")
            for c in range(NC):
                last = act.activation(n["nT"][:, c, :], b[:, c * T:(c + 1) * T], ACT.Identity,
                                      bias=bias["beta"][:, c:c + 1], scale=bias["gamma"][:, c:c + 1])
            last.then_inc(bk.emptied("g_nT"), 1)

        def pool_gated(pool, s):
            v, bk = st[s], st[s]["bk"]
            n = v["g"]
            yield 400
            pool.wait_ge(sem(f"x3_{s}"), 1)
            pool.tensor_tensor(out=v["res"][:], in0=v["x"][:], in1=rows["go"][:, None, :].to_broadcast([P, NT, D]),
                               op=ALU.add).then_inc(sem(f"res{s}"), 1)
            for i, (key, rot, _, _, _) in enumerate(ROPES):
                bk.await_emptied(pool, "g_" + rot)
                pool.tensor_tensor(out=n[key][:], in0=n["ra"][:], in1=n["rb"][:], op=ALU.add).then_inc(sem(f"g_rope{s}"), 1)
                pool.wait_ge(sem(f"g_rope{s}"), 2 * i + 1)
                pool.tensor_copy(n[key + "b"][:], n[key][:]).then_inc(sem(f"g_rope{s}"), 1)
            pool.memset(n["v"][:, :, :, HD2], 1.0)
            pool.memset(n["neg"][:], 0.0).then_inc(sem(f"g_ones{s}"), 1)
            yield 420
            pool_norm(pool, s, "4")
            yield 422
            pool_norm(pool, s, "5")

        LAYERS = (("nystrom", 0), ("dilated", 1), ("ffn", 2), ("memory", 3), ("gated", 4))[:stop]
        parts = {"pe": (pe_nystrom, pe_dilated, pe_ffn, pe_memory, pe_gated),
                 "dve": (dve_nystrom, dve_dilated, dve_ffn, dve_memory, dve_gated),
                 "act": (act_nystrom, act_dilated, act_ffn, act_memory, act_gated),
                 "pool": (pool_nystrom, pool_dilated, pool_ffn, pool_memory, pool_gated)}

        def interleaved(programs):
            due = [[0, s, g] for s, g in enumerate(programs)]
            while due:
                due.sort(key=lambda d: (d[0], d[1]))
                try:
                    stage = next(due[0][2])
                    assert stage >= due[0][0]
                    due[0][0] = stage
                except StopIteration:
                    due.pop(0)

        def chain(fns, *args):
            for f in fns[:stop]:
                yield from f(*args)

        final = "x" if stop < 5 else "y"
        key = str(stop - 1) if stop < 5 else "5"
        with nc.Fori(0, BATCH // STREAMS) as turn:
            with nc.Block() as block:
                @block.sync
                def _(sp):
                    for s in range(STREAMS):
                        v = st[s]
                        tok = (turn * STREAMS + s) * T
                        sp.dma_start(v["x"][:], a["x"][bass.ds(tok, T), :].rearrange("(t p) d -> p t d", p=P))\
                            .then_inc(sem(f"inputs{s}"), 16)
                        sp.dma_start(x_of(s), a["xT"][:, bass.ds(tok, T)].rearrange("(c p) t -> p c t", p=P))\
                            .then_inc(sem(f"inputs{s}"), 16)
                        sp.dma_start(v["ctx"][:], a["ctxT"][:, bass.ds(tok, T)].rearrange("(c p) t -> p c t", p=P))\
                            .then_inc(sem(f"inputs{s}"), 16)
                    for s in range(STREAMS):
                        sp.wait_ge(sem(f"x{key}_{s}"), 1)
                        tok = (turn * STREAMS + s) * T
                        sp.dma_start(a["y"][bass.ds(tok, T), :].rearrange("(t p) d -> p t d", p=P), st[s][final][:])\
                            .then_inc(sem(f"stored{s}"), 16)
                    for s in range(STREAMS):
                        sp.wait_ge(sem(f"stored{s}"), 16)

                @block.tensor
                def _(pe):
                    interleaved([chain(parts["pe"], pe, s) for s in range(STREAMS)])

                @block.vector
                def _(dve):
                    links = 0
                    dve_link = sem("dve_link")

                    def link(ins):
                        nonlocal links
                        links += 1
                        ins.then_inc(dve_link, 1)
                        dve.wait_ge(dve_link, links)

                    interleaved([chain(parts["dve"], dve, s, link) for s in range(STREAMS)])

                @block.scalar
                def _(act):
                    interleaved([chain(parts["act"], act, s) for s in range(STREAMS)])

                @block.gpsimd
                def _(pool):
                    interleaved([chain(parts["pool"], pool, s) for s in range(STREAMS)])
            with nc.Block() as block:
                @block.sync
                def _(sp):
                    for x in sems.values():
                        if x.name[:4] != "load" and x.name[:5] != "setup":
                            sp.sem_clear(x)


TOK = BATCH * T
TT = TOK // P
TOPK = 2
SLOTS = 256
SHIFT = 8
TILES = (TOK * TOPK + E * (SLOTS - 1)) // SLOTS
TILES += TILES % 2
ST = SLOTS // P


def experts_kernel(nc, a):
    ctx = ExitStack()
    with ctx:
        def sb(name, shape, dt=F32):
            return ctx.enter_context(nc.sbuf_tensor(name, shape, dt))

        def sem(name):
            return ctx.enter_context(nc.semaphore(name))

        I32 = mybir.dt.int32
        U32 = mybir.dt.uint32
        x = sb("m_x", [P, TT, D])
        xs = sb("m_xs", [P, TOPK, TT, D])
        xT = sb("m_xT", [P, NC, TOK])
        wg = sb("m_wg", [P, NC, E])
        bg = sb("m_bg", [P, E])
        ident = sb("m_ident", [P, P])
        tri = sb("m_tri", [P, P], BF16)
        ones = sb("m_ones", [P, P], BF16)
        eids = sb("m_eids", [P, E])
        jids = sb("m_jids", [P, TILES])
        lg = sb("m_lg", [P, TT, E])
        top = sb("m_top", [P, TT, E])
        topi = sb("m_topi", [P, TT, E], U32)
        topf = sb("m_topf", [P, TT, TOPK])
        wts = sb("m_wts", [P, TOPK, TT])
        tmp = sb("m_tmp", [P, 4, TT])
        hit = sb("m_hit", [P, TOPK, TT, E])
        sel = sb("m_sel", [P, TT, E])
        selb = sb("m_selb", [P, TT, E], BF16)
        cum = sb("m_cum", [P, 2, TT, E])
        pre = sb("m_pre", [P, TT, E])
        cnt = sb("m_cnt", [P, 8, E])
        cnti = sb("m_cnti", [P, 2, E], I32)
        posf = sb("m_posf", [P, TOPK, TT])
        posi = sb("m_posi", [P, TOPK, TT], U32)
        tile_e = sb("m_tile_e", [P, TILES, E])
        tef = sb("m_tef", [P, TILES])
        tei = sb("m_tei", [P, TILES], I32)

        bank = [ctx.enter_context(nc.psum_tensor(f"m_bank{i}", [P, 512], F32)) for i in range(8)]
        loaded, routed, step, soft = sem("m_loaded"), sem("m_routed"), sem("m_step"), sem("m_soft")
        pe_done, act_done = sem("m_pe"), sem("m_act")
        scaled, positions, sent = sem("m_scaled"), sem("m_positions"), sem("m_sent")

        loads = [(x[:], a["x5"].rearrange("(t p) d -> p t d", p=P)),
                 (wg[:], a["Wg"].rearrange("(c p) e -> p c e", p=P)), (bg[:], a["R_bg"]),
                 (ident[:], a["C_ident"]), (tri[:], a["C_tri"]), (ones[:], a["C_onesb"]),
                 (eids[:], a["C_eids"]), (jids[:], a["C_jids"])]

        with nc.Block() as block:
            @block.sync
            def _(sp):
                for dst, src in loads:
                    sp.dma_start(dst, src).then_inc(loaded, 16)

            @block.tensor
            def _(pe):
                pe.wait_ge(loaded, 16 * len(loads))
                for t in range(TT):
                    if t >= 4:
                        pe.wait_ge(act_done, t - 3)
                    for c in range(NC):
                        last = pe.transpose(bank[t % 4][:, c * P:(c + 1) * P], x[:, t, c * P:(c + 1) * P], ident[:])
                    last.then_inc(pe_done, 1)
                pe.wait_ge(act_done, TT)
                for t in range(TT):
                    for c in range(NC):
                        last = pe.matmul(bank[4][:, t * E:(t + 1) * E], xT[:, c, t * P:(t + 1) * P], wg[:, c, :],
                                         start=c == 0, stop=c == NC - 1)
                last.then_inc(pe_done, 1)
                pe.wait_ge(routed, 1)
                pe.matmul(bank[5][:, 0:TT * E], tri[:], selb[:].rearrange("p t e -> p (t e)"), start=True, stop=True)
                pe.matmul(bank[6][:, 0:TT * E], ones[:], selb[:].rearrange("p t e -> p (t e)"), start=True, stop=True)\
                    .then_inc(pe_done, 1)

            @block.scalar
            def _(act):
                for t in range(TT):
                    act.wait_ge(pe_done, t + 1)
                    act.copy(xT[:, :, t * P:(t + 1) * P], bank[t % 4][:, 0:D].rearrange("p (c t) -> p c t", c=NC))\
                        .then_inc(act_done, 1)
                act.wait_ge(soft, 1)
                act.activation(tmp[:, 1, :], tmp[:, 0, :], ACT.Exp).then_inc(soft, 1)

            @block.vector
            def _(dve):
                n = 0

                def link(ins):
                    nonlocal n
                    n += 1
                    ins.then_inc(step, 1)
                    dve.wait_ge(step, n)

                dve.wait_ge(pe_done, TT + 1)
                link(dve.tensor_tensor(lg[:], bank[4][:, 0:TT * E].rearrange("p (t e) -> p t e", e=E),
                                       bg[:, None, :].to_broadcast([P, TT, E]), ALU.add))
                for t in range(TT):
                    last = dve.max(top[:, t, :], lg[:, t, :])
                link(last)
                for t in range(TT):
                    last = dve.max_index(topi[:, t, :], top[:, t, :], lg[:, t, :])
                link(last)
                dve.tensor_tensor(tmp[:, 0, :], top[:, :, 1], top[:, :, 0], ALU.subtract).then_inc(soft, 1)
                link(dve.tensor_copy(topf[:], topi[:, :, 0:TOPK]))
                for k in range(TOPK):
                    last = dve.tensor_tensor(hit[:, k], topf[:, :, k, None].to_broadcast([P, TT, E]),
                                             eids[:, None, :].to_broadcast([P, TT, E]), ALU.is_equal)
                link(last)
                link(dve.tensor_tensor(sel[:], hit[:, 0], hit[:, 1], ALU.add))
                dve.tensor_copy(selb[:], sel[:]).then_inc(routed, 1)
                dve.wait_ge(soft, 2)
                link(dve.tensor_scalar(tmp[:, 2, :], tmp[:, 1, :], 1.0, None, ALU.add))
                link(dve.reciprocal(wts[:, 0, :], tmp[:, 2, :]))
                link(dve.tensor_tensor(wts[:, 1, :], tmp[:, 1, :], wts[:, 0, :], ALU.mult))
                for k in range(TOPK):
                    for t in range(TT):
                        last = dve.tensor_scalar(xs[:, k, t, :], x[:, t, :], wts[:, k, t:t + 1], None, ALU.mult)
                last.then_inc(scaled, 1)
                dve.wait_ge(pe_done, TT + 2)
                link(dve.tensor_copy(cum[:, 0], bank[6][:, 0:TT * E].rearrange("p (t e) -> p t e", e=E)))
                at, d = 0, 1
                while d < TT:
                    dve.tensor_copy(cum[:, 1 - at, 0:d], cum[:, at, 0:d])
                    link(dve.tensor_tensor(cum[:, 1 - at, d:TT], cum[:, at, d:TT], cum[:, at, 0:TT - d], ALU.add))
                    at, d = 1 - at, 2 * d
                total = cum[:, at, TT - 1, :]
                link(dve.tensor_tensor(pre[:], cum[:, at], bank[6][:, 0:TT * E].rearrange("p (t e) -> p t e", e=E),
                                       ALU.subtract))
                link(dve.tensor_tensor(pre[:], pre[:], bank[5][:, 0:TT * E].rearrange("p (t e) -> p t e", e=E), ALU.add))
                link(dve.tensor_scalar(cnt[:, 0, :], total, float(SLOTS - 1), None, ALU.add))
                link(dve.tensor_copy(cnti[:, 0, :], cnt[:, 0, :]))
                link(dve.tensor_scalar(cnti[:, 1, :], cnti[:, 0, :], SHIFT, None, ALU.arith_shift_right))
                link(dve.tensor_copy(cnt[:, 1, :], cnti[:, 1, :]))
                k, d = 2, 1
                link(dve.tensor_copy(cnt[:, 2, :], cnt[:, 1, :]))
                while d < E:
                    dve.tensor_copy(cnt[:, k + 1, 0:d], cnt[:, k, 0:d])
                    link(dve.tensor_tensor(cnt[:, k + 1, d:E], cnt[:, k, d:E], cnt[:, k, 0:E - d], ALU.add))
                    k, d = k + 1, 2 * d
                link(dve.tensor_tensor(cnt[:, 6, :], cnt[:, k, :], cnt[:, 1, :], ALU.subtract))
                link(dve.tensor_scalar(cnt[:, 7, :], cnt[:, 6, :], float(SLOTS), None, ALU.mult))
                link(dve.tensor_tensor(pre[:], pre[:], cnt[:, 7, None, :].to_broadcast([P, TT, E]), ALU.add))
                for j in range(TOPK):
                    last = dve.tensor_tensor(hit[:, j], hit[:, j], pre[:], ALU.mult)
                link(last)
                link(dve.tensor_reduce(posf[:].rearrange("p k t -> p (k t)"), hit[:].rearrange("p k t e -> p (k t) e"),
                                       axis=AX.X, op=ALU.add))
                link(dve.tensor_tensor(tile_e[:], jids[:, :, None].to_broadcast([P, TILES, E]),
                                       cnt[:, k, None, :].to_broadcast([P, TILES, E]), ALU.is_ge))
                link(dve.tensor_reduce(tef[:], tile_e[:], axis=AX.X, op=ALU.add))
                link(dve.tensor_scalar(tef[:], tef[:], float(E - 1), None, ALU.min))
                dve.tensor_copy(tei[:], tef[:])
                dve.tensor_copy(posi[:], posf[:]).then_inc(positions, 1)

            @block.gpsimd
            def _(pool):
                pool.wait_ge(scaled, 1)
                pool.wait_ge(positions, 1)
                for k in range(TOPK):
                    for t in range(TT):
                        pool.indirect_dma_start(out=a["slots"], out_offset=bass.IndirectOffsetOnAxis(posi[:, k, t:t + 1], 0),
                                                in_=xs[:, k, t, :], in_offset=None).then_inc(sent, 16)
                pool.wait_ge(sent, 16 * TOPK * TT)

        w1 = [sb(f"e_w1_{i}", [P, NC, HF]) for i in range(2)]
        w3 = [sb(f"e_w3_{i}", [P, NC, HF]) for i in range(2)]
        w2 = xT[:, 0, :].rearrange("p (b f d) -> p b f d", b=1, d=D), xT[:, 1, :].rearrange("p (b f d) -> p b f d", b=1, d=D)
        w2 = [w[:, 0] for w in w2]
        xe = [sb(f"e_x{i}", [P, ST, D]) for i in range(2)]
        xeT = [sb(f"e_xT{i}", [P, NC, SLOTS]) for i in range(2)]
        h = [sb(f"e_h{i}", [P, HF // P, SLOTS]) for i in range(2)]
        silu = [sb(f"e_silu{i}", [P, SLOTS]) for i in range(4)]
        yo = [sb(f"e_y{i}", [P, ST, D]) for i in range(2)]
        wl = [sem(f"e_weights{i}") for i in range(2)]
        xl = [sem(f"e_rows{i}") for i in range(2)]
        tf = [sem(f"e_turned{i}") for i in range(2)]
        te = [sem(f"e_turned_sbuf{i}") for i in range(2)]
        hf = [sem(f"e_hidden{i}") for i in range(4)]
        sd = [sem(f"e_silu{i}") for i in range(4)]
        hr = [sem(f"e_gated{i}") for i in range(4)]
        yf = [sem(f"e_answer{i}") for i in range(2)]
        ye = [sem(f"e_answer_sbuf{i}") for i in range(2)]
        ys = [sem(f"e_stored{i}") for i in range(2)]
        FE = HF // P

        with nc.Block() as block:
            @block.gpsimd
            def _(pool):
                for i in range(2):
                    pool.memset(yo[i][:], 0.0).then_inc(yf[i], 1)
                    pool.memset(xeT[i][:], 0.0).then_inc(te[i], 1)
                    pool.memset(h[i][:, 0, 0:2], 0.0).then_inc(ye[i], 1)
                    pool.memset(h[i][:, 1, 0:2], 0.0).then_inc(ys[i], 16)
                for i in range(4):
                    pool.memset(silu[i][:], 0.0).then_inc(hr[i], 1)

        with nc.Block() as block:
            @block.sync
            def _(sp):
                with sp.Fori(0, TILES // 2) as i:
                    for u in range(2):
                        j = i * 2 + u
                        expert = sp.value_load(tei[0:1, bass.ds(j, 1)], min_val=0, max_val=E - 1)
                        sp.wait_ge(te[u], i + 1)
                        sp.dma_start(xe[u][:], a["slots"][bass.ds(j * SLOTS, SLOTS), :].rearrange("(t p) d -> p t d", p=P))\
                            .then_inc(xl[u], 16)
                        sp.wait_ge(yf[u], i + 1)
                        for dst, src in ((w1[u], a["E1"]), (w3[u], a["E3"]), (w2[u], a["E2"])):
                            sp.dma_start(dst[:], src[bass.ds(expert, 1)].rearrange("o (c p) n -> p (o c) n", p=P))\
                                .then_inc(wl[u], 16)

            @block.tensor
            def _(pe):
                with pe.Fori(0, TILES // 2) as i:
                    for u in range(2):
                        pe.wait_ge(xl[u], i * 16 + 16)
                        pe.wait_ge(te[u], i + 1)
                        for c in range(NC):
                            for t in range(ST):
                                last = pe.transpose(bank[4 + u][:, c * SLOTS + t * P:c * SLOTS + (t + 1) * P],
                                                    xe[u][:, t, c * P:(c + 1) * P], ident[:])
                        last.then_inc(tf[u], 1)
                    for u in range(2):
                        pe.wait_ge(te[u], i + 2)
                        pe.wait_ge(wl[u], i * 48 + 48)
                        for f in range(FE):
                            b = f % 4
                            pe.wait_ge(hr[b], i * 4 + 2 * u + f // 4 + 1)
                            for col, w in ((0, w1[u]), (SLOTS, w3[u])):
                                for c in range(NC):
                                    last = pe.matmul(bank[b][:, col:col + SLOTS], w[:, c, f * P:(f + 1) * P], xeT[u][:, c, :],
                                                     start=c == 0, stop=c == NC - 1)
                            last.then_inc(hf[b], 1)
                    for u in range(2):
                        pe.wait_ge(ye[u], i + 1)
                        for b in range(4):
                            pe.wait_ge(hr[b], i * 4 + 2 * u + 3)
                        for t in range(ST):
                            for f in range(FE):
                                last = pe.matmul(bank[6 + u][:, t * D:(t + 1) * D], h[u][:, f, t * P:(t + 1) * P],
                                                 w2[u][:, f, :], start=f == 0, stop=f == FE - 1)
                        last.then_inc(yf[u], 1)

            @block.scalar
            def _(act):
                with act.Fori(0, TILES // 2) as i:
                    for u in range(2):
                        act.wait_ge(tf[u], i + 1)
                        act.copy(xeT[u][:].rearrange("p c s -> p (c s)"), bank[4 + u][:]).then_inc(te[u], 1)
                    for u in range(2):
                        for f in range(FE):
                            b = f % 4
                            act.wait_ge(hf[b], i * 4 + 2 * u + f // 4 + 1)
                            act.activation(silu[b][:], bank[b][:, 0:SLOTS], ACT.Silu).then_inc(sd[b], 1)
                    for u in range(2):
                        act.wait_ge(yf[u], i + 2)
                        act.wait_ge(ys[u], i * 16 + 16)
                        act.copy(yo[u][:].rearrange("p t d -> p (t d)"), bank[6 + u][:]).then_inc(ye[u], 1)
                        act.wait_ge(ye[u], i + 2)
                        act.dma_start(a["back"][bass.ds((i * 2 + u) * SLOTS, SLOTS), :].rearrange("(t p) d -> p t d", p=P),
                                      yo[u][:]).then_inc(ys[u], 16)
                for u in range(2):
                    act.wait_ge(ys[u], 16 * (TILES // 2) + 16)

            @block.vector
            def _(dve):
                with dve.Fori(0, TILES // 2) as i:
                    for u in range(2):
                        for f in range(FE):
                            b = f % 4
                            dve.wait_ge(sd[b], i * 4 + 2 * u + f // 4 + 1)
                            dve.tensor_tensor(h[u][:, f, :], bank[b][:, SLOTS:2 * SLOTS], silu[b][:], ALU.mult)\
                                .then_inc(hr[b], 1)

        fetched, summed, normed = sem("m_fetched"), sem("m_summed"), sem("m_normed")
        halved = sem("m_half")
        vend, ready, out_done = sem("m_variance"), sem("m_rstd"), sem("m_out")
        stt, mv, ve, rstd, half = (sb("m_st", [P, TT, 6]), sb("m_mv", [P, TT, 2]), sb("m_ve", [P, TT]),
                                   sb("m_rstd", [P, TT]), sb("m_halves", [P, TT]))
        with nc.Block() as block:
            @block.gpsimd
            def _(pool):
                pool.memset(half[:], -0.5).then_inc(halved, 1)
                for t in range(TT):
                    for k in range(TOPK):
                        pool.indirect_dma_start(out=xs[:, k, t, :], out_offset=None, in_=a["back"],
                                                in_offset=bass.IndirectOffsetOnAxis(posi[:, k, t:t + 1], 0))\
                            .then_inc(fetched, 16)
                pool.wait_ge(halved, 1)
                pool.wait_ge(vend, 1)
                pool.tensor_tensor(out=rstd[:], in0=ve[:], in1=half[:], op=ALU.pow).then_inc(ready, 1)

            @block.vector
            def _(dve):
                dve.wait_ge(fetched, 16 * TOPK * TT)
                dve.tensor_tensor(xs[:, 0], xs[:, 0], xs[:, 1], ALU.add).then_inc(summed, 1)
                dve.wait_ge(summed, 1)
                for t in range(TT):
                    last = dve.scalar_tensor_tensor(xs[:, 0, t, :], x[:, t, :], 2.0, xs[:, 0, t, :], ALU.mult, ALU.add)
                last.then_inc(summed, 1)
                dve.wait_ge(summed, 2)
                for t in range(TT):
                    last = dve.bn_stats(stt[:, t, :], xs[:, 0, t, :])
                last.then_inc(summed, 1)
                dve.wait_ge(summed, 3)
                for t in range(TT):
                    last = dve.bn_aggr(mv[:, t, :], stt[:, t, :])
                last.then_inc(summed, 1)
                dve.wait_ge(summed, 4)
                dve.tensor_scalar(ve[:], mv[:, :, 1], EPS, None, ALU.add).then_inc(vend, 1)
                dve.wait_ge(ready, 1)
                for t in range(TT):
                    dve.tensor_scalar(xs[:, 0, t, :], xs[:, 0, t, :], mv[:, t, 0:1], rstd[:, t:t + 1],
                                      ALU.subtract, ALU.mult).then_inc(normed, 1)

            @block.sync
            def _(sp):
                q = TT // 4
                for i in range(4):
                    sp.wait_ge(normed, (i + 1) * q)
                    sp.dma_start(a["y"][i * q * P:(i + 1) * q * P, :].rearrange("(t p) d -> p t d", p=P),
                                 xs[:, 0, i * q:(i + 1) * q, :]).then_inc(out_done, 16)
                sp.wait_ge(out_done, 64)


def clear_slots(nc, a):
    with (nc.sbuf_tensor("zeros", [P, D], F32) as zeros, nc.semaphore("zeros_made") as made,
          nc.semaphore("slots_cleared") as cleared, nc.Block() as block):
        @block.gpsimd
        def _(pool):
            pool.memset(zeros[:], 0.0).then_inc(made, 1)

        @block.sync
        def _(sp):
            sp.wait_ge(made, 1)
            n = TILES * SLOTS // P
            sp.dma_start(a["slots"].rearrange("(n p) d -> p n d", p=P), zeros[:, None, :].to_broadcast([P, n, D]))\
                .then_inc(cleared, 16)
            sp.wait_ge(cleared, 16)


def lay_out(i):
    f = lambda n: np.asarray(i[n])
    e = 3
    swap = np.arange(D) ^ 1
    cols = lambda b: np.ascontiguousarray(b.reshape(-1, P).T)
    rep = lambda b: np.ascontiguousarray(np.broadcast_to(b.reshape(1, -1), (P, b.size)))
    a = {}
    x, c = f("x").reshape(-1, D), f("ctx_1024").reshape(-1, D)
    a["x"], a["xT"], a["ctxT"] = x, x.T, c.T
    g = lambda n: f("L1_xattn_" + n)[e]
    a["W_qkv"], a["W_out"] = f("L0_attn_Wqkv"), f("L0_attn_Wout")
    for n in "qkvo":
        a["W_d" + n] = f("L0_xattn_W" + n).T
    a["W_ff1"], a["W_ff2"] = f("L0_ffn_W1").T, f("L0_ffn_W2").T
    a["W_mw"], a["W_mr"] = f("L1_attn_W_write").T, f("L1_attn_W_read").T
    for n in ("qa", "ka", "qt", "kt"):
        a["W_" + n], a["W_" + n + "r"] = g("W_" + n).T, g("W_" + n)[swap].T
        a["B_" + n], a["B_" + n + "r"] = cols(g("b_" + n)), cols(g("b_" + n)[swap])
    a["W_va"], a["W_vt"], a["W_go"], a["W_gf"] = g("W_va").T, g("W_vt").T, g("W_o").T, g("W_ffn").T
    bq = f("L0_attn_bqkv")
    a["B_q0"], a["B_k0"], a["R_v0"] = cols(bq[:D]), cols(bq[D:2 * D]), rep(bq[2 * D:])
    a["R_o0"] = rep(f("L0_attn_bout"))
    a["B_dq"], a["B_dk"], a["R_dv"], a["R_do"] = (cols(f("L0_xattn_bq")), cols(f("L0_xattn_bk")),
                                                  rep(f("L0_xattn_bv")), rep(f("L0_xattn_bo")))
    a["B_ff1"], a["R_ff2"] = cols(f("L0_ffn_b1")), rep(f("L0_ffn_b2"))
    a["B_decay"], a["B_alpha"] = rep(f("L1_attn_decay")), rep(f("L1_attn_log_alpha"))
    a["R_va"], a["R_vt"], a["R_go"], a["R_gf"] = rep(g("b_va")), rep(g("b_vt")), rep(g("b_o")), rep(g("b_ffn"))
    a["B_gamma"], a["B_beta"] = cols(g("gamma")), cols(g("beta"))
    a["B_gate"] = rep(f("L1_xattn_gating_factor")[e:e + 1])
    a["Wg"], a["R_bg"] = f("L1_ffn_Wg"), rep(f("L1_ffn_bg"))
    a["E1"], a["E2"], a["E3"] = f("L1_ffn_W1"), f("L1_ffn_W2"), f("L1_ffn_W3")
    for n, t in shape_constants().items():
        a["C_" + n] = t
    return {n: np.ascontiguousarray(t) for n, t in a.items()}


def build(nc, a, y):
    tokens = nc.dram_tensor("tokens", (TOK, D), F32, kind="Internal").ap()
    slots = nc.dram_tensor("slots", (TILES * SLOTS, D), F32, kind="Internal").ap()
    back = nc.dram_tensor("back", (TILES * SLOTS, D), F32, kind="Internal").ap()
    clear_slots(nc, {"slots": slots})
    layers_kernel(nc, {**a, "y": tokens}, 5)
    experts_kernel(nc, {**a, "x5": tokens, "slots": slots, "back": back, "y": y})


def kernel(**inputs):
    import concourse.bacc as _bacc
    from concourse.bass_utils import run_bass_kernel_spmd as _run

    nc = _bacc.Bacc("TRN2", target_bir_lowering=False, num_devices=1)
    arrays = lay_out(inputs)
    args = {n: nc.dram_tensor(n, t.shape, mybir.dt.from_np(t.dtype), kind="ExternalInput").ap()
            for n, t in arrays.items()}
    y = nc.dram_tensor("y_out", (TOK, D), F32, kind="ExternalOutput").ap()
    build(nc, args, y)
    r = _run(nc, [arrays], core_ids=[0])
    return r.results[0]["y_out"].reshape(BATCH, T, D)
```

```python
import numpy as np
import concourse.bass as bass
from concourse import mybir
from concourse.alu_op_type import AluOpType as ALU
from contextlib import ExitStack

F32 = mybir.dt.float32
BF16 = mybir.dt.bfloat16
ACT = mybir.ActivationFunctionType
AX = mybir.AxisListType

P = 128
BATCH = 8
T = 256
D = 256
NT = T // P
NC = D // P
STREAMS = 2
EPS = 1e-5

H0 = 16
DH0 = D // H0
HC = P // DH0
M = 64
LM = T // M
PAIRS = H0 // 2
PINV_ITERS = 6
BR = 3
VW = DH0 + 1
NEG = -100000000.0
BIG = -1e30
TINY = 2.0 ** -63
FF = 4 * D
FC = FF // P
H1 = 4
HD1 = D // H1
H2 = 8
HD2 = D // H2
VW2 = HD2 + 1
KT2 = 2 * T // P
E = 8
HF = 1024


class BankTurns:

    def __init__(self, tensors, filled, emptied, order):
        self.turn = {}
        count = [0] * len(tensors)
        for name, b in order:
            count[b] += 1
            assert name not in self.turn, name
            self.turn[name] = (tensors[b], filled[b], emptied[b], count[b])

    def claim(self, pe, name):
        tensor, _, emptied, k = self.turn[name]
        if k > 1:
            pe.wait_ge(emptied, k - 1)
        return tensor

    def await_filled(self, eng, name):
        tensor, filled, _, k = self.turn[name]
        eng.wait_ge(filled, k)
        return tensor

    await_done = await_filled

    def await_emptied(self, eng, name):
        _, _, emptied, k = self.turn[name]
        eng.wait_ge(emptied, k)

    def filled(self, name):
        return self.turn[name][1]

    def emptied(self, name):
        return self.turn[name][2]


def bank_order():
    o = [("n_q", 0), ("n_k", 1), ("n_v", 2)]
    o += [("n_sim2", 3)]
    o += [(f"n_max1_{t}{c}", (0, 1, 2, 3)[2 * t + c]) for t in range(NT) for c in range(NC)]
    o += [(f"n_max3_{i}", i) for i in range(4)]
    o += [("n_negT", 0)]
    o += [(f"n_s1_{i}", (1, 2, 3, 0)[i]) for i in range(4)]
    o += [(f"n_s3_{t}{c}", (1, 2, 3, 0)[2 * t + c]) for t in range(NT) for c in range(NC)]
    o += [("n_aT_0", 1), ("n_aT_1", 2), ("n_y", 3)]
    for g in range(2):
        o += [(f"n_k0_{g}", g), (f"n_kT0_{g}", 2 + g)]
    for i in range(PINV_ITERS - 1):
        for g in range(2):
            o += [(f"n_p{i}_{g}", g)]
        for g in range(2):
            o += [(f"n_t{i}_{g}", 2 + g)]
        for g in range(2):
            o += [(f"n_kT{i + 1}_{g}", 2 + g), (f"n_k{i + 1}_{g}", g)]
    for j in range(4):
        o += [(f"n_w{j}", 2 + j % 2)]
    o += [(f"n_o{t}", t) for t in range(NT)]
    o += [("n_oT", 2), ("n_out", 3), ("n_xT", 0)]
    o += [("d_q", 1), ("d_k", 2), ("d_v", 3)]
    for c in range(NC):
        o += [(f"d_m{c}_{i}", i % 3 + 1) for i in range(6)]
        o += [(f"d_negT{c}", 0)]
        o += [(f"d_s{c}_{i}", i % 3 + 1) for i in range(6)]
        o += [(f"d_o{c}_{t}", (0, 1)[t]) for t in range(NT)]
    o += [("d_oT", 2), ("d_out", 3), ("d_xT", 0)]
    o += [(f"f_h{i}", (1, 2, 3, 0)[i]) for i in range(FC // 2)]
    o += [("f_out", 1), ("f_xT", 2)]
    o += [("r_v", 3), ("r_s0", 0), ("r_s1", 1), ("r_s2", 2), ("r_s3", 3), ("r_r", 2),
          ("r_out", 0), ("r_xT", 1)]
    o += [("g_ka", 2), ("g_kt", 3), ("g_qa", 0), ("g_qt", 1)]
    o += [("g_va", 2), ("g_vt", 3)]
    o += [(f"g_m{h}_{t}", 2 * (h % 2) + t) for h in range(H2) for t in range(NT)]
    o += [("g_negT", 0)]
    o += [(f"g_o{t}", t) for t in range(NT)]
    o += [(f"g_s{h}_{i}", 2 + i) for h in range(H2) for i in range(2)]
    o += [("g_oT", 2), ("g_out", 3), ("g_nT", 0), ("g_ffn", 1), ("g_xT", 2)]
    return o


def words(kind, shape):
    n = int(np.prod(shape))
    n = n if kind == F32 else (n + 1) // 2
    return n + n % 2


def words_before(table, name):
    names = list(table)
    return words_of({n: table[n] for n in names[:names.index(name)]})


def words_of(table):
    return sum(words(kind, shape) for kind, *shape in table.values())


def carve(arena, sizes):
    at, out = 0, {}
    for name, (kind, *shape) in sizes.items():
        n = int(np.prod(shape))
        w = words(kind, shape)
        v = arena[:, at:at + w]
        if kind == BF16:
            v = v.bitcast(BF16)
        v = v[:, 0:n]
        if len(shape) == 2:
            v = v.rearrange("p (a b) -> p a b", a=shape[0])
        if len(shape) == 3:
            v = v.rearrange("p (a b c) -> p a b c", a=shape[0], b=shape[1])
        if len(shape) == 4:
            v = v.rearrange("p (a b c d) -> p a b c d", a=shape[0], b=shape[1], c=shape[2])
        out[name] = v
        at += w
    return out, at


NYSTROM = {
    "q": (F32, NC, T), "k": (F32, NC, T), "qb": (BF16, NC, T), "kb": (BF16, NC, T),
    "v": (F32, NT, H0, VW), "qs": (F32, NC, M), "ks": (F32, NC, M), "kl": (F32, NC, M),
    "qlm": (F32, NC, HC, M), "klm": (F32, NC, HC, M), "qlmb": (BF16, NC, HC, M), "klmb": (BF16, NC, HC, M),
    "mx1": (F32, NT, H0), "mx3": (F32, PAIRS), "mx2": (F32, PAIRS), "sum2": (F32, PAIRS), "rs2": (F32, PAIRS),
    "neg": (BF16, 3, P), "negT": (BF16, 3, P),
    "a": (F32, PAIRS, M), "ry": (F32, PAIRS), "z2": (F32, PAIRS, DH0), "g": (F32, PAIRS, 2 * VW),
    "ro": (F32, NT, H0),
    "e1": (F32, PAIRS, T), "e3": (F32, NT, NC, HC * M),
}
DIAGONAL = (F32, PAIRS, P)
PINV = {
    "q": {"aT": DIAGONAL}, "qb": {"t1": (F32, PAIRS, M)}, "v": {"kz": (F32, PAIRS, M + DH0)},
    "qlm": {"t3": DIAGONAL}, "klm": {"kk": DIAGONAL}, "qlmb": {"ad": DIAGONAL},
    "e3": {"kkT": DIAGONAL, "t2": DIAGONAL},
}
DILATED = {
    "q": (F32, NC, T), "k": (F32, NC, T), "kb": (BF16, NC, T), "v": (F32, NT, H0, BR, VW),
    "qm": (F32, HC, T), "qmb": (BF16, HC, T), "p0": (F32, HC, T), "p1": (F32, HC, P),
    "mx": (F32, NT, H0), "neg": (BF16, NT, P), "negT": (BF16, NT, P),
    "s": (F32, NT, H0, BR), "ls": (F32, NT, H0, BR), "isz": (F32, NT, H0, BR), "w": (F32, NT, H0, BR),
    "rc": (F32, NT, H0, BR), "lm": (F32, NT, H0), "rz": (F32, NT, H0),
    "n": (F32, NT, H0, BR, VW),
}
FFN = {"h": (F32, FC, T)}
MEMORY = {"v": (F32, NT, D), "s0": (F32, H1, T), "s1": (F32, H1, P), "r": (F32, NC, T)}
GATED = {
    "hl": (BF16, 2, 4, NC * T), "rot": (F32, 2, NC, T),
    "stack": (BF16, 4, H2, T),
    "p": (BF16, 4, KT2, T), "e": (F32, 2, 2, T), "v": (BF16, 2, KT2, H2, VW2),
    "mx": (F32, NT, H2), "neg": (BF16, NT, H2), "negT": (BF16, NT, P), "ro": (F32, NT, H2),
}
GATED_UNDER = {
    "p": {"feat": (F32, 2, NC, T), "sum": (F32, 2, NC, T)}, "e": {"v32": (F32, KT2, D)},
    "hl": {"o": (F32, NT, D), "oT": (F32, NC, T), "u": (F32, NT, D), "n": (F32, NT, D)},
    "rot": {"nT": (F32, NC, T), "f": (F32, NT, D)},
}
STACK = 3 * HD2 + 1

MATRICES = {"qkv": 3 * D, "out": D, "dq": D, "dk": D, "dv": D, "do": D, "ff1": FF, "mw": D, "mr": D,
            "qa": D, "ka": D, "va": D, "qt": D, "kt": D, "vt": D,
            "go": D, "gf": D}
COLUMNS = {"q0": NC, "k0": NC, "dq": NC, "dk": NC, "ff1": FC, "decay": H1, "alpha": H1,
           "qa": NC, "ka": NC, "qt": NC, "kt": NC,
           "gamma": NC, "beta": NC, "gate": 1}
ROWS = ("v0", "o0", "dv", "do", "ff2", "va", "vt", "go", "gf")


def shape_constants():

    bf = np.dtype("bfloat16")
    p = np.arange(P)
    c = {"ident": np.eye(P, dtype=np.float32), "identb": np.eye(P).astype(bf)}
    mask = (p[:, None] // DH0 == np.arange(HC)[None]).astype(np.float32)
    c["hmask"] = np.concatenate([mask, mask / LM], 1)
    c["halves"] = (p[:, None] // M == np.arange(2)[None]).astype(np.float32)
    c["ones"] = np.ones((P, P), np.float32)
    c["eye"] = np.tile(np.eye(M, dtype=np.float32), (2, 1))
    c["eye325"] = 3.25 * np.eye(P, dtype=np.float32)
    selp = np.zeros((P, PAIRS, P), np.float32)
    sel16 = np.zeros((P, H0, P), np.float32)
    for h in range(H0):
        selp[h, h // 2, (h % 2) * M:(h % 2 + 1) * M] = 1
        sel16[h, h, :] = 1
    c["selp"], c["sel16"] = (x.reshape(P, -1).astype(bf) for x in (selp, sel16))
    c["above"] = np.where(p[:, None] < p[None], BIG, 0.0).astype(bf)
    c["below"] = np.where(p[:, None] > p[None], BIG, 0.0).astype(bf)
    heads = np.arange(H0)
    on = np.stack([np.ones((P, H0)), p[:, None] % 2 == heads // 8, p[:, None] % 4 == heads // 4], 2)
    c["valid"] = on.reshape(P, -1).astype(np.float32)
    freq = (1.0 / 10000.0 ** (np.arange(0, HD2, 2, dtype=np.float32) / np.float32(HD2))).astype(np.float32)
    ang = np.arange(T, dtype=np.float32)[None] * freq[(p % HD2) % (HD2 // 2)][:, None]
    sign = np.where(p % 2 == 0, -1.0, 1.0).astype(np.float32)[:, None]
    c["tri"] = (p[:, None] < p[None]).astype(bf)
    c["onesb"] = np.ones((P, P)).astype(bf)
    c["eids"] = np.tile(np.arange(E, dtype=np.float32), (P, 1))
    c["jids"] = np.tile(np.arange(TILES, dtype=np.float32), (P, 1))
    c["cosk"], c["sink"] = np.cos(ang).astype(np.float32), (np.sin(ang) * sign).astype(np.float32)
    r = np.float32(1.0 / np.sqrt(HD2))
    c["cosq"], c["sinq"] = c["cosk"] * r, c["sink"] * r
    t = np.arange(T)
    c["exponents"] = np.maximum(t[None] - 1 - p[:, None], 0).astype(np.float32)
    c["keep"] = (t[None] > p[:, None]).astype(np.float32)
    return c


def layers_kernel(nc, a, stop):
    ctx = ExitStack()
    with ctx:
        def sb(name, shape, dt=F32):
            return ctx.enter_context(nc.sbuf_tensor(name, shape, dt))

        sems = {}

        def sem(name):
            if name not in sems:
                sems[name] = ctx.enter_context(nc.semaphore(name))
            return sems[name]

        W = {n: sb("w_" + n, [P, NC, cols]) for n, cols in MATRICES.items()}
        w2 = sb("w_ff2", [P, FC, D])
        bias = {n: sb("b_" + n, [P, cols]) for n, cols in COLUMNS.items()}
        rows = {n: sb("r_" + n, [P, D]) for n in ROWS}
        ident = sb("ident", [P, P])
        identb = sb("identb", [P, P], BF16)
        width = max(words_of(table) for table in (NYSTROM, DILATED, FFN, MEMORY, GATED))
        arenas = [sb(f"arena{s}", [P, width]) for s in range(STREAMS)]
        scratch, exponents, keep = arenas[0][:, 0:1024], arenas[0][:, 1024:1024 + T], arenas[0][:, 1280:1280 + T]
        consts = {n: sb("c_" + n, [P, c.shape[1]], BF16 if c.dtype != np.float32 else F32)
                  for n, c in shape_constants().items() if n not in ("ident", "identb", "exponents", "keep", "tri", "onesb", "eids", "jids")}
        hmask = consts["hmask"]
        selp = consts["selp"][:].rearrange("p (a b) -> p a b", b=P)
        sel16 = consts["sel16"][:].rearrange("p (a b) -> p a b", b=P)
        cosg = sb("cosg", [P, T])
        sing = sb("sing", [P, T])
        dec0 = sb("dec0", [P, H1, T])
        dec1 = sb("dec1", [P, H1, P])
        small = sb("small", [P, 64])

        st = []
        psum = [ctx.enter_context(nc.psum_tensor(f"bank{i}", [P, 512], F32)) for i in range(8)]
        for s in range(STREAMS):
            arena = arenas[s]
            v = {"x": sb(f"x{s}", [P, NT, D]), "y": sb(f"y{s}", [P, NT, D]), "res": sb(f"res{s}", [P, NT, D]),
                 "xz": sb(f"xz{s}", [P, NC, T + 1]), "ctx": sb(f"ctx{s}", [P, NC, T]),
                 "st": sb(f"st{s}", [P, NT, 6]), "mv": sb(f"mv{s}", [P, NT, 2]),
                 "ve": sb(f"ve{s}", [P, NT]), "rstd": sb(f"rstd{s}", [P, NT])}
            for key, table in (("n", NYSTROM), ("d", DILATED), ("f", FFN), ("r", MEMORY), ("g", GATED)):
                v[key], _ = carve(arena[:], table)
            for under, table in PINV.items():
                v["n"].update(carve(arena[:, words_before(NYSTROM, under):], table)[0])
            for under, table in GATED_UNDER.items():
                v["g"].update(carve(arena[:, words_before(GATED, under):], table)[0])
            v["n"]["z"] = v["n"]["kz"][:, :, M:M + DH0]
            for key in "nd":
                v[key]["o"], v[key]["oT"] = v[key]["q"], v[key]["k"]
            v["bk"] = BankTurns([psum[4 * s + i] for i in range(4)],
                            [sem(f"bank_filled{s}_{i}") for i in range(4)],
                            [sem(f"bank_emptied{s}_{i}") for i in range(4)], bank_order())
            st.append(v)

        NEGH = sb("neghalf", [P, NT])

        with nc.Block() as block:
            loaded = {n: sem("load_" + n) for n in ("sp", "act")}
            order = [(W[n][:], a["W_" + n].rearrange("(c p) n -> p c n", p=P)) for n in MATRICES]
            order += [(w2[:], a["W_ff2"].rearrange("(c p) n -> p c n", p=P))]
            order2 = [(bias[n][:], a["B_" + n]) for n in COLUMNS] + [(rows[n][:], a["R_" + n]) for n in ROWS]
            order2 += [(ident[:], a["C_ident"]), (identb[:], a["C_identb"])]
            order2 += [(consts[n][:], a["C_" + n]) for n in consts]
            order2 += [(exponents, a["C_exponents"]), (keep, a["C_keep"])]
            n_sp, n_act = 16 * len(order), 16 * len(order2)
            step = sem("setup_dve")
            act_step = sem("setup_act")
            pool_step = sem("setup_pool")
            pe_step = sem("setup_pe")

            @block.sync
            def _(sp):
                for dst, src in order:
                    sp.dma_start(dst, src).then_inc(loaded["sp"], 16)

            @block.gpsimd
            def _(pool):
                for s in range(STREAMS):
                    pool.memset(st[s]["xz"][:], 0.0)
                pool.memset(NEGH[:], -0.5)
                pool.memset(small[:, 63:64], 1.0 / (FF * D)).then_inc(pool_step, 1)

            @block.scalar
            def _(act):
                for dst, src in order2:
                    act.dma_start(dst, src).then_inc(loaded["act"], 16)
                act.wait_ge(loaded["act"], n_act)
                act.activation(small[:, 0:4], bias["decay"][:], ACT.Exp, scale=-1.0).then_inc(act_step, 1)
                act.wait_ge(act_step, 1)
                act.activation(small[:, 4:8], small[:, 0:4], ACT.Ln, bias=1.0).then_inc(act_step, 1)
                act.wait_ge(step, 1)
                for h in range(H1):
                    act.activation(dec0[:, h, :], exponents, ACT.Exp, bias=bias["alpha"][:, h:h + 1],
                                   scale=small[:, 8 + h:9 + h])
                    act.activation(dec1[:, h, :], exponents[:, 0:P], ACT.Exp, bias=bias["alpha"][:, h:h + 1],
                                   scale=small[:, 8 + h:9 + h]).then_inc(act_step, 1)
                act.activation(small[:, 12:13], bias["gate"][:], ACT.Exp, scale=-1.0).then_inc(act_step, 1)

            @block.vector
            def _(dve):
                n = 0

                def link(ins):
                    nonlocal n
                    n += 1
                    ins.then_inc(step, 1)
                    dve.wait_ge(step, n)

                dve.wait_ge(act_step, 2)
                link(dve.tensor_scalar(small[:, 8:12], small[:, 4:8], -1.0, None, ALU.mult))
                dve.wait_ge(act_step, 2 + H1)
                link(dve.tensor_tensor(dec0[:], dec0[:], keep[:, None, :].to_broadcast([P, H1, T]), ALU.mult))
                link(dve.tensor_tensor(dec1[:], dec1[:], keep[:, None, 0:P].to_broadcast([P, H1, P]), ALU.mult))
                dve.wait_ge(act_step, 3 + H1)
                link(dve.tensor_scalar(small[:, 13:14], small[:, 12:13], 1.0, None, ALU.add))
                link(dve.reciprocal(small[:, 14:15], small[:, 13:14]))
                link(dve.tensor_scalar(cosg[:], consts["cosq"][:], small[:, 14:15], None, ALU.mult))
                link(dve.tensor_scalar(sing[:], consts["sinq"][:], small[:, 14:15], None, ALU.mult))
                dve.wait_ge(loaded["sp"], n_sp)
                for i, w in enumerate((W["ff1"], w2)):
                    flat = w[:].rearrange("p c n -> p (c n)")
                    link(dve.tensor_reduce(small[:, 16 + i:17 + i], flat, axis=AX.X, op=ALU.add,
                                           apply_absolute_value=True))
                dve.wait_ge(pe_step, 1)
                for i, w in enumerate((W["ff1"], w2)):
                    flat = w[:].rearrange("p c n -> p (c n)")
                    c = small[:, 20 + 4 * i:24 + 4 * i]
                    link(dve.tensor_scalar(c[:, 0:1], psum[0][:, i:i + 1], small[:, 63:64], 1e-8, ALU.mult, ALU.max))
                    link(dve.reciprocal(c[:, 1:2], c[:, 0:1]))
                    for half in range(2):
                        f = flat[:, half * 1024:(half + 1) * 1024]
                        link(dve.tensor_scalar(f, f, c[:, 1:2], None, ALU.mult))
                        link(dve.tensor_scalar(scratch, f, -0.5, -1.0, ALU.is_lt, ALU.mult))
                        link(dve.scalar_tensor_tensor(f, f, 0.5, scratch, ALU.is_gt, ALU.add))

            @block.tensor
            def _(pe):
                pe.wait_ge(loaded["act"], n_act)
                pe.wait_ge(pool_step, 1)
                pe.wait_ge(step, 9)
                pe.matmul(psum[0][:, 0:2], consts["ones"][:], small[:, 16:18], start=True, stop=True).then_inc(pe_step, 1)

        def transposed(x, t, c):
            return x[:, t, c * P:(c + 1) * P]

        x_of = lambda s: st[s]["xz"][:, :, 1:T + 1]

        def pe_transposes(pe, s, name, src):
            b = st[s]["bk"].claim(pe, name)
            for c in range(NC):
                for t in range(NT):
                    last = pe.transpose(b[:, c * T + t * P:c * T + (t + 1) * P], transposed(src, t, c), ident[:])
            last.then_inc(st[s]["bk"].filled(name), 1)

        def pe_features(pe, s, name, w, col, x):
            b = st[s]["bk"].claim(pe, name)
            for m in range(NC):
                for c in range(NC):
                    last = pe.matmul(b[:, m * T:(m + 1) * T], w[:, c, col + m * P:col + (m + 1) * P], x[:, c, :],
                                     start=c == 0, stop=c == NC - 1)
            last.then_inc(st[s]["bk"].filled(name), 1)

        def pe_tokens(pe, s, name, w, col, x, chunks=NC):
            b = st[s]["bk"].claim(pe, name)
            for t in range(NT):
                for c in range(chunks):
                    last = pe.matmul(b[:, t * D:(t + 1) * D], x[:, c, t * P:(t + 1) * P], w[:, c, col:col + D],
                                     start=c == 0, stop=c == chunks - 1)
            last.then_inc(st[s]["bk"].filled(name), 1)

        def pe_nystrom(pe, s):
            v, bk = st[s], st[s]["bk"]
            n, x = v["n"], x_of(s)
            pe.wait_ge(sem(f"inputs{s}"), 48)
            pe_features(pe, s, "n_q", W["qkv"], 0, x)
            pe_features(pe, s, "n_k", W["qkv"], D, x)
            pe_tokens(pe, s, "n_v", W["qkv"], 2 * D, x)
            yield 1
            pe.wait_ge(sem(f"n_landmarks{s}"), 1)
            b = bk.claim(pe, "n_sim2")
            for p in range(PAIRS):
                c, h = p // 4, 2 * (p % 4)
                last = pe.matmul(b[:, p * M:(p + 1) * M], n["qlm"][:, c, h:h + 2, :], n["kl"][:, c, :], start=True, stop=True)
            last.then_inc(bk.filled("n_sim2"), 1)
            pe.wait_ge(sem(f"n_half{s}"), 4)
            for t in range(NT):
                for c in range(NC):
                    b = bk.claim(pe, f"n_max1_{t}{c}")
                    pe.matmul(b[:], n["qb"][:, c, t * P:(t + 1) * P], n["klmb"][:, c, :, :], start=True, stop=True)\
                        .then_inc(bk.filled(f"n_max1_{t}{c}"), 1)
            for i in range(4):
                b = bk.claim(pe, f"n_max3_{i}")
                for j in range(2):
                    p = 2 * i + j
                    c, h = p // 4, 2 * (p % 4)
                    last = pe.matmul(b[:, j * T:(j + 1) * T], n["qlmb"][:, c, h:h + 2, :], n["kb"][:, c, :], start=True, stop=True)
                last.then_inc(bk.filled(f"n_max3_{i}"), 1)
            yield 2
            pe.wait_ge(sem(f"n_neg{s}"), 1)
            b = bk.claim(pe, "n_negT")
            bb = b[:, 0:3 * P // 2].bitcast(BF16)
            for i in range(3):
                last = pe.transpose(bb[:, i * P:(i + 1) * P], n["neg"][:, i, :], identb[:])
            last.then_inc(bk.filled("n_negT"), 1)
            yield 3
            bk.await_emptied(pe, "n_negT")
            bk.await_emptied(pe, "n_k")
            for i in range(4):
                b = bk.claim(pe, f"n_s1_{i}")
                for j in range(2):
                    p = 2 * i + j
                    c, h = p // 4, 2 * (p % 4)
                    pe.matmul(b[:, j * T:(j + 1) * T], n["klm"][:, c, h:h + 2, :], n["q"][:, c, :], start=True, stop=False)
                    last = pe.matmul(b[:, j * T:(j + 1) * T], selp[:, p, :], n["negT"][:, 0:2, :], start=False, stop=True)
                last.then_inc(bk.filled(f"n_s1_{i}"), 1)
            for t in range(NT):
                for c in range(NC):
                    name = f"n_s3_{t}{c}"
                    b = bk.claim(pe, name)
                    pe.matmul(b[:], n["k"][:, c, t * P:(t + 1) * P], n["qlm"][:, c, :, :], start=True, stop=False)
                    for j in range(4):
                        last = pe.matmul(b[:, j * P:(j + 1) * P], sel16[:, 4 * c + j, :], n["negT"][:, 2, :],
                                         start=False, stop=j == 3)
                    last.then_inc(bk.filled(name), 1)
            yield 4
            pe.wait_ge(sem(f"n_diagonal_a{s}"), 1)
            for g in range(2):
                b = bk.claim(pe, f"n_aT_{g}")
                for p in range(4):
                    last = pe.transpose(b[:, p * P:(p + 1) * P], n["ad"][:, 4 * g + p, :], ident[:])
                last.then_inc(bk.filled(f"n_aT_{g}"), 1)
            b = bk.claim(pe, "n_y")
            bk.await_emptied(pe, "n_v")
            pe.wait_ge(sem(f"n_vones{s}"), 1)
            bk.await_emptied(pe, "n_s3_11")
            for p in range(PAIRS):
                for t in range(NT):
                    last = pe.matmul(b[:, p * 2 * VW:(p + 1) * 2 * VW], n["e3"][:, t, p // 4, (p % 4) * P:(p % 4 + 1) * P],
                                     n["v"][:, t, 2 * p:2 * p + 2, :], start=t == 0, stop=t == NT - 1)
            last.then_inc(bk.filled("n_y"), 1)
            yield 5

            def products(name, g, lhs, rhs, width):
                b = bk.claim(pe, f"{name}_{g}")
                for p in range(4):
                    last = pe.matmul(b[:, p * width:(p + 1) * width], lhs[:, 4 * g + p, :], rhs[:, 4 * g + p, :],
                                     start=True, stop=True)
                last.then_inc(bk.filled(f"{name}_{g}"), 1)

            for g in range(2):
                bk.await_emptied(pe, f"n_aT_{g}")
                products("n_k0", g, n["aT"], n["a"], M)
                products("n_kT0", g, n["ad"], n["aT"], P)
            for i in range(PINV_ITERS - 1):
                yield 6 + 3 * i
                for g in range(2):
                    bk.await_emptied(pe, f"n_k{i}_{g}")
                    bk.await_emptied(pe, f"n_kT{i}_{g}")
                    products(f"n_p{i}", g, n["kkT"], n["t1"], M)
                yield 7 + 3 * i
                for g in range(2):
                    bk.await_emptied(pe, f"n_p{i}_{g}")
                    products(f"n_t{i}", g, n["t2"], n["kkT"], P)
                yield 8 + 3 * i
                for g in range(2):
                    bk.await_emptied(pe, f"n_t{i}_{g}")
                    pe.wait_ge(sem(f"n_diagonal_k{s}"), 2 * i + g + 1)
                    products(f"n_kT{i + 1}", g, n["kk"], n["t3"], P)
                    if i == 0:
                        bk.await_emptied(pe, "n_y")
                    if i < PINV_ITERS - 2:
                        products(f"n_k{i + 1}", g, n["t3"], n["kz"], M + DH0)
                    else:
                        products(f"n_k{i + 1}", g, n["t3"], n["z"], DH0)
            yield 21
            for g in range(2):
                bk.await_emptied(pe, f"n_kT{PINV_ITERS - 1}_{g}")
                bk.await_emptied(pe, f"n_k{PINV_ITERS - 1}_{g}")
            for j in range(4):
                if j:
                    yield 21 + j
                    bk.await_emptied(pe, f"n_w{j - 1}")
                b = bk.claim(pe, f"n_w{j}")
                for p in range(PAIRS):
                    last = pe.matmul(b[:, p * DH0:(p + 1) * DH0], (n["kkT"] if j < 3 else n["aT"])[:, p, :],
                                     (n["z"] if j == 0 else n["z2"])[:, p, :], start=True, stop=True)
                last.then_inc(bk.filled(f"n_w{j}"), 1)
            yield 25
            bk.await_emptied(pe, "n_w3")
            for t in range(NT):
                b = bk.claim(pe, f"n_o{t}")
                for p in range(PAIRS):
                    last = pe.matmul(b[:, p * 2 * VW:(p + 1) * 2 * VW], n["e1"][:, p, t * P:(t + 1) * P], n["g"][:, p, :],
                                     start=True, stop=True)
                last.then_inc(bk.filled(f"n_o{t}"), 1)
            yield 26
            bk.await_emptied(pe, "n_o0")
            bk.await_emptied(pe, "n_o1")
            pe_transposes(pe, s, "n_oT", n["o"])
            yield 27
            bk.await_emptied(pe, "n_oT")
            pe_tokens(pe, s, "n_out", W["out"], 0, n["oT"])
            yield 28
            pe_norm(pe, s, "0", "n_xT")

        def dve_nystrom(dve, s, link):
            v, bk = st[s], st[s]["bk"]
            n = v["n"]
            b = bk.await_filled(dve, "n_q")
            for m in range(NC):
                last = dve.tensor_scalar(n["q"][:, m, :], b[:, m * T:(m + 1) * T], bias["q0"][:, m:m + 1],
                                         1.0 / np.sqrt(DH0), ALU.add, ALU.mult)
            last.then_inc(bk.emptied("n_q"), 1)
            bk.await_emptied(dve, "n_q")
            dve.tensor_reduce(n["qs"][:], n["q"][:].rearrange("p c (m l) -> p c m l", l=LM), axis=AX.X, op=ALU.add)
            bk.await_emptied(dve, "n_k")
            link(dve.tensor_reduce(n["ks"][:], n["k"][:].rearrange("p c (m l) -> p c m l", l=LM), axis=AX.X, op=ALU.add))
            for c in range(NC):
                m = hmask[:, HC:2 * HC, None].to_broadcast([P, HC, M])
                dve.tensor_tensor(n["qlm"][:, c], n["qs"][:, c, None, :].to_broadcast([P, HC, M]), m, ALU.mult)
                dve.tensor_tensor(n["klm"][:, c], n["ks"][:, c, None, :].to_broadcast([P, HC, M]), m, ALU.mult)
            dve.tensor_scalar(n["kl"][:], n["ks"][:], 1.0 / LM, None, ALU.mult).then_inc(sem(f"n_landmarks{s}"), 1)
            b = bk.await_filled(dve, "n_v")
            dve.tensor_tensor(n["v"][:, :, :, 0:DH0], b[:].rearrange("p (t h d) -> p t h d", t=NT, h=H0),
                              rows["v0"][:].rearrange("p (h d) -> p h d", h=H0)[:, None].to_broadcast([P, NT, H0, DH0]),
                              ALU.add).then_inc(bk.emptied("n_v"), 1)
            yield 1
            b = bk.await_filled(dve, "n_sim2")
            b3 = b[:].rearrange("p (a m) -> p a m", m=M)
            link(dve.tensor_reduce(n["mx2"][:], b3, axis=AX.X, op=ALU.max))
            dve.tensor_tensor(n["a"][:], b3, n["mx2"][:, :, None].to_broadcast([P, PAIRS, M]), ALU.subtract)\
                .then_inc(bk.emptied("n_sim2"), 1)
            for t in range(NT):
                for c in range(NC):
                    b = bk.await_filled(dve, f"n_max1_{t}{c}")
                    dve.tensor_reduce(n["mx1"][:, t, c * HC:(c + 1) * HC], b[:].rearrange("p (h m) -> p h m", m=M),
                                      axis=AX.X, op=ALU.max).then_inc(bk.emptied(f"n_max1_{t}{c}"), 1)
            for i in range(4):
                b = bk.await_filled(dve, f"n_max3_{i}")
                dve.tensor_reduce(n["mx3"][:, 2 * i:2 * i + 2], b[:].rearrange("p (a t) -> p a t", t=T),
                                  axis=AX.X, op=ALU.max).then_inc(bk.emptied(f"n_max3_{i}"), 1)
            bk.await_emptied(dve, "n_max1_11")
            bk.await_emptied(dve, "n_max3_3")
            dve.wait_ge(sem(f"n_zeros{s}"), 1)
            dve.tensor_scalar(n["neg"][:, 0:2, 0:H0], n["mx1"][:], -1.0, None, ALU.mult)
            dve.tensor_scalar(n["neg"][:, 2, 0:PAIRS], n["mx3"][:], -1.0, None, ALU.mult).then_inc(sem(f"n_neg{s}"), 1)
            yield 2
            dve.wait_ge(sem(f"n_exp2{s}"), 1)
            link(dve.tensor_reduce(n["sum2"][:], n["a"][:], axis=AX.X, op=ALU.add))
            link(dve.reciprocal(n["rs2"][:], n["sum2"][:]))
            dve.tensor_tensor(n["a"][:], n["a"][:], n["rs2"][:, :, None].to_broadcast([P, PAIRS, M]), ALU.mult)\
                .then_inc(sem(f"n_a{s}"), 1)
            yield 4
            b = bk.await_filled(dve, "n_y")
            y = b[:, 0:PAIRS * 2 * VW].rearrange("p (a w) -> p a w", w=2 * VW)
            for u in range(2):
                last = dve.reciprocal(n["ry"][u * M:(u + 1) * M, :], y[u * M:(u + 1) * M, :, u * VW + DH0])
            link(last)
            for u in range(2):
                r = slice(u * M, (u + 1) * M)
                last = dve.tensor_tensor(n["z"][r], y[r, :, u * VW:u * VW + DH0],
                                         n["ry"][r, :, None].to_broadcast([M, PAIRS, DH0]), ALU.mult)
            last.then_inc(bk.emptied("n_y"), 1)
            eye = consts["eye"][:, None, :].to_broadcast([P, 4, M])
            eye325 = consts["eye325"][:, None, :].to_broadcast([P, 4, P])

            def part(b, width, lo, hi):
                return b[:, 0:4 * width].rearrange("p (a m) -> p a m", m=width)[:, :, lo:hi]

            for i in range(PINV_ITERS):
                yield 5 + 3 * i
                for g in range(2):
                    q = slice(4 * g, 4 * g + 4)
                    b = bk.await_filled(dve, f"n_k{i}_{g}")
                    if i == PINV_ITERS - 1:
                        dve.tensor_copy(n["z"][:, q], part(b, DH0, 0, DH0)).then_inc(bk.emptied(f"n_k{i}_{g}"), 1)
                        continue
                    w = M + DH0 if i else M
                    dve.tensor_copy(n["kz"][:, q, 0:w], part(b, w, 0, w))
                    dve.scalar_tensor_tensor(n["t1"][:, q], eye, 7.0, part(b, w, 0, M), ALU.mult, ALU.subtract)\
                        .then_inc(bk.emptied(f"n_k{i}_{g}"), 1)
                if i == PINV_ITERS - 1:
                    break
                yield 6 + 3 * i
                for g in range(2):
                    q = slice(4 * g, 4 * g + 4)
                    b = bk.await_filled(dve, f"n_p{i}_{g}")
                    if i == 0:
                        dve.wait_ge(sem(f"n_cleared{s}"), 2)
                    for u in (0, M):
                        last = dve.scalar_tensor_tensor(n["t2"][u:u + M, q, u:u + M], eye[u:u + M], 15.0,
                                                        part(b, M, 0, M)[u:u + M], ALU.mult, ALU.subtract)
                    last.then_inc(bk.emptied(f"n_p{i}_{g}"), 1)
                yield 7 + 3 * i
                for g in range(2):
                    q = slice(4 * g, 4 * g + 4)
                    b = bk.await_filled(dve, f"n_t{i}_{g}")
                    dve.scalar_tensor_tensor(n["t3"][:, q], part(b, P, 0, P), -0.25, eye325, ALU.mult, ALU.add)\
                        .then_inc(bk.emptied(f"n_t{i}_{g}"), 1)
            for j in range(4):
                yield 21 + j
                b = bk.await_filled(dve, f"n_w{j}")
                w = b[:, 0:PAIRS * DH0].rearrange("p (a d) -> p a d", d=DH0)
                if j < 3:
                    dve.scalar_tensor_tensor(n["z2"][:], n["z"][:], (7.0, 15.0, 13.0)[j], w, ALU.mult, ALU.subtract)\
                        .then_inc(bk.emptied(f"n_w{j}"), 1)
                else:
                    dve.wait_ge(sem(f"n_vones{s}"), 1)
                    for u in range(2):
                        r = slice(u * M, (u + 1) * M)
                        last = dve.tensor_scalar(n["g"][r, :, u * VW:u * VW + DH0], w[r], 0.25, None, ALU.mult)
                    last.then_inc(bk.emptied(f"n_w{j}"), 1)
            yield 25
            for t in range(NT):
                b = bk.await_filled(dve, f"n_o{t}")
                o = b[:, 0:H0 * VW].rearrange("p (h w) -> p h w", w=VW)
                link(dve.reciprocal(n["ro"][:, t, :], o[:, :, DH0]))
                dve.tensor_tensor(n["o"][:, t].rearrange("p (h d) -> p h d", h=H0), o[:, :, 0:DH0],
                                  n["ro"][:, t, :, None].to_broadcast([P, H0, DH0]), ALU.mult)\
                    .then_inc(bk.emptied(f"n_o{t}"), 1)
            yield 27
            dve_residual_norm(dve, s, link, "n_out", "0")

        def act_nystrom(act, s):
            v, bk = st[s], st[s]["bk"]
            n = v["n"]
            b = bk.await_filled(act, "n_k")
            for m in range(NC):
                last = act.activation(n["k"][:, m, :], b[:, m * T:(m + 1) * T], ACT.Identity, bias=bias["k0"][:, m:m + 1])
            last.then_inc(bk.emptied("n_k"), 1)
            yield 1
            bk.await_emptied(act, "n_sim2")
            act.activation(n["a"][:], n["a"][:], ACT.Exp).then_inc(sem(f"n_exp2{s}"), 1)
            yield 2
            b = bk.await_filled(act, "n_negT")
            act.copy(n["negT"][:].rearrange("p a b -> p (a b)"), b[:, 0:3 * P // 2].bitcast(BF16))\
                .then_inc(bk.emptied("n_negT"), 1)
            yield 3
            for i in range(4):
                b = bk.await_filled(act, f"n_s1_{i}")
                act.activation(n["e1"][:, 2 * i:2 * i + 2, :], b[:].rearrange("p (a t) -> p a t", t=T), ACT.Exp)\
                    .then_inc(bk.emptied(f"n_s1_{i}"), 1)
            for t in range(NT):
                for c in range(NC):
                    b = bk.await_filled(act, f"n_s3_{t}{c}")
                    act.activation(n["e3"][:, t, c, :], b[:], ACT.Exp).then_inc(bk.emptied(f"n_s3_{t}{c}"), 1)
            yield 4
            for g in range(2):
                b = bk.await_filled(act, f"n_aT_{g}")
                act.copy(n["aT"][:, 4 * g:4 * g + 4], b[:].rearrange("p (a m) -> p a m", m=P))\
                    .then_inc(bk.emptied(f"n_aT_{g}"), 1)
            for i in range(PINV_ITERS):
                yield 5 + 3 * i
                for g in range(2):
                    b = bk.await_filled(act, f"n_kT{i}_{g}")
                    act.copy(n["kkT"][:, 4 * g:4 * g + 4], b[:].rearrange("p (a m) -> p a m", m=P))\
                        .then_inc(bk.emptied(f"n_kT{i}_{g}"), 1)
                if i < PINV_ITERS - 1:
                    yield 6 + 3 * i
                    for g in range(2):
                        q = slice(4 * g, 4 * g + 4)
                        bk.await_emptied(act, f"n_k{i}_{g}")
                        if i == 0:
                            act.wait_ge(sem(f"n_cleared{s}"), 1)
                        for u in (0, M):
                            last = act.copy(n["kk"][u:u + M, q, u:u + M], n["kz"][u:u + M, q, 0:M])
                        last.then_inc(sem(f"n_diagonal_k{s}"), 1)
            yield 26
            b = bk.await_filled(act, "n_oT")
            act.copy(n["oT"][:].rearrange("p c t -> p (c t)"), b[:]).then_inc(bk.emptied("n_oT"), 1)
            yield 28
            act_norm(act, s, "n_xT")

        def pool_nystrom(pool, s):
            v, bk = st[s], st[s]["bk"]
            n = v["n"]
            pool.wait_ge(sem(f"inputs{s}"), 48)
            pool.memset(n["neg"][:], 0.0).then_inc(sem(f"n_zeros{s}"), 1)
            pool.tensor_tensor(out=v["res"][:], in0=v["x"][:], in1=rows["o0"][:, None, :].to_broadcast([P, NT, D]),
                               op=ALU.add).then_inc(sem(f"res{s}"), 1)
            pool.memset(n["v"][:, :, :, DH0], 1.0)
            pool.memset(n["g"][:], 0.0).then_inc(sem(f"n_gz{s}"), 1)
            pool.wait_ge(sem(f"n_gz{s}"), 1)
            pool.memset(n["g"][0:M, :, DH0], 1.0)
            pool.memset(n["g"][M:P, :, VW + DH0], 1.0).then_inc(sem(f"n_vones{s}"), 1)
            pool.wait_ge(sem(f"n_vones{s}"), 1)
            bk.await_emptied(pool, "n_q")
            pool.tensor_copy(n["qb"][:], n["q"][:]).then_inc(sem(f"n_half{s}"), 1)
            bk.await_emptied(pool, "n_k")
            pool.tensor_copy(n["kb"][:], n["k"][:]).then_inc(sem(f"n_half{s}"), 1)
            pool.wait_ge(sem(f"n_landmarks{s}"), 1)
            pool.tensor_copy(n["klmb"][:], n["klm"][:]).then_inc(sem(f"n_half{s}"), 1)
            pool.tensor_copy(n["qlmb"][:], n["qlm"][:]).then_inc(sem(f"n_half{s}"), 1)
            yield 2
            bk.await_done(pool, "n_max3_3")
            pool.wait_ge(sem(f"n_a{s}"), 1)
            pool.tensor_tensor(out=n["ad"].rearrange("p a (u m) -> p a u m", u=2),
                               in0=n["a"][:, :, None, :].to_broadcast([P, PAIRS, 2, M]),
                               in1=consts["halves"][:, None, :, None].to_broadcast([P, PAIRS, 2, M]), op=ALU.mult)\
                .then_inc(sem(f"n_diagonal_a{s}"), 1)
            yield 4
            bk.await_done(pool, "n_s3_11")
            pool.memset(n["kk"], 0.0).then_inc(sem(f"n_cleared{s}"), 1)
            bk.await_done(pool, "n_y")
            pool.memset(n["t2"], 0.0).then_inc(sem(f"n_cleared{s}"), 1)
            yield 27
            pool_norm(pool, s, "0")

        def dve_norm(dve, s, link, key, src, dst):
            v = st[s]
            for t in range(NT):
                last = dve.bn_stats(v["st"][:, t, :], src[:, t, :])
            link(last)
            for t in range(NT):
                last = dve.bn_aggr(v["mv"][:, t, :], v["st"][:, t, :])
            link(last)
            dve.tensor_scalar(v["ve"][:], v["mv"][:, :, 1], EPS, None, ALU.add).then_inc(sem(f"variance{key}_{s}"), 1)
            dve.wait_ge(sem(f"rstd{key}_{s}"), 1)
            for t in range(NT):
                last = dve.tensor_scalar(dst[:, t, :], src[:, t, :], v["mv"][:, t, 0:1], v["rstd"][:, t:t + 1],
                                         ALU.subtract, ALU.mult)
            last.then_inc(sem(f"x{key}_{s}"), 1)

        def dve_residual_norm(dve, s, link, name, key):
            v, bk = st[s], st[s]["bk"]
            b = bk.await_filled(dve, name)
            dve.wait_ge(sem(f"res{s}"), 1 + int(key))
            dve.tensor_tensor(v["y"][:].rearrange("p t d -> p (t d)"), b[:], v["res"][:].rearrange("p t d -> p (t d)"),
                              ALU.add).then_inc(bk.emptied(name), 1)
            bk.await_emptied(dve, name)
            dve_norm(dve, s, link, key, v["y"], v["x"])

        def pool_norm(pool, s, key):
            v = st[s]
            pool.wait_ge(sem(f"variance{key}_{s}"), 1)
            pool.tensor_tensor(out=v["rstd"][:], in0=v["ve"][:], in1=NEGH[:], op=ALU.pow)\
                .then_inc(sem(f"rstd{key}_{s}"), 1)

        def pe_norm(pe, s, key, name):
            pe.wait_ge(sem(f"x{key}_{s}"), 1)
            pe_transposes(pe, s, name, st[s]["x"])

        def act_norm(act, s, name):
            v, bk = st[s], st[s]["bk"]
            b = bk.await_filled(act, name)
            act.copy(x_of(s), b[:].rearrange("p (c t) -> p c t", c=NC)).then_inc(bk.emptied(name), 1)

        def pe_dilated(pe, s):
            v, bk = st[s], st[s]["bk"]
            n, x = v["d"], x_of(s)
            yield 100
            bk.await_emptied(pe, "n_xT")
            pe_features(pe, s, "d_q", W["dq"], 0, x)
            pe_features(pe, s, "d_k", W["dk"], 0, v["ctx"])
            pe_tokens(pe, s, "d_v", W["dv"], 0, v["ctx"])
            for c in range(NC):
                yield 110 + 10 * c
                pe.wait_ge(sem(f"d_half{s}"), 2 + c)
                for i in range(6):
                    t, heads, keys = (0, range(4 * i, 4 * i + 4), P) if i < 2 else (1, range(2 * i - 4, 2 * i - 2), T)
                    b = bk.claim(pe, f"d_m{c}_{i}")
                    for j, h in enumerate(heads):
                        pe.matmul(b[:, j * keys:(j + 1) * keys], n["qmb"][:, h, t * P:(t + 1) * P], n["kb"][:, c, 0:keys],
                                  start=True, stop=False)
                        last = pe.matmul(b[:, (j + 1) * keys - P:(j + 1) * keys], identb[:], consts["above"][:],
                                         start=False, stop=True)
                    last.then_inc(bk.filled(f"d_m{c}_{i}"), 1)
                yield 111 + 10 * c
                pe.wait_ge(sem(f"d_neg{s}"), 1 + c)
                b = bk.claim(pe, f"d_negT{c}")
                bb = b[:, 0:P].bitcast(BF16)
                for t in range(NT):
                    last = pe.transpose(bb[:, t * P:(t + 1) * P], n["neg"][:, t, :], identb[:])
                last.then_inc(bk.filled(f"d_negT{c}"), 1)
                yield 112 + 10 * c
                pe.wait_ge(sem(f"d_qm{s}"), 1 + c)
                bk.await_emptied(pe, f"d_negT{c}")
                bk.await_emptied(pe, "d_k")
                for i in range(6):
                    b = bk.claim(pe, f"d_s{c}_{i}")
                    if i < 4:
                        pe.matmul(b[:], n["k"][:, c, 0:P], n["qm"][:, 2 * i:2 * i + 2, :], start=True, stop=False)
                        for j in range(2):
                            pe.matmul(b[:, j * T:(j + 1) * T], sel16[:, c * HC + 2 * i + j, :], n["negT"][:, 0:2, :],
                                      start=False, stop=False)
                            last = pe.matmul(b[:, j * T:j * T + P], identb[:], consts["below"][:], start=False, stop=j == 1)
                    else:
                        h = 4 * (i - 4)
                        pe.matmul(b[:], n["k"][:, c, P:T], n["qm"][:, h:h + 4, P:T], start=True, stop=False)
                        for j in range(4):
                            pe.matmul(b[:, j * P:(j + 1) * P], sel16[:, c * HC + h + j, :], n["negT"][:, 1, :],
                                      start=False, stop=False)
                            last = pe.matmul(b[:, j * P:(j + 1) * P], identb[:], consts["below"][:], start=False, stop=j == 3)
                    last.then_inc(bk.filled(f"d_s{c}_{i}"), 1)
                yield 113 + 10 * c
                pe.wait_ge(sem(f"d_v{s}"), 2)
                bk.await_emptied(pe, f"d_s{c}_5")
                for t in range(NT):
                    b = bk.claim(pe, f"d_o{c}_{t}")
                    for h in range(HC):
                        out = b[:, h * BR * VW:(h + 1) * BR * VW]
                        last = pe.matmul(out, n["p0"][:, h, t * P:(t + 1) * P], n["v"][:, 0, c * HC + h, :, :],
                                         start=True, stop=t == 0)
                        if t:
                            last = pe.matmul(out, n["p1"][:, h, :], n["v"][:, 1, c * HC + h, :, :], start=False, stop=True)
                    last.then_inc(bk.filled(f"d_o{c}_{t}"), 1)
            yield 131
            pe.wait_ge(sem(f"d_o{s}"), 1)
            pe_transposes(pe, s, "d_oT", n["o"])
            yield 132
            bk.await_emptied(pe, "d_oT")
            pe_tokens(pe, s, "d_out", W["do"], 0, n["oT"])
            yield 133
            pe_norm(pe, s, "1", "d_xT")

        def dve_dilated(dve, s, link):
            v, bk = st[s], st[s]["bk"]
            n = v["d"]
            yield 100
            b = bk.await_filled(dve, "d_q")
            for m in range(NC):
                last = dve.tensor_scalar(n["q"][:, m, :], b[:, m * T:(m + 1) * T], bias["dq"][:, m:m + 1],
                                         float(DH0) ** -0.5, ALU.add, ALU.mult)
            last.then_inc(bk.emptied("d_q"), 1)
            b = bk.await_filled(dve, "d_v")
            dve.tensor_tensor(n["v"][:, :, :, 0, 0:DH0], b[:].rearrange("p (t h d) -> p t h d", t=NT, h=H0),
                              rows["dv"][:].rearrange("p (h d) -> p h d", h=H0)[:, None].to_broadcast([P, NT, H0, DH0]),
                              ALU.add).then_inc(bk.emptied("d_v"), 1)
            for c in range(NC):
                yield 110 + 10 * c
                bk.await_emptied(dve, "d_q")
                if c:
                    bk.await_done(dve, f"d_s{c - 1}_5")
                dve.tensor_tensor(n["qm"][:], n["q"][:, c, None, :].to_broadcast([P, HC, T]),
                                  hmask[:, 0:HC, None].to_broadcast([P, HC, T]), ALU.mult).then_inc(sem(f"d_qm{s}"), 1)
                for i in range(6):
                    b = bk.await_filled(dve, f"d_m{c}_{i}")
                    t, h, k = (0, 4 * i, 4) if i < 2 else (1, 2 * i - 4, 2)
                    dve.tensor_reduce(n["mx"][:, t, c * HC + h:c * HC + h + k], b[:].rearrange("p (h k) -> p h k", h=k),
                                      axis=AX.X, op=ALU.max).then_inc(bk.emptied(f"d_m{c}_{i}"), 1)
                for i in (3, 4, 5):
                    bk.await_emptied(dve, f"d_m{c}_{i}")
                dve.wait_ge(sem(f"d_v{s}"), 1)
                if c:
                    bk.await_done(dve, f"d_negT{c - 1}")
                dve.tensor_scalar(n["neg"][:, :, c * HC:(c + 1) * HC], n["mx"][:, :, c * HC:(c + 1) * HC], -1.0, None,
                                  ALU.mult).then_inc(sem(f"d_neg{s}"), 1)
            yield 130
            for c in range(NC):
                for t in range(NT):
                    bk.await_emptied(dve, f"d_o{c}_{t}")
            dve.tensor_scalar(n["s"][:].rearrange("p t h b -> p (t h b)"),
                              n["n"][:].rearrange("p t h b w -> p (t h b) w")[:, :, DH0], TINY, None, ALU.max)\
                .then_inc(sem(f"d_sum{s}"), 1)
            valid = consts["valid"][:].rearrange("p (h b) -> p h b", b=BR)[:, None].to_broadcast([P, NT, H0, BR])
            allh = [P, NT * H0, BR]

            def flat(key):
                return n[key][:].rearrange("p t h b -> p (t h) b")

            lm = n["lm"][:].rearrange("p t h -> p (t h)")
            rz = n["rz"][:].rearrange("p t h -> p (t h)")
            dve.wait_ge(sem(f"d_sum{s}"), 2)
            for t in range(NT):
                last = dve.tensor_tensor(n["ls"][:, t], n["ls"][:, t], n["neg"][:, t, 0:H0, None].to_broadcast([P, H0, BR]),
                                         ALU.subtract)
            link(last)
            link(dve.tensor_tensor(n["ls"][:], n["ls"][:], valid, ALU.mult))
            link(dve.tensor_scalar(n["isz"][:], n["ls"][:], 0.0, NEG, ALU.is_equal, ALU.mult))
            link(dve.tensor_tensor(n["ls"][:], n["ls"][:], n["isz"][:], ALU.add))
            link(dve.tensor_reduce(lm, flat("ls"), axis=AX.X, op=ALU.max))
            dve.tensor_tensor(flat("w"), flat("ls"), lm[:, :, None].to_broadcast(allh), ALU.subtract)\
                .then_inc(sem(f"d_sum{s}"), 1)
            dve.wait_ge(sem(f"d_sum{s}"), 4)
            link(dve.tensor_reduce(lm, flat("w"), axis=AX.X, op=ALU.add))
            dve.reciprocal(rz, lm)
            link(dve.reciprocal(n["rc"][:], n["s"][:]))
            link(dve.tensor_tensor(flat("w"), flat("w"), rz[:, :, None].to_broadcast(allh), ALU.mult))
            link(dve.tensor_tensor(n["w"][:], n["w"][:], valid, ALU.mult))
            link(dve.tensor_tensor(n["w"][:], n["w"][:], n["rc"][:], ALU.mult))
            for t in range(NT):
                r = n["n"][:, t].rearrange("p h b w -> p (h b) w")[:, :, 0:DH0]
                last = dve.tensor_tensor(r, r, n["w"][:, t].rearrange("p h b -> p (h b)")[:, :, None]
                                         .to_broadcast([P, H0 * BR, DH0]), ALU.mult)
            link(last)
            for t in range(NT):
                last = dve.tensor_reduce(n["o"][:, t].rearrange("p (h d) -> p h d", h=H0),
                                         n["n"][:, t].rearrange("p h b w -> p h w b")[:, :, 0:DH0, :], axis=AX.X, op=ALU.add)
            last.then_inc(sem(f"d_o{s}"), 1)
            yield 132
            dve_residual_norm(dve, s, link, "d_out", "1")

        def act_dilated(act, s):
            v, bk = st[s], st[s]["bk"]
            n = v["d"]
            yield 100
            b = bk.await_filled(act, "d_k")
            for m in range(NC):
                last = act.activation(n["k"][:, m, :], b[:, m * T:(m + 1) * T], ACT.Identity, bias=bias["dk"][:, m:m + 1])
            last.then_inc(bk.emptied("d_k"), 1)
            for c in range(NC):
                yield 111 + 10 * c
                b = bk.await_filled(act, f"d_negT{c}")
                act.copy(n["negT"][:].rearrange("p a b -> p (a b)"), b[:, 0:P].bitcast(BF16))\
                    .then_inc(bk.emptied(f"d_negT{c}"), 1)
                yield 112 + 10 * c
                if c:
                    bk.await_done(act, f"d_o{c - 1}_1")
                for i in range(6):
                    b = bk.await_filled(act, f"d_s{c}_{i}")
                    if i < 4:
                        out = n["p0"][:, 2 * i:2 * i + 2, :].rearrange("p h t -> p (h t)")
                    else:
                        out = n["p1"][:, 4 * i - 16:4 * i - 12, :].rearrange("p h t -> p (h t)")
                    act.activation(out, b[:], ACT.Exp).then_inc(bk.emptied(f"d_s{c}_{i}"), 1)
                yield 113 + 10 * c
                for t in range(NT):
                    b = bk.await_filled(act, f"d_o{c}_{t}")
                    act.copy(n["n"][:, t, c * HC:(c + 1) * HC].rearrange("p h b w -> p (h b w)"), b[:, 0:HC * BR * VW])\
                        .then_inc(bk.emptied(f"d_o{c}_{t}"), 1)
            yield 130
            act.wait_ge(sem(f"d_sum{s}"), 1)
            act.activation(n["ls"][:], n["s"][:], ACT.Ln).then_inc(sem(f"d_sum{s}"), 1)
            act.wait_ge(sem(f"d_sum{s}"), 3)
            act.activation(n["w"][:], n["w"][:], ACT.Exp).then_inc(sem(f"d_sum{s}"), 1)
            yield 131
            b = bk.await_filled(act, "d_oT")
            act.copy(n["oT"][:].rearrange("p c t -> p (c t)"), b[:]).then_inc(bk.emptied("d_oT"), 1)
            yield 133
            act_norm(act, s, "d_xT")

        def pool_dilated(pool, s):
            v, bk = st[s], st[s]["bk"]
            n = v["d"]
            yield 100
            pool.wait_ge(sem(f"x0_{s}"), 1)
            pool.tensor_tensor(out=v["res"][:], in0=v["x"][:], in1=rows["do"][:, None, :].to_broadcast([P, NT, D]),
                               op=ALU.add).then_inc(sem(f"res{s}"), 1)
            pool.memset(n["neg"][:], 0.0).then_inc(sem(f"d_v{s}"), 1)
            bk.await_emptied(pool, "d_k")
            pool.tensor_copy(n["kb"][:], n["k"][:]).then_inc(sem(f"d_half{s}"), 1)
            for c in range(NC):
                if c:
                    yield 110 + 10 * c
                bk.await_emptied(pool, "d_q")
                if c:
                    bk.await_done(pool, f"d_m{c - 1}_5")
                pool.tensor_tensor(out=n["qmb"][:], in0=n["q"][:, c, None, :].to_broadcast([P, HC, T]),
                                   in1=hmask[:, 0:HC, None].to_broadcast([P, HC, T]), op=ALU.mult)\
                    .then_inc(sem(f"d_half{s}"), 1)
                if c == 0:
                    bk.await_emptied(pool, "d_v")
                    pool.memset(n["v"][:, :, :, 0, DH0], 1.0).then_inc(sem(f"d_ones{s}"), 1)
                    pool.wait_ge(sem(f"d_ones{s}"), 1)
                    valid = consts["valid"][:].rearrange("p (h b) -> p h b", b=BR)
                    for br in range(1, BR):
                        last = pool.tensor_tensor(out=n["v"][:, :, :, br, :], in0=n["v"][:, :, :, 0, :],
                                                  in1=valid[:, None, :, br, None].to_broadcast([P, NT, H0, VW]), op=ALU.mult)
                    last.then_inc(sem(f"d_v{s}"), 1)
            yield 132
            pool_norm(pool, s, "1")

        def pe_ffn(pe, s):
            v, bk = st[s], st[s]["bk"]
            n, x = v["f"], x_of(s)
            yield 200
            bk.await_emptied(pe, "d_xT")
            for i in range(FC // 2):
                b = bk.claim(pe, f"f_h{i}")
                for j in range(2):
                    f = 2 * i + j
                    for c in range(NC):
                        last = pe.matmul(b[:, j * T:(j + 1) * T], W["ff1"][:, c, f * P:(f + 1) * P], x[:, c, :],
                                         start=c == 0, stop=c == NC - 1)
                last.then_inc(bk.filled(f"f_h{i}"), 1)
            yield 201
            for i in range(FC // 2):
                bk.await_emptied(pe, f"f_h{i}")
            pe_tokens(pe, s, "f_out", w2, 0, n["h"], FC)
            yield 202
            pe_norm(pe, s, "2", "f_xT")

        def act_ffn(act, s):
            v, bk = st[s], st[s]["bk"]
            n = v["f"]
            yield 200
            for i in range(FC // 2):
                b = bk.await_filled(act, f"f_h{i}")
                for j in range(2):
                    f = 2 * i + j
                    last = act.activation(n["h"][:, f, :], b[:, j * T:(j + 1) * T], ACT.Gelu, bias=bias["ff1"][:, f:f + 1])
                last.then_inc(bk.emptied(f"f_h{i}"), 1)
            yield 202
            act_norm(act, s, "f_xT")

        def dve_ffn(dve, s, link):
            yield 201
            dve_residual_norm(dve, s, link, "f_out", "2")

        def pool_ffn(pool, s):
            v = st[s]
            yield 200
            pool.wait_ge(sem(f"x1_{s}"), 1)
            pool.tensor_tensor(out=v["res"][:], in0=v["x"][:], in1=rows["ff2"][:, None, :].to_broadcast([P, NT, D]),
                               op=ALU.add).then_inc(sem(f"res{s}"), 1)
            yield 201
            pool_norm(pool, s, "2")

        def pe_memory(pe, s):
            v, bk = st[s], st[s]["bk"]
            n, xz, x = v["r"], v["xz"], x_of(s)
            yield 300
            bk.await_emptied(pe, "f_xT")
            pe_tokens(pe, s, "r_v", W["mw"], 0, x)
            for i in range(4):
                r = slice(HD1 * (i % 2), HD1 * (i % 2 + 1))
                b = bk.claim(pe, f"r_s{i}")
                for c in range(NC):
                    if i < 2:
                        last = pe.matmul(b[:, c * T:(c + 1) * T], xz[r, c, 0:P], xz[r, c, 1:T + 1], start=True, stop=True)
                    else:
                        last = pe.matmul(b[:, c * P:(c + 1) * P], xz[r, c, P:T], xz[r, c, P + 1:T + 1], start=True, stop=True)
                last.then_inc(bk.filled(f"r_s{i}"), 1)
            yield 301
            for name in ("r_v", "r_s0", "r_s1", "r_s2", "r_s3"):
                bk.await_emptied(pe, name)
            b = bk.claim(pe, "r_r")
            for h in range(H1):
                r, c = slice(HD1 * (h % 2), HD1 * (h % 2 + 1)), h // 2
                pe.matmul(b[r, c * T:(c + 1) * T], n["v"][:, 0, h * HD1:(h + 1) * HD1], n["s0"][:, h, :],
                          start=True, stop=False)
                last = pe.matmul(b[r, c * T + P:(c + 1) * T], n["v"][:, 1, h * HD1:(h + 1) * HD1], n["s1"][:, h, :],
                                 start=False, stop=True)
            last.then_inc(bk.filled("r_r"), 1)
            yield 302
            bk.await_emptied(pe, "r_r")
            pe_tokens(pe, s, "r_out", W["mr"], 0, n["r"])
            yield 303
            pe_norm(pe, s, "3", "r_xT")

        def act_memory(act, s):
            v, bk = st[s], st[s]["bk"]
            n = v["r"]
            yield 300
            b = bk.await_filled(act, "r_v")
            act.copy(n["v"][:].rearrange("p t d -> p (t d)"), b[:]).then_inc(bk.emptied("r_v"), 1)
            yield 301
            b = bk.await_filled(act, "r_r")
            act.copy(n["r"][:].rearrange("p c t -> p (c t)"), b[:]).then_inc(bk.emptied("r_r"), 1)
            yield 303
            act_norm(act, s, "r_xT")

        def dve_memory(dve, s, link):
            v, bk = st[s], st[s]["bk"]
            n = v["r"]
            yield 300
            for i in range(4):
                b = bk.await_filled(dve, f"r_s{i}")
                out, table, t = (n["s0"], dec0, T) if i < 2 else (n["s1"], dec1, P)
                dve.tensor_tensor(out[:, i % 2::2, :], b[:, 0:NC * t].rearrange("p (h t) -> p h t", t=t),
                                  table[:, i % 2::2, :], ALU.mult).then_inc(bk.emptied(f"r_s{i}"), 1)
            yield 302
            dve_residual_norm(dve, s, link, "r_out", "3")

        def pool_memory(pool, s):
            v = st[s]
            yield 300
            pool.wait_ge(sem(f"x2_{s}"), 1)
            pool.tensor_tensor(out=v["res"][:], in0=v["x"][:], in1=v["x"][:], op=ALU.add).then_inc(sem(f"res{s}"), 1)
            yield 302
            pool_norm(pool, s, "3")

        ROPES = (("ka", "ctx", "cosk", "sink"), ("kt", "ctx", "cosk", "sink"),
                 ("qa", "x", "cosq", "sinq"), ("qt", "x", "cosg", "sing"))
        HIGH, LOW = 0, 1
        tables = {"cosg": cosg, "sing": sing, **{k: consts[k] for k in ("cosk", "sink", "cosq", "sinq")}}

        def pe_gated(pe, s):
            v, bk = st[s], st[s]["bk"]
            n, x = v["g"], x_of(s)
            yield 400
            bk.await_emptied(pe, "r_xT")
            for key, src, _, _ in ROPES:
                pe_features(pe, s, "g_" + key, W[key], 0, x if src == "x" else v["ctx"])
            pe_tokens(pe, s, "g_va", W["va"], 0, v["ctx"])
            pe_tokens(pe, s, "g_vt", W["vt"], 0, v["ctx"])
            yield 401
            pe.wait_ge(sem(f"g_high{s}"), len(ROPES))
            for h in range(H2):
                r, c = slice(HD2 * (h % 4), HD2 * (h % 4 + 1)), h // 4
                for t in range(NT):
                    b = bk.claim(pe, f"g_m{h}_{t}")
                    for i in range(2):
                        last = pe.matmul(b[:, i * T:(i + 1) * T], n["hl"][r, HIGH, 2 + i, c * T + t * P:c * T + (t + 1) * P],
                                         n["hl"][r, HIGH, i, c * T:(c + 1) * T], start=True, stop=True)
                    last.then_inc(bk.filled(f"g_m{h}_{t}"), 1)
            yield 402
            pe.wait_ge(sem(f"g_neg{s}"), 1)
            b = bk.claim(pe, "g_negT")
            bb = b[:, 0:P].bitcast(BF16)
            for t in range(NT):
                last = pe.transpose(bb[0:H2, t * P:(t + 1) * P], n["neg"][:, t, :], identb[:])
            last.then_inc(bk.filled("g_negT"), 1)

            def values(h):
                pe.wait_ge(sem(f"g_split{s}"), 2 * h + 2)
                for t in range(NT):
                    terms = [(k, w, x) for k in range(KT2) for w, x in ((HIGH, HIGH), (HIGH, LOW), (LOW, HIGH))]
                    for j, (k, w, x) in enumerate(terms):
                        last = pe.matmul(o[t][:, h * VW2:(h + 1) * VW2], n["p"][:, 2 * (h % 2) + w, k, t * P:(t + 1) * P],
                                         n["v"][:, x, k, h, :], start=j == 0, stop=j == len(terms) - 1)
                    if h == H2 - 1:
                        last.then_inc(bk.filled(f"g_o{t}"), 1)
                if h < H2 - 2:
                    last.then_inc(sem(f"g_weights_used{s}"), 1)

            for h in range(H2):
                yield 410 + h
                if h == 0:
                    pe.wait_ge(sem(f"g_stacked{s}"), 16 * STACKED)
                    pe.wait_ge(sem(f"g_values{s}"), 2)
                    o = [bk.claim(pe, f"g_o{t}") for t in range(NT)]
                for i in range(2):
                    b = bk.claim(pe, f"g_s{h}_{i}")
                    for j in range(NT):
                        last = pe.matmul(b[:, j * T:(j + 1) * T], n["stack"][0:STACK, i, h, j * P:(j + 1) * P],
                                         n["stack"][0:STACK, 2 + i, h, :], start=True, stop=True)
                    last.then_inc(bk.filled(f"g_s{h}_{i}"), 1)
                if h:
                    values(h - 1)
            yield 410 + H2
            values(H2 - 1)
            yield 419
            for t in range(NT):
                bk.await_emptied(pe, f"g_o{t}")
            pe_transposes(pe, s, "g_oT", n["o"])
            yield 420
            bk.await_emptied(pe, "g_oT")
            pe_tokens(pe, s, "g_out", W["go"], 0, n["oT"])
            yield 421
            pe.wait_ge(sem(f"x4_{s}"), 1)
            pe_transposes(pe, s, "g_nT", n["n"])
            yield 422
            bk.await_emptied(pe, "g_nT")
            pe_tokens(pe, s, "g_ffn", W["gf"], 0, n["nT"])

        def dve_gated(dve, s, link):
            v, bk = st[s], st[s]["bk"]
            n = v["g"]
            yield 400
            for i, (key, _, _, sin) in enumerate(ROPES):
                bk.await_emptied(dve, "g_" + key)
                rot = n["rot"][:, i % 2]
                link(dve.stream_shuffle(rot.rearrange("p c t -> p (c t)"), n["feat"][:, i % 2].rearrange("p c t -> p (c t)"),
                                        [j ^ 1 for j in range(32)]))
                link(dve.tensor_tensor(rot, rot, tables[sin][:, None, :].to_broadcast([P, NC, T]), ALU.mult))
                dve.wait_ge(sem(f"g_cos{s}"), i + 1)
                dve.tensor_tensor(n["sum"][:, i % 2], n["sum"][:, i % 2], rot, ALU.add).then_inc(sem(f"g_sum{s}"), 1)
            for i, k in enumerate(("va", "vt")):
                b = bk.await_filled(dve, "g_" + k)
                dve.tensor_tensor(n["v32"][:, 2 * i:2 * i + 2, :], b[:].rearrange("p (t d) -> p t d", t=NT),
                                  rows[k][:, None, :].to_broadcast([P, NT, D]), ALU.add).then_inc(bk.emptied("g_" + k), 1)
            yield 401
            for h in range(H2):
                for t in range(NT):
                    b = bk.await_filled(dve, f"g_m{h}_{t}")
                    dve.tensor_reduce(n["mx"][:, t, h:h + 1], b[:], axis=AX.X, op=ALU.max)\
                        .then_inc(bk.emptied(f"g_m{h}_{t}"), 1)
            for h in (H2 - 2, H2 - 1):
                for t in range(NT):
                    bk.await_emptied(dve, f"g_m{h}_{t}")
            dve.tensor_scalar(n["neg"][:], n["mx"][:], -1.0, None, ALU.mult).then_inc(sem(f"g_neg{s}"), 1)
            for h in range(H2):
                yield 410 + h
                w = n["p"][:, 2 * (h % 2):2 * (h % 2) + 2]
                bk.await_emptied(dve, f"g_s{h}_1")
                if h >= 2:
                    dve.wait_ge(sem(f"g_weights_used{s}"), h - 1)
                dve.tensor_copy(w[:, HIGH, 2:4, :], n["e"][:, 1]).then_inc(sem(f"g_high_second{s}"), 1)
                dve.wait_ge(sem(f"g_high_first{s}"), h + 1)
                dve.tensor_tensor(w[:, LOW, 0:2, :], n["e"][:, 0], w[:, HIGH, 0:2, :], ALU.subtract)\
                    .then_inc(sem(f"g_split{s}"), 1)
                dve.wait_ge(sem(f"g_high_second{s}"), h + 1)
                dve.tensor_tensor(w[:, LOW, 2:4, :], n["e"][:, 1], w[:, HIGH, 2:4, :], ALU.subtract)\
                    .then_inc(sem(f"g_split{s}"), 1)
            yield 418
            for t in range(NT):
                b = bk.await_filled(dve, f"g_o{t}")
                o = b[:, 0:H2 * VW2].rearrange("p (h w) -> p h w", w=VW2)
                link(dve.reciprocal(n["ro"][:, t, :], o[:, :, HD2]))
                dve.tensor_tensor(n["o"][:, t].rearrange("p (h d) -> p h d", h=H2), o[:, :, 0:HD2],
                                  n["ro"][:, t, :, None].to_broadcast([P, H2, HD2]), ALU.mult)\
                    .then_inc(bk.emptied(f"g_o{t}"), 1)
            yield 420
            b = bk.await_filled(dve, "g_out")
            dve.wait_ge(sem(f"res{s}"), 5)
            dve.tensor_tensor(n["u"][:].rearrange("p t d -> p (t d)"), b[:], v["res"][:].rearrange("p t d -> p (t d)"),
                              ALU.add).then_inc(bk.emptied("g_out"), 1)
            bk.await_emptied(dve, "g_out")
            dve_norm(dve, s, link, "4", n["u"], n["n"])
            yield 422
            b = bk.await_filled(dve, "g_ffn")
            dve.tensor_tensor(n["f"][:], b[:].rearrange("p (t d) -> p t d", t=NT),
                              rows["gf"][:, None, :].to_broadcast([P, NT, D]), ALU.add).then_inc(bk.emptied("g_ffn"), 1)
            bk.await_emptied(dve, "g_ffn")
            link(dve.scalar_tensor_tensor(v["y"][:], n["f"][:], 0.0, v["x"][:], ALU.max, ALU.add))
            dve_norm(dve, s, link, "5", v["y"], v["y"])

        def act_gated(act, s):
            v, bk = st[s], st[s]["bk"]
            n = v["g"]
            yield 400

            def high(i):
                act.wait_ge(sem(f"g_sum{s}"), i + 1)
                act.copy(n["hl"][:, HIGH, i], n["sum"][:, i % 2].rearrange("p c t -> p (c t)"))\
                    .then_inc(sem(f"g_high{s}"), 1)

            for i, (key, _, _, _) in enumerate(ROPES):
                b = bk.await_filled(act, "g_" + key)
                if i >= 2:
                    act.wait_ge(sem(f"g_sum{s}"), i - 1)
                for m in range(NC):
                    last = act.activation(n["feat"][:, i % 2, m, :], b[:, m * T:(m + 1) * T], ACT.Identity,
                                          bias=bias[key][:, m:m + 1])
                last.then_inc(bk.emptied("g_" + key), 1)
                if i:
                    high(i - 1)
            high(len(ROPES) - 1)
            yield 402
            b = bk.await_filled(act, "g_negT")
            act.copy(n["negT"][0:H2].rearrange("p a b -> p (a b)"), b[0:H2, 0:P].bitcast(BF16))\
                .then_inc(bk.emptied("g_negT"), 1)
            for h in range(H2):
                yield 410 + h
                for i in range(2):
                    b = bk.await_filled(act, f"g_s{h}_{i}")
                    if h:
                        act.wait_ge(sem(f"g_split{s}"), 2 * h - 1 + i)
                    act.activation(n["e"][:, i], b[:].rearrange("p (k t) -> p k t", t=T), ACT.Exp)\
                        .then_inc(bk.emptied(f"g_s{h}_{i}"), 1)
                bk.await_emptied(act, f"g_s{h}_0")
                if h >= 2:
                    act.wait_ge(sem(f"g_weights_used{s}"), h - 1)
                act.copy(n["p"][:, 2 * (h % 2) + HIGH, 0:2, :], n["e"][:, 0]).then_inc(sem(f"g_high_first{s}"), 1)
            yield 419
            b = bk.await_filled(act, "g_oT")
            act.copy(n["oT"][:].rearrange("p c t -> p (c t)"), b[:]).then_inc(bk.emptied("g_oT"), 1)
            yield 421
            b = bk.await_filled(act, "g_nT")
            for c in range(NC):
                last = act.activation(n["nT"][:, c, :], b[:, c * T:(c + 1) * T], ACT.Identity,
                                      bias=bias["beta"][:, c:c + 1], scale=bias["gamma"][:, c:c + 1])
            last.then_inc(bk.emptied("g_nT"), 1)

        def pool_gated(pool, s):
            v, bk = st[s], st[s]["bk"]
            n = v["g"]
            yield 400
            pool.wait_ge(sem(f"x3_{s}"), 1)
            pool.tensor_tensor(out=v["res"][:], in0=v["x"][:], in1=rows["go"][:, None, :].to_broadcast([P, NT, D]),
                               op=ALU.add).then_inc(sem(f"res{s}"), 1)

            def low(i):
                pool.wait_ge(sem(f"g_high{s}"), i + 1)
                pool.tensor_tensor(out=n["hl"][:, LOW, i], in0=n["sum"][:, i % 2].rearrange("p c t -> p (c t)"),
                                   in1=n["hl"][:, HIGH, i], op=ALU.subtract).then_inc(sem(f"g_low{s}"), 1)

            for i, (key, _, cos, _) in enumerate(ROPES):
                bk.await_emptied(pool, "g_" + key)
                if i >= 2:
                    pool.wait_ge(sem(f"g_low{s}"), i - 1)
                pool.tensor_tensor(out=n["sum"][:, i % 2], in0=n["feat"][:, i % 2],
                                   in1=tables[cos][:, None, :].to_broadcast([P, NC, T]), op=ALU.mult)\
                    .then_inc(sem(f"g_cos{s}"), 1)
                if i:
                    low(i - 1)
            low(len(ROPES) - 1)
            bk.await_emptied(pool, "g_va")
            bk.await_emptied(pool, "g_vt")
            v32 = n["v32"].rearrange("p k (h d) -> p k h d", h=H2)
            pool.memset(n["v"][:, HIGH, :, :, HD2], 1.0)
            pool.memset(n["v"][:, LOW, :, :, HD2], 0.0)
            pool.tensor_copy(n["v"][:, HIGH, :, :, 0:HD2], v32).then_inc(sem(f"g_values{s}"), 1)
            pool.wait_ge(sem(f"g_values{s}"), 1)
            pool.tensor_tensor(out=n["v"][:, LOW, :, :, 0:HD2], in0=v32, in1=n["v"][:, HIGH, :, :, 0:HD2],
                               op=ALU.subtract).then_inc(sem(f"g_values{s}"), 1)
            yield 420
            pool_norm(pool, s, "4")
            yield 422
            pool_norm(pool, s, "5")

        STACKED = 1 + 2 * 3 * 4 + 2

        def sp_stack(sp, s):
            n = st[s]["g"]
            done = sem(f"g_stacked{s}")
            yield 400
            sp.wait_ge(sem(f"x3_{s}"), 1)
            sp.dma_start(n["stack"][STACK - 1:STACK, 0:2].rearrange("p i h t -> p (i h t)"),
                         a["C_onesb"][0:2 * H2 * T // P, :].rearrange("(o a) b -> o (a b)", o=1)).then_inc(done, 16)
            for i, parts in ((0, (HIGH, HIGH, LOW)), (2, (HIGH, LOW, HIGH))):
                yield 400 + i / 4
                sp.wait_ge(sem(f"g_low{s}"), i + 2)
                for g in range(4):
                    for row, part in enumerate(parts):
                        heads = n["stack"][row * HD2:(row + 1) * HD2, i:i + 2].rearrange("p i (c g) t -> p i c g t", g=4)
                        sp.dma_start(heads[:, :, :, g, :], n["hl"][g * HD2:(g + 1) * HD2, part, i:i + 2, :]
                                     .rearrange("p i (c t) -> p i c t", c=NC)).then_inc(done, 16)
            yield 402
            bk = st[s]["bk"]
            bk.await_emptied(sp, "g_negT")
            for i in (2, 3):
                sp.dma_start(n["stack"][STACK - 1:STACK, i], n["negT"][0:H2].rearrange("p a b -> p (a b)")).then_inc(done, 16)

        LAYERS = (("nystrom", 0), ("dilated", 1), ("ffn", 2), ("memory", 3), ("gated", 4))[:stop]
        parts = {"pe": (pe_nystrom, pe_dilated, pe_ffn, pe_memory, pe_gated),
                 "dve": (dve_nystrom, dve_dilated, dve_ffn, dve_memory, dve_gated),
                 "act": (act_nystrom, act_dilated, act_ffn, act_memory, act_gated),
                 "pool": (pool_nystrom, pool_dilated, pool_ffn, pool_memory, pool_gated)}

        def interleaved(programs):
            due = [[0, s, g] for s, g in enumerate(programs)]
            while due:
                due.sort(key=lambda d: (d[0], d[1]))
                try:
                    stage = next(due[0][2])
                    assert stage >= due[0][0]
                    due[0][0] = stage
                except StopIteration:
                    due.pop(0)

        def chain(fns, *args):
            for f in fns[:stop]:
                yield from f(*args)

        final = "x" if stop < 5 else "y"
        key = str(stop - 1) if stop < 5 else "5"
        with nc.Fori(0, BATCH // STREAMS) as turn:
            with nc.Block() as block:
                @block.sync
                def _(sp):
                    for s in range(STREAMS):
                        v = st[s]
                        tok = (turn * STREAMS + s) * T
                        sp.dma_start(v["x"][:], a["x"][bass.ds(tok, T), :].rearrange("(t p) d -> p t d", p=P))\
                            .then_inc(sem(f"inputs{s}"), 16)
                        sp.dma_start(x_of(s), a["xT"][:, bass.ds(tok, T)].rearrange("(c p) t -> p c t", p=P))\
                            .then_inc(sem(f"inputs{s}"), 16)
                        sp.dma_start(v["ctx"][:], a["ctxT"][:, bass.ds(tok, T)].rearrange("(c p) t -> p c t", p=P))\
                            .then_inc(sem(f"inputs{s}"), 16)
                    if stop > 4:
                        interleaved([sp_stack(sp, s) for s in range(STREAMS)])
                    for s in range(STREAMS):
                        sp.wait_ge(sem(f"x{key}_{s}"), 1)
                        tok = (turn * STREAMS + s) * T
                        sp.dma_start(a["y"][bass.ds(tok, T), :].rearrange("(t p) d -> p t d", p=P), st[s][final][:])\
                            .then_inc(sem(f"stored{s}"), 16)
                    for s in range(STREAMS):
                        sp.wait_ge(sem(f"stored{s}"), 16)

                @block.tensor
                def _(pe):
                    interleaved([chain(parts["pe"], pe, s) for s in range(STREAMS)])

                @block.vector
                def _(dve):
                    links = 0
                    dve_link = sem("dve_link")

                    def link(ins):
                        nonlocal links
                        links += 1
                        ins.then_inc(dve_link, 1)
                        dve.wait_ge(dve_link, links)

                    interleaved([chain(parts["dve"], dve, s, link) for s in range(STREAMS)])

                @block.scalar
                def _(act):
                    interleaved([chain(parts["act"], act, s) for s in range(STREAMS)])

                @block.gpsimd
                def _(pool):
                    interleaved([chain(parts["pool"], pool, s) for s in range(STREAMS)])
            with nc.Block() as block:
                @block.sync
                def _(sp):
                    for x in sems.values():
                        if x.name[:4] != "load" and x.name[:5] != "setup":
                            sp.sem_clear(x)
        with nc.Block() as block:
            @block.sync
            def _(sp):
                for x in sems.values():
                    if x.name[:4] == "load" or x.name[:5] == "setup":
                        sp.sem_clear(x)


TOK = BATCH * T
TT = TOK // P
TOPK = 2
SLOTS = 256
SHIFT = 8
TILES = (TOK * TOPK + E * (SLOTS - 1)) // SLOTS
TILES += TILES % 2
ST = SLOTS // P


def experts_kernel(nc, a):
    ctx = ExitStack()
    with ctx:
        def sb(name, shape, dt=F32):
            return ctx.enter_context(nc.sbuf_tensor(name, shape, dt))

        def sem(name):
            return ctx.enter_context(nc.semaphore(name))

        I32 = mybir.dt.int32
        U32 = mybir.dt.uint32
        x = sb("m_x", [P, TT, D])
        xs = sb("m_xs", [P, TOPK, TT, D])
        xT = sb("m_xT", [P, NC, TOK])
        wg = sb("m_wg", [P, NC, E])
        bg = sb("m_bg", [P, E])
        ident = sb("m_ident", [P, P])
        tri = sb("m_tri", [P, P], BF16)
        ones = sb("m_ones", [P, P], BF16)
        eids = sb("m_eids", [P, E])
        jids = sb("m_jids", [P, TILES])
        lg = sb("m_lg", [P, TT, E])
        top = sb("m_top", [P, TT, E])
        topi = sb("m_topi", [P, TT, E], U32)
        topf = sb("m_topf", [P, TT, TOPK])
        wts = sb("m_wts", [P, TOPK, TT])
        tmp = sb("m_tmp", [P, 4, TT])
        hit = sb("m_hit", [P, TOPK, TT, E])
        sel = sb("m_sel", [P, TT, E])
        selb = sb("m_selb", [P, TT, E], BF16)
        cum = sb("m_cum", [P, 2, TT, E])
        pre = sb("m_pre", [P, TT, E])
        cnt = sb("m_cnt", [P, 8, E])
        cnti = sb("m_cnti", [P, 2, E], I32)
        posf = sb("m_posf", [P, TOPK, TT])
        posi = sb("m_posi", [P, TOPK, TT], U32)
        tile_e = sb("m_tile_e", [P, TILES, E])
        tef = sb("m_tef", [P, TILES])
        tei = sb("m_tei", [P, TILES], I32)

        bank = [ctx.enter_context(nc.psum_tensor(f"m_bank{i}", [P, 512], F32)) for i in range(8)]
        loaded, routed, step, soft = sem("m_loaded"), sem("m_routed"), sem("m_step"), sem("m_soft")
        pe_done, act_done = sem("m_pe"), sem("m_act")
        scaled, positions, sent = sem("m_scaled"), sem("m_positions"), sem("m_sent")

        loads = [(x[:], a["x5"].rearrange("(t p) d -> p t d", p=P)),
                 (wg[:], a["Wg"].rearrange("(c p) e -> p c e", p=P)), (bg[:], a["R_bg"]),
                 (ident[:], a["C_ident"]), (tri[:], a["C_tri"]), (ones[:], a["C_onesb"]),
                 (eids[:], a["C_eids"]), (jids[:], a["C_jids"])]

        with nc.Block() as block:
            @block.sync
            def _(sp):
                for dst, src in loads:
                    sp.dma_start(dst, src).then_inc(loaded, 16)

            @block.tensor
            def _(pe):
                pe.wait_ge(loaded, 16 * len(loads))
                for t in range(TT):
                    if t >= 4:
                        pe.wait_ge(act_done, t - 3)
                    for c in range(NC):
                        last = pe.transpose(bank[t % 4][:, c * P:(c + 1) * P], x[:, t, c * P:(c + 1) * P], ident[:])
                    last.then_inc(pe_done, 1)
                pe.wait_ge(act_done, TT)
                for t in range(TT):
                    for c in range(NC):
                        last = pe.matmul(bank[4][:, t * E:(t + 1) * E], xT[:, c, t * P:(t + 1) * P], wg[:, c, :],
                                         start=c == 0, stop=c == NC - 1)
                last.then_inc(pe_done, 1)
                pe.wait_ge(routed, 1)
                pe.matmul(bank[5][:, 0:TT * E], tri[:], selb[:].rearrange("p t e -> p (t e)"), start=True, stop=True)
                pe.matmul(bank[6][:, 0:TT * E], ones[:], selb[:].rearrange("p t e -> p (t e)"), start=True, stop=True)\
                    .then_inc(pe_done, 1)

            @block.scalar
            def _(act):
                for t in range(TT):
                    act.wait_ge(pe_done, t + 1)
                    act.copy(xT[:, :, t * P:(t + 1) * P], bank[t % 4][:, 0:D].rearrange("p (c t) -> p c t", c=NC))\
                        .then_inc(act_done, 1)
                act.wait_ge(soft, 1)
                act.activation(tmp[:, 1, :], tmp[:, 0, :], ACT.Exp).then_inc(soft, 1)

            @block.vector
            def _(dve):
                n = 0

                def link(ins):
                    nonlocal n
                    n += 1
                    ins.then_inc(step, 1)
                    dve.wait_ge(step, n)

                dve.wait_ge(pe_done, TT + 1)
                link(dve.tensor_tensor(lg[:], bank[4][:, 0:TT * E].rearrange("p (t e) -> p t e", e=E),
                                       bg[:, None, :].to_broadcast([P, TT, E]), ALU.add))
                for t in range(TT):
                    last = dve.max(top[:, t, :], lg[:, t, :])
                link(last)
                for t in range(TT):
                    last = dve.max_index(topi[:, t, :], top[:, t, :], lg[:, t, :])
                link(last)
                dve.tensor_tensor(tmp[:, 0, :], top[:, :, 1], top[:, :, 0], ALU.subtract).then_inc(soft, 1)
                link(dve.tensor_copy(topf[:], topi[:, :, 0:TOPK]))
                for k in range(TOPK):
                    last = dve.tensor_tensor(hit[:, k], topf[:, :, k, None].to_broadcast([P, TT, E]),
                                             eids[:, None, :].to_broadcast([P, TT, E]), ALU.is_equal)
                link(last)
                link(dve.tensor_tensor(sel[:], hit[:, 0], hit[:, 1], ALU.add))
                dve.tensor_copy(selb[:], sel[:]).then_inc(routed, 1)
                dve.wait_ge(soft, 2)
                link(dve.tensor_scalar(tmp[:, 2, :], tmp[:, 1, :], 1.0, None, ALU.add))
                link(dve.reciprocal(wts[:, 0, :], tmp[:, 2, :]))
                link(dve.tensor_tensor(wts[:, 1, :], tmp[:, 1, :], wts[:, 0, :], ALU.mult))
                for k in range(TOPK):
                    for t in range(TT):
                        last = dve.tensor_scalar(xs[:, k, t, :], x[:, t, :], wts[:, k, t:t + 1], None, ALU.mult)
                last.then_inc(scaled, 1)
                dve.wait_ge(pe_done, TT + 2)
                link(dve.tensor_copy(cum[:, 0], bank[6][:, 0:TT * E].rearrange("p (t e) -> p t e", e=E)))
                at, d = 0, 1
                while d < TT:
                    dve.tensor_copy(cum[:, 1 - at, 0:d], cum[:, at, 0:d])
                    link(dve.tensor_tensor(cum[:, 1 - at, d:TT], cum[:, at, d:TT], cum[:, at, 0:TT - d], ALU.add))
                    at, d = 1 - at, 2 * d
                total = cum[:, at, TT - 1, :]
                link(dve.tensor_tensor(pre[:], cum[:, at], bank[6][:, 0:TT * E].rearrange("p (t e) -> p t e", e=E),
                                       ALU.subtract))
                link(dve.tensor_tensor(pre[:], pre[:], bank[5][:, 0:TT * E].rearrange("p (t e) -> p t e", e=E), ALU.add))
                link(dve.tensor_scalar(cnt[:, 0, :], total, float(SLOTS - 1), None, ALU.add))
                link(dve.tensor_copy(cnti[:, 0, :], cnt[:, 0, :]))
                link(dve.tensor_scalar(cnti[:, 1, :], cnti[:, 0, :], SHIFT, None, ALU.arith_shift_right))
                link(dve.tensor_copy(cnt[:, 1, :], cnti[:, 1, :]))
                k, d = 2, 1
                link(dve.tensor_copy(cnt[:, 2, :], cnt[:, 1, :]))
                while d < E:
                    dve.tensor_copy(cnt[:, k + 1, 0:d], cnt[:, k, 0:d])
                    link(dve.tensor_tensor(cnt[:, k + 1, d:E], cnt[:, k, d:E], cnt[:, k, 0:E - d], ALU.add))
                    k, d = k + 1, 2 * d
                link(dve.tensor_tensor(cnt[:, 6, :], cnt[:, k, :], cnt[:, 1, :], ALU.subtract))
                link(dve.tensor_scalar(cnt[:, 7, :], cnt[:, 6, :], float(SLOTS), None, ALU.mult))
                link(dve.tensor_tensor(pre[:], pre[:], cnt[:, 7, None, :].to_broadcast([P, TT, E]), ALU.add))
                for j in range(TOPK):
                    last = dve.tensor_tensor(hit[:, j], hit[:, j], pre[:], ALU.mult)
                link(last)
                link(dve.tensor_reduce(posf[:].rearrange("p k t -> p (k t)"), hit[:].rearrange("p k t e -> p (k t) e"),
                                       axis=AX.X, op=ALU.add))
                link(dve.tensor_tensor(tile_e[:], jids[:, :, None].to_broadcast([P, TILES, E]),
                                       cnt[:, k, None, :].to_broadcast([P, TILES, E]), ALU.is_ge))
                link(dve.tensor_reduce(tef[:], tile_e[:], axis=AX.X, op=ALU.add))
                link(dve.tensor_scalar(tef[:], tef[:], float(E - 1), None, ALU.min))
                dve.tensor_copy(tei[:], tef[:])
                dve.tensor_copy(posi[:], posf[:]).then_inc(positions, 1)

            @block.gpsimd
            def _(pool):
                pool.wait_ge(scaled, 1)
                pool.wait_ge(positions, 1)
                for k in range(TOPK):
                    for t in range(TT):
                        pool.indirect_dma_start(out=a["slots"], out_offset=bass.IndirectOffsetOnAxis(posi[:, k, t:t + 1], 0),
                                                in_=xs[:, k, t, :], in_offset=None).then_inc(sent, 16)
                pool.wait_ge(sent, 16 * TOPK * TT)

        w1 = [sb(f"e_w1_{i}", [P, NC, HF]) for i in range(2)]
        w3 = [sb(f"e_w3_{i}", [P, NC, HF]) for i in range(2)]
        w2 = xT[:, 0, :].rearrange("p (b f d) -> p b f d", b=1, d=D), xT[:, 1, :].rearrange("p (b f d) -> p b f d", b=1, d=D)
        w2 = [w[:, 0] for w in w2]
        xe = [sb(f"e_x{i}", [P, ST, D]) for i in range(2)]
        xeT = [sb(f"e_xT{i}", [P, NC, SLOTS]) for i in range(2)]
        h = [sb(f"e_h{i}", [P, HF // P, SLOTS]) for i in range(2)]
        silu = [sb(f"e_silu{i}", [P, SLOTS]) for i in range(4)]
        yo = [sb(f"e_y{i}", [P, ST, D]) for i in range(2)]
        wl = [sem(f"e_weights{i}") for i in range(2)]
        xl = [sem(f"e_rows{i}") for i in range(2)]
        tf = [sem(f"e_turned{i}") for i in range(2)]
        te = [sem(f"e_turned_sbuf{i}") for i in range(2)]
        hf = [sem(f"e_hidden{i}") for i in range(4)]
        sd = [sem(f"e_silu{i}") for i in range(4)]
        hr = [sem(f"e_gated{i}") for i in range(4)]
        yf = [sem(f"e_answer{i}") for i in range(2)]
        ye = [sem(f"e_answer_sbuf{i}") for i in range(2)]
        ys = [sem(f"e_stored{i}") for i in range(2)]
        FE = HF // P

        with nc.Block() as block:
            @block.gpsimd
            def _(pool):
                for i in range(2):
                    pool.memset(yo[i][:], 0.0).then_inc(yf[i], 1)
                    pool.memset(xeT[i][:], 0.0).then_inc(te[i], 1)
                    pool.memset(h[i][:, 0, 0:2], 0.0).then_inc(ye[i], 1)
                    pool.memset(h[i][:, 1, 0:2], 0.0).then_inc(ys[i], 16)
                for i in range(4):
                    pool.memset(silu[i][:], 0.0).then_inc(hr[i], 1)

        with nc.Block() as block:
            @block.sync
            def _(sp):
                with sp.Fori(0, TILES // 2) as i:
                    for u in range(2):
                        j = i * 2 + u
                        expert = sp.value_load(tei[0:1, bass.ds(j, 1)], min_val=0, max_val=E - 1)
                        sp.wait_ge(te[u], i + 1)
                        sp.dma_start(xe[u][:], a["slots"][bass.ds(j * SLOTS, SLOTS), :].rearrange("(t p) d -> p t d", p=P))\
                            .then_inc(xl[u], 16)
                        sp.wait_ge(yf[u], i + 1)
                        for dst, src in ((w1[u], a["E1"]), (w3[u], a["E3"]), (w2[u], a["E2"])):
                            sp.dma_start(dst[:], src[bass.ds(expert, 1)].rearrange("o (c p) n -> p (o c) n", p=P))\
                                .then_inc(wl[u], 16)

            @block.tensor
            def _(pe):
                with pe.Fori(0, TILES // 2) as i:
                    for u in range(2):
                        pe.wait_ge(xl[u], i * 16 + 16)
                        pe.wait_ge(te[u], i + 1)
                        for c in range(NC):
                            for t in range(ST):
                                last = pe.transpose(bank[4 + u][:, c * SLOTS + t * P:c * SLOTS + (t + 1) * P],
                                                    xe[u][:, t, c * P:(c + 1) * P], ident[:])
                        last.then_inc(tf[u], 1)
                    for u in range(2):
                        pe.wait_ge(te[u], i + 2)
                        pe.wait_ge(wl[u], i * 48 + 48)
                        for f in range(FE):
                            b = f % 4
                            pe.wait_ge(hr[b], i * 4 + 2 * u + f // 4 + 1)
                            for col, w in ((0, w1[u]), (SLOTS, w3[u])):
                                for c in range(NC):
                                    last = pe.matmul(bank[b][:, col:col + SLOTS], w[:, c, f * P:(f + 1) * P], xeT[u][:, c, :],
                                                     start=c == 0, stop=c == NC - 1)
                            last.then_inc(hf[b], 1)
                    for u in range(2):
                        pe.wait_ge(ye[u], i + 1)
                        for b in range(4):
                            pe.wait_ge(hr[b], i * 4 + 2 * u + 3)
                        for t in range(ST):
                            for f in range(FE):
                                last = pe.matmul(bank[6 + u][:, t * D:(t + 1) * D], h[u][:, f, t * P:(t + 1) * P],
                                                 w2[u][:, f, :], start=f == 0, stop=f == FE - 1)
                        last.then_inc(yf[u], 1)

            @block.scalar
            def _(act):
                with act.Fori(0, TILES // 2) as i:
                    for u in range(2):
                        act.wait_ge(tf[u], i + 1)
                        act.copy(xeT[u][:].rearrange("p c s -> p (c s)"), bank[4 + u][:]).then_inc(te[u], 1)
                    for u in range(2):
                        for f in range(FE):
                            b = f % 4
                            act.wait_ge(hf[b], i * 4 + 2 * u + f // 4 + 1)
                            act.activation(silu[b][:], bank[b][:, 0:SLOTS], ACT.Silu).then_inc(sd[b], 1)
                    for u in range(2):
                        act.wait_ge(yf[u], i + 2)
                        act.wait_ge(ys[u], i * 16 + 16)
                        act.copy(yo[u][:].rearrange("p t d -> p (t d)"), bank[6 + u][:]).then_inc(ye[u], 1)
                        act.wait_ge(ye[u], i + 2)
                        act.dma_start(a["back"][bass.ds((i * 2 + u) * SLOTS, SLOTS), :].rearrange("(t p) d -> p t d", p=P),
                                      yo[u][:]).then_inc(ys[u], 16)
                for u in range(2):
                    act.wait_ge(ys[u], 16 * (TILES // 2) + 16)

            @block.vector
            def _(dve):
                with dve.Fori(0, TILES // 2) as i:
                    for u in range(2):
                        for f in range(FE):
                            b = f % 4
                            dve.wait_ge(sd[b], i * 4 + 2 * u + f // 4 + 1)
                            dve.tensor_tensor(h[u][:, f, :], bank[b][:, SLOTS:2 * SLOTS], silu[b][:], ALU.mult)\
                                .then_inc(hr[b], 1)

        fetched, summed, normed = sem("m_fetched"), sem("m_summed"), sem("m_normed")
        halved = sem("m_half")
        vend, ready, out_done = sem("m_variance"), sem("m_rstd"), sem("m_out")
        stt, mv, ve, rstd, half = (sb("m_st", [P, TT, 6]), sb("m_mv", [P, TT, 2]), sb("m_ve", [P, TT]),
                                   sb("m_rstd", [P, TT]), sb("m_halves", [P, TT]))
        with nc.Block() as block:
            @block.gpsimd
            def _(pool):
                pool.memset(half[:], -0.5).then_inc(halved, 1)
                for t in range(TT):
                    for k in range(TOPK):
                        pool.indirect_dma_start(out=xs[:, k, t, :], out_offset=None, in_=a["back"],
                                                in_offset=bass.IndirectOffsetOnAxis(posi[:, k, t:t + 1], 0))\
                            .then_inc(fetched, 16)
                pool.wait_ge(halved, 1)
                pool.wait_ge(vend, 1)
                pool.tensor_tensor(out=rstd[:], in0=ve[:], in1=half[:], op=ALU.pow).then_inc(ready, 1)

            @block.vector
            def _(dve):
                dve.wait_ge(fetched, 16 * TOPK * TT)
                dve.tensor_tensor(xs[:, 0], xs[:, 0], xs[:, 1], ALU.add).then_inc(summed, 1)
                dve.wait_ge(summed, 1)
                for t in range(TT):
                    last = dve.scalar_tensor_tensor(xs[:, 0, t, :], x[:, t, :], 2.0, xs[:, 0, t, :], ALU.mult, ALU.add)
                last.then_inc(summed, 1)
                dve.wait_ge(summed, 2)
                for t in range(TT):
                    last = dve.bn_stats(stt[:, t, :], xs[:, 0, t, :])
                last.then_inc(summed, 1)
                dve.wait_ge(summed, 3)
                for t in range(TT):
                    last = dve.bn_aggr(mv[:, t, :], stt[:, t, :])
                last.then_inc(summed, 1)
                dve.wait_ge(summed, 4)
                dve.tensor_scalar(ve[:], mv[:, :, 1], EPS, None, ALU.add).then_inc(vend, 1)
                dve.wait_ge(ready, 1)
                for t in range(TT):
                    dve.tensor_scalar(xs[:, 0, t, :], xs[:, 0, t, :], mv[:, t, 0:1], rstd[:, t:t + 1],
                                      ALU.subtract, ALU.mult).then_inc(normed, 1)

            @block.sync
            def _(sp):
                q = TT // 4
                for i in range(4):
                    sp.wait_ge(normed, (i + 1) * q)
                    sp.dma_start(a["y"][i * q * P:(i + 1) * q * P, :].rearrange("(t p) d -> p t d", p=P),
                                 xs[:, 0, i * q:(i + 1) * q, :]).then_inc(out_done, 16)
                sp.wait_ge(out_done, 64)


def clear_slots(nc, a):
    with (nc.sbuf_tensor("zeros", [P, D], F32) as zeros, nc.semaphore("zeros_made") as made,
          nc.semaphore("slots_cleared") as cleared):
        with nc.Block() as block:
            @block.gpsimd
            def _(pool):
                pool.memset(zeros[:], 0.0).then_inc(made, 1)

            @block.sync
            def _(sp):
                sp.wait_ge(made, 1)
                n = TILES * SLOTS // P
                sp.dma_start(a["slots"].rearrange("(n p) d -> p n d", p=P), zeros[:, None, :].to_broadcast([P, n, D]))\
                    .then_inc(cleared, 16)
                sp.wait_ge(cleared, 16)
        with nc.Block() as block:
            @block.sync
            def _(sp):
                sp.sem_clear(made)
                sp.sem_clear(cleared)


def lay_out(i):
    f = lambda n: np.asarray(i[n])
    e = 3
    cols = lambda b: np.ascontiguousarray(b.reshape(-1, P).T)
    rep = lambda b: np.ascontiguousarray(np.broadcast_to(b.reshape(1, -1), (P, b.size)))
    a = {}
    x, c = f("x").reshape(-1, D), f("ctx_1024").reshape(-1, D)
    a["x"], a["xT"], a["ctxT"] = x, x.T, c.T
    g = lambda n: f("L1_xattn_" + n)[e]
    a["W_qkv"], a["W_out"] = f("L0_attn_Wqkv"), f("L0_attn_Wout")
    for n in "qkvo":
        a["W_d" + n] = f("L0_xattn_W" + n).T
    a["W_ff1"], a["W_ff2"] = f("L0_ffn_W1").T, f("L0_ffn_W2").T
    a["W_mw"], a["W_mr"] = f("L1_attn_W_write").T, f("L1_attn_W_read").T
    for n in ("qa", "ka", "qt", "kt"):
        a["W_" + n], a["B_" + n] = g("W_" + n).T, cols(g("b_" + n))
    a["W_va"], a["W_vt"], a["W_go"], a["W_gf"] = g("W_va").T, g("W_vt").T, g("W_o").T, g("W_ffn").T
    bq = f("L0_attn_bqkv")
    a["B_q0"], a["B_k0"], a["R_v0"] = cols(bq[:D]), cols(bq[D:2 * D]), rep(bq[2 * D:])
    a["R_o0"] = rep(f("L0_attn_bout"))
    a["B_dq"], a["B_dk"], a["R_dv"], a["R_do"] = (cols(f("L0_xattn_bq")), cols(f("L0_xattn_bk")),
                                                  rep(f("L0_xattn_bv")), rep(f("L0_xattn_bo")))
    a["B_ff1"], a["R_ff2"] = cols(f("L0_ffn_b1")), rep(f("L0_ffn_b2"))
    a["B_decay"], a["B_alpha"] = rep(f("L1_attn_decay")), rep(f("L1_attn_log_alpha"))
    a["R_va"], a["R_vt"], a["R_go"], a["R_gf"] = rep(g("b_va")), rep(g("b_vt")), rep(g("b_o")), rep(g("b_ffn"))
    a["B_gamma"], a["B_beta"] = cols(g("gamma")), cols(g("beta"))
    a["B_gate"] = rep(f("L1_xattn_gating_factor")[e:e + 1])
    a["Wg"], a["R_bg"] = f("L1_ffn_Wg"), rep(f("L1_ffn_bg"))
    a["E1"], a["E2"], a["E3"] = f("L1_ffn_W1"), f("L1_ffn_W2"), f("L1_ffn_W3")
    for n, t in shape_constants().items():
        a["C_" + n] = t
    return {n: np.ascontiguousarray(t) for n, t in a.items()}


def build(nc, a, y):
    tokens = nc.dram_tensor("tokens", (TOK, D), F32, kind="Internal").ap()
    slots = nc.dram_tensor("slots", (TILES * SLOTS, D), F32, kind="Internal").ap()
    back = nc.dram_tensor("back", (TILES * SLOTS, D), F32, kind="Internal").ap()
    clear_slots(nc, {"slots": slots})
    layers_kernel(nc, {**a, "y": tokens}, 5)
    experts_kernel(nc, {**a, "x5": tokens, "slots": slots, "back": back, "y": y})


def kernel(**inputs):
    import concourse.bacc as _bacc
    from concourse.bass_utils import run_bass_kernel_spmd as _run

    nc = _bacc.Bacc("TRN2", target_bir_lowering=False, num_devices=1)
    arrays = lay_out(inputs)
    args = {n: nc.dram_tensor(n, t.shape, mybir.dt.from_np(t.dtype), kind="ExternalInput").ap()
            for n, t in arrays.items()}
    y = nc.dram_tensor("y_out", (TOK, D), F32, kind="ExternalOutput").ap()
    build(nc, args, y)
    r = _run(nc, [arrays], core_ids=[0])
    return r.results[0]["y_out"].reshape(BATCH, T, D)
```

```python
import numpy as np
import concourse.bass as bass
from concourse import mybir
from concourse.alu_op_type import AluOpType as ALU
from contextlib import ExitStack

F32 = mybir.dt.float32
BF16 = mybir.dt.bfloat16
ACT = mybir.ActivationFunctionType
AX = mybir.AxisListType

P = 128
BATCH = 8
T = 256
D = 256
NT = T // P
NC = D // P
STREAMS = 2
EPS = 1e-5

H0 = 16
DH0 = D // H0
HC = P // DH0
M = 64
LM = T // M
PAIRS = H0 // 2
PINV_ITERS = 6
BR = 3
VW = DH0 + 1
BIG = -1e30
TINY = 2.0 ** -63
SMALLEST = 2.0 ** -100
FF = 4 * D
FC = FF // P
H1 = 4
HD1 = D // H1
H2 = 8
HD2 = D // H2
VW2 = HD2 + 1
KT2 = 2 * T // P
E = 8
HF = 1024


class BankTurns:

    def __init__(self, tensors, filled, emptied, order):
        self.turn = {}
        count = [0] * len(tensors)
        for name, b in order:
            count[b] += 1
            assert name not in self.turn, name
            self.turn[name] = (tensors[b], filled[b], emptied[b], count[b])

    def claim(self, pe, name):
        tensor, _, emptied, k = self.turn[name]
        if k > 1:
            pe.wait_ge(emptied, k - 1)
        return tensor

    def await_filled(self, eng, name):
        tensor, filled, _, k = self.turn[name]
        eng.wait_ge(filled, k)
        return tensor

    await_done = await_filled

    def await_emptied(self, eng, name):
        _, _, emptied, k = self.turn[name]
        eng.wait_ge(emptied, k)

    def filled(self, name):
        return self.turn[name][1]

    def emptied(self, name):
        return self.turn[name][2]


def bank_order():
    o = [("n_q", 0), ("n_k", 1), ("n_v", 2)]
    o += [("n_sim2", 3)]
    o += [(f"n_max1_{t}{c}", (0, 1, 2, 3)[2 * t + c]) for t in range(NT) for c in range(NC)]
    o += [(f"n_max3_{i}", i) for i in range(4)]
    o += [("n_negT", 0)]
    o += [(f"n_s1_{i}", (1, 2, 3, 0)[i]) for i in range(4)]
    o += [(f"n_s3_{t}{c}", (1, 2, 3, 0)[2 * t + c]) for t in range(NT) for c in range(NC)]
    o += [("n_aT_0", 1), ("n_aT_1", 2), ("n_y", 3)]
    for g in range(2):
        o += [(f"n_k0_{g}", g), (f"n_kT0_{g}", 2 + g)]
    for i in range(PINV_ITERS - 1):
        for g in range(2):
            o += [(f"n_p{i}_{g}", g)]
        for g in range(2):
            o += [(f"n_t{i}_{g}", 2 + g)]
        for g in range(2):
            o += [(f"n_kT{i + 1}_{g}", 2 + g), (f"n_k{i + 1}_{g}", g)]
    for j in range(4):
        o += [(f"n_w{j}", 2 + j % 2)]
    o += [(f"n_o{t}", t) for t in range(NT)]
    o += [("n_oT", 2), ("n_out", 3), ("n_xT", 0)]
    o += [("d_q", 1), ("d_k", 2), ("d_v", 3)]
    for c in range(NC):
        o += [(f"d_m{c}_{i}", i % 3 + 1) for i in range(6)]
        o += [(f"d_negT{c}", 0)]
        o += [(f"d_s{c}_{i}", i % 3 + 1) for i in range(6)]
        o += [(f"d_o{c}_{t}", (0, 1)[t]) for t in range(NT)]
    o += [("d_oT", 2), ("d_out", 3), ("d_xT", 0)]
    o += [(f"f_h{i}", (1, 2, 3, 0)[i]) for i in range(FC // 2)]
    o += [("f_out", 1), ("f_xT", 2)]
    o += [("r_v", 3), ("r_s0", 0), ("r_s1", 1), ("r_s2", 2), ("r_s3", 3), ("r_r", 2),
          ("r_out", 0), ("r_xT", 1)]
    o += [("g_ka", 2), ("g_kt", 3), ("g_qa", 0), ("g_qt", 1)]
    o += [("g_va", 2), ("g_vt", 3)]
    o += [(f"g_m{h}_{t}", 2 * (h % 2) + t) for h in range(H2) for t in range(NT)]
    o += [("g_negT", 0)]
    o += [(f"g_o{t}", t) for t in range(NT)]
    o += [(f"g_s{h}_{i}", 2 + i) for h in range(H2) for i in range(2)]
    o += [("g_oT", 2), ("g_out", 3), ("g_nT", 0), ("g_ffn", 1), ("g_xT", 2)]
    return o


def words(kind, shape):
    n = int(np.prod(shape))
    n = n if kind == F32 else (n + 1) // 2
    return n + n % 2


def words_before(table, name):
    names = list(table)
    return words_of({n: table[n] for n in names[:names.index(name)]})


def words_of(table):
    return sum(words(kind, shape) for kind, *shape in table.values())


def carve(arena, sizes):
    at, out = 0, {}
    for name, (kind, *shape) in sizes.items():
        n = int(np.prod(shape))
        w = words(kind, shape)
        v = arena[:, at:at + w]
        if kind == BF16:
            v = v.bitcast(BF16)
        v = v[:, 0:n]
        if len(shape) == 2:
            v = v.rearrange("p (a b) -> p a b", a=shape[0])
        if len(shape) == 3:
            v = v.rearrange("p (a b c) -> p a b c", a=shape[0], b=shape[1])
        if len(shape) == 4:
            v = v.rearrange("p (a b c d) -> p a b c d", a=shape[0], b=shape[1], c=shape[2])
        out[name] = v
        at += w
    return out, at


NYSTROM = {
    "q": (F32, NC, T), "k": (F32, NC, T), "qb": (BF16, NC, T), "kb": (BF16, NC, T),
    "v": (BF16, 2 * NT, H0, VW), "qs": (F32, NC, M), "ks": (F32, NC, M), "kl": (F32, NC, M),
    "qlm": (F32, NC, HC, M), "klm": (F32, NC, HC, M), "qlmb": (BF16, NC, HC, M), "klmb": (BF16, NC, HC, M),
    "mx1": (F32, NT, H0), "mx3": (F32, PAIRS), "mx2": (F32, PAIRS), "sum2": (F32, PAIRS), "rs2": (F32, PAIRS),
    "neg": (BF16, 3, P), "negT": (BF16, 3, P),
    "a": (F32, PAIRS, M), "ry": (F32, PAIRS), "z2": (F32, PAIRS, DH0), "g": (BF16, 2, PAIRS, 2 * VW),
    "ro": (F32, NT, H0), "e": (F32, 2, 2 * T),
    "e1": (BF16, 2, PAIRS, T), "e3": (BF16, 2 * NT, NC, HC * M),
}
HIGH, LOW = 0, 1
TERMS = ((HIGH, HIGH), (HIGH, LOW), (LOW, HIGH))
DIAGONAL = (F32, PAIRS, P)
PINV = {
    "q": {"aT": DIAGONAL}, "qb": {"t1": (F32, PAIRS, M)}, "v": {"kz": (F32, PAIRS, M + DH0)},
    "qlm": {"t3": DIAGONAL}, "klm": {"kk": DIAGONAL}, "qlmb": {"ad": DIAGONAL},
    "e3": {"kkT": DIAGONAL, "t2": DIAGONAL}, "e": {"v32": (F32, NT, D)},
}
DILATED = {
    "q": (F32, NC, T), "k": (F32, NC, T), "kb": (BF16, NC, T), "v": (BF16, 2 * NT, H0, BR * VW),
    "kl": (BF16, NC, T), "ql": (BF16, NC, T), "qh": (BF16, NC, T), "qml": (BF16, HC, T), "qmb": (BF16, HC, T), "p0": (BF16, 2, HC, T), "p1": (BF16, 2, HC, P), "e": (F32, 2, 2 * T),
    "mx": (F32, NT, H0), "neg": (BF16, NT, P), "negT": (BF16, NT, P),
    "s": (F32, NT, H0, BR), "ls": (F32, NT, H0, BR), "isz": (F32, NT, H0, BR), "w": (F32, NT, H0, BR),
    "rc": (F32, NT, H0, BR), "lm": (F32, NT, H0), "rz": (F32, NT, H0),
    "n": (F32, NT, H0, BR, VW),
}
DILATED_UNDER = {"e": {"v32": (F32, NT, D)}}
FFN = {"h": (F32, FC, T)}
MEMORY = {"v": (F32, NT, D), "s0": (F32, H1, T), "s1": (F32, H1, P), "r": (F32, NC, T)}
GATED = {
    "hl": (BF16, 2, 4, NC * T), "rot": (F32, 2, NC, T),
    "stack": (BF16, 4, H2, T),
    "p": (BF16, 4, KT2, T), "e": (F32, 2, 2, T), "v": (BF16, 2, KT2, H2, VW2),
    "mx": (F32, NT, H2), "neg": (BF16, NT, H2), "negT": (BF16, NT, P), "ro": (F32, NT, H2),
}
GATED_UNDER = {
    "p": {"feat": (F32, 2, NC, T), "sum": (F32, 2, NC, T)}, "e": {"v32": (F32, KT2, D)},
    "hl": {"o": (F32, NT, D), "oT": (F32, NC, T), "u": (F32, NT, D), "n": (F32, NT, D)},
    "rot": {"nT": (F32, NC, T), "f": (F32, NT, D)},
}
STACK = 3 * HD2 + 1

MATRICES = {"qkv": 3 * D, "out": D, "dq": D, "dk": D, "dv": D, "do": D, "ff1": FF, "mw": D, "mr": D,
            "qa": D, "ka": D, "va": D, "qt": D, "kt": D, "vt": D,
            "go": D, "gf": D}
COLUMNS = {"q0": NC, "k0": NC, "dq": NC, "dk": NC, "ff1": FC, "decay": H1, "alpha": H1,
           "qa": NC, "ka": NC, "qt": NC, "kt": NC,
           "gamma": NC, "beta": NC, "gate": 1}
ROWS = ("v0", "o0", "dv", "do", "ff2", "va", "vt", "go", "gf")


ROUTING = ("tri", "onesb", "eids", "jids")
EARLY = ("exponents", "keep", "ones")
GROUPS = {"nystrom": ("qkv", "out"), "rest": tuple(n for n in MATRICES if n not in ("qkv", "out", "ff1"))}


def constant_groups(tables):
    late = [n for n in tables if n not in EARLY + ROUTING]
    return {"early": list(EARLY), "fp32": [n for n in late if tables[n].dtype == np.float32],
            "bf16": [n for n in late if tables[n].dtype != np.float32]}


def shape_constants():

    bf = np.dtype("bfloat16")
    p = np.arange(P)
    c = {"ident": np.eye(P, dtype=np.float32), "identb": np.eye(P).astype(bf)}
    mask = (p[:, None] // DH0 == np.arange(HC)[None]).astype(np.float32)
    c["hmask"] = np.concatenate([mask, mask / LM], 1)
    c["halves"] = (p[:, None] // M == np.arange(2)[None]).astype(np.float32)
    c["ones"] = np.ones((P, P), np.float32)
    c["eye"] = np.tile(np.eye(M, dtype=np.float32), (2, 1))
    c["eye325"] = 3.25 * np.eye(P, dtype=np.float32)
    selp = np.zeros((P, PAIRS, P), np.float32)
    sel16 = np.zeros((P, H0, P), np.float32)
    for h in range(H0):
        selp[h, h // 2, (h % 2) * M:(h % 2 + 1) * M] = 1
        sel16[h, h, :] = 1
    c["selp"], c["sel16"] = (x.reshape(P, -1).astype(bf) for x in (selp, sel16))
    c["above"] = np.where(p[:, None] < p[None], BIG, 0.0).astype(bf)
    c["below"] = np.where(p[:, None] > p[None], BIG, 0.0).astype(bf)
    heads = np.arange(H0)
    on = np.stack([np.ones((P, H0)), p[:, None] % 2 == heads // 8, p[:, None] % 4 == heads // 4], 2)
    c["valid"] = on.reshape(P, -1).astype(np.float32)
    freq = (1.0 / 10000.0 ** (np.arange(0, HD2, 2, dtype=np.float32) / np.float32(HD2))).astype(np.float32)
    ang = np.arange(T, dtype=np.float32)[None] * freq[(p % HD2) % (HD2 // 2)][:, None]
    sign = np.where(p % 2 == 0, -1.0, 1.0).astype(np.float32)[:, None]
    c["tri"] = (p[:, None] < p[None]).astype(bf)
    c["onesb"] = np.ones((P, P)).astype(bf)
    c["eids"] = np.tile(np.arange(E, dtype=np.float32), (P, 1))
    c["jids"] = np.tile(np.arange(TILES, dtype=np.float32), (P, 1))
    c["cosk"], c["sink"] = np.cos(ang).astype(np.float32), (np.sin(ang) * sign).astype(np.float32)
    r = np.float32(1.0 / np.sqrt(HD2))
    c["cosq"], c["sinq"] = c["cosk"] * r, c["sink"] * r
    t = np.arange(T)
    c["exponents"] = np.maximum(t[None] - 1 - p[:, None], 0).astype(np.float32)
    c["keep"] = (t[None] > p[:, None]).astype(np.float32)
    return c


def layers_kernel(nc, a, stop):
    ctx = ExitStack()
    with ctx:
        def sb(name, shape, dt=F32):
            return ctx.enter_context(nc.sbuf_tensor(name, shape, dt))

        sems = {}

        def sem(name):
            if name not in sems:
                sems[name] = ctx.enter_context(nc.semaphore(name))
            return sems[name]

        def side_by_side(name, widths, kind=F32, rows=1, room=None):
            total = sum(widths.values())
            whole = sb(name, [P, rows, total], kind) if room is None else room[:, None, 0:total]
            at, views = 0, {}
            for n, w in widths.items():
                views[n] = whole[:, :, at:at + w] if rows > 1 else whole[:, 0, at:at + w]
                at += w
            return whole, views

        W, whole_W = {"ff1": sb("w_ff1", [P, NC, FF])}, {}
        for group, names in GROUPS.items():
            whole_W[group], views = side_by_side("w_" + group, {n: MATRICES[n] for n in names}, rows=NC)
            W.update(views)
        w2 = sb("w_ff2", [P, FC, D])
        whole_bias, bias = side_by_side("biases", COLUMNS)
        whole_rows, rows = side_by_side("rows", {n: D for n in ROWS})
        width = max(words_of(table) for table in (NYSTROM, DILATED, FFN, MEMORY, GATED))
        arenas = [sb(f"arena{s}", [P, width]) for s in range(STREAMS)]
        scratch = arenas[0][:, 0:1024]
        tables_of_shapes = shape_constants()
        whole_consts, consts = {}, {}
        for group, names in constant_groups(tables_of_shapes).items():
            whole_consts[group], views = side_by_side("c_" + group, {n: tables_of_shapes[n].shape[1] for n in names},
                                                      BF16 if group == "bf16" else F32,
                                                      room=arenas[0][:, 1024:] if group == "early" else None)
            consts.update(views)
        ident, identb, exponents, keep = (consts[n] for n in ("ident", "identb", "exponents", "keep"))
        hmask = consts["hmask"]
        selp = consts["selp"][:].rearrange("p (a b) -> p a b", b=P)
        sel16 = consts["sel16"][:].rearrange("p (a b) -> p a b", b=P)
        cosg = sb("cosg", [P, T])
        sing = sb("sing", [P, T])
        dec0 = sb("dec0", [P, H1, T])
        dec1 = sb("dec1", [P, H1, P])
        small = sb("small", [P, 64])
        zeros = sb("zeros", [P, D])
        e_whole = sb("e_whole", [P, 2, 512])
        e_parts = sb("e_parts", [P, 2, 2, 512], BF16)

        st = []
        psum = [ctx.enter_context(nc.psum_tensor(f"bank{i}", [P, 512], F32)) for i in range(8)]
        for s in range(STREAMS):
            arena = arenas[s]
            v = {"x": sb(f"x{s}", [P, NT, D]), "y": sb(f"y{s}", [P, NT, D]), "res": sb(f"res{s}", [P, NT, D]),
                 "xz": sb(f"xz{s}", [P, NC, T + 1]), "ctx": sb(f"ctx{s}", [P, NC, T]),
                 "st": sb(f"st{s}", [P, NT, 6]), "mv": sb(f"mv{s}", [P, NT, 2]),
                 "ve": sb(f"ve{s}", [P, NT]), "rstd": sb(f"rstd{s}", [P, NT])}
            for key, table in (("n", NYSTROM), ("d", DILATED), ("f", FFN), ("r", MEMORY), ("g", GATED)):
                v[key], _ = carve(arena[:], table)
            for under, table in PINV.items():
                v["n"].update(carve(arena[:, words_before(NYSTROM, under):], table)[0])
            for under, table in DILATED_UNDER.items():
                v["d"].update(carve(arena[:, words_before(DILATED, under):], table)[0])
            for under, table in GATED_UNDER.items():
                v["g"].update(carve(arena[:, words_before(GATED, under):], table)[0])
            v["n"]["z"] = v["n"]["kz"][:, :, M:M + DH0]
            for key in "nd":
                v[key]["o"], v[key]["oT"] = v[key]["q"], v[key]["k"]
            v["bk"] = BankTurns([psum[4 * s + i] for i in range(4)],
                            [sem(f"bank_filled{s}_{i}") for i in range(4)],
                            [sem(f"bank_emptied{s}_{i}") for i in range(4)], bank_order())
            st.append(v)

        NEGH = sb("neghalf", [P, NT])

        with nc.Block() as block:
            loaded = {n: sem("load_" + n) for n in ("ternary", "tables", "act", "nystrom", "rest")}
            columns_of = lambda n: a["W_" + n].rearrange("(c p) n -> p c n", p=P)
            order = [(W["ff1"][:], columns_of("ff1"), "ternary"), (w2[:], columns_of("ff2"), "ternary")]
            order += [(whole_W[n][:], columns_of(n), n) for n in GROUPS]
            early = [(whole_bias[:, 0], a["B"]), (whole_consts["early"][:, 0], a["C_early"])]
            order2 = [(whole_consts[n][:, 0], a["C_" + n]) for n in ("fp32", "bf16")] + [(whole_rows[:, 0], a["R"])]
            n_act = 16 * len(order2)
            step = sem("setup_dve")
            act_step = sem("setup_act")
            pool_step = sem("setup_pool")
            pe_step = sem("setup_pe")

            @block.sync
            def _(sp):
                for dst, src, group in order:
                    sp.dma_start(dst, src).then_inc(loaded[group], 16)

            @block.gpsimd
            def _(pool):
                for s in range(STREAMS):
                    pool.memset(st[s]["xz"][:], 0.0)
                pool.memset(NEGH[:], -0.5)
                pool.memset(zeros[:], 0.0)
                pool.memset(small[:, 63:64], 1.0 / (FF * D)).then_inc(pool_step, 1)

            @block.scalar
            def _(act):
                for dst, src in early:
                    act.dma_start(dst, src).then_inc(loaded["tables"], 16)
                for dst, src in order2:
                    act.dma_start(dst, src).then_inc(loaded["act"], 16)
                act.wait_ge(loaded["tables"], 16 * len(early))
                act.activation(small[:, 0:4], bias["decay"][:], ACT.Exp, scale=-1.0).then_inc(act_step, 1)
                act.wait_ge(act_step, 1)
                act.activation(small[:, 4:8], small[:, 0:4], ACT.Ln, bias=1.0).then_inc(act_step, 1)
                act.wait_ge(step, 1)
                for h in range(H1):
                    act.activation(dec0[:, h, :], exponents, ACT.Exp, bias=bias["alpha"][:, h:h + 1],
                                   scale=small[:, 8 + h:9 + h])
                    act.activation(dec1[:, h, :], exponents[:, 0:P], ACT.Exp, bias=bias["alpha"][:, h:h + 1],
                                   scale=small[:, 8 + h:9 + h]).then_inc(act_step, 1)
                act.activation(small[:, 12:13], bias["gate"][:], ACT.Exp, scale=-1.0).then_inc(act_step, 1)
                act.wait_ge(loaded["act"], n_act)

            @block.vector
            def _(dve):
                n = 0

                def link(ins):
                    nonlocal n
                    n += 1
                    ins.then_inc(step, 1)
                    dve.wait_ge(step, n)

                dve.wait_ge(act_step, 2)
                link(dve.tensor_scalar(small[:, 8:12], small[:, 4:8], -1.0, None, ALU.mult))
                dve.wait_ge(loaded["ternary"], 32)
                for i, w in enumerate((W["ff1"], w2)):
                    flat = w[:].rearrange("p c n -> p (c n)")
                    link(dve.tensor_reduce(small[:, 16 + i:17 + i], flat, axis=AX.X, op=ALU.add,
                                           apply_absolute_value=True))
                dve.wait_ge(pe_step, 1)
                for i, w in enumerate((W["ff1"], w2)):
                    flat = w[:].rearrange("p c n -> p (c n)")
                    c = small[:, 20 + 4 * i:24 + 4 * i]
                    link(dve.tensor_scalar(c[:, 0:1], psum[0][:, i:i + 1], small[:, 63:64], 1e-8, ALU.mult, ALU.max))
                    link(dve.reciprocal(c[:, 1:2], c[:, 0:1]))
                    for half in range(2):
                        f = flat[:, half * 1024:(half + 1) * 1024]
                        link(dve.tensor_scalar(f, f, c[:, 1:2], None, ALU.mult))
                        link(dve.tensor_scalar(scratch, f, -0.5, -1.0, ALU.is_lt, ALU.mult))
                        link(dve.scalar_tensor_tensor(f, f, 0.5, scratch, ALU.is_gt, ALU.add))
                dve.wait_ge(act_step, 2 + H1)
                link(dve.tensor_tensor(dec0[:], dec0[:], keep[:, None, :].to_broadcast([P, H1, T]), ALU.mult))
                link(dve.tensor_tensor(dec1[:], dec1[:], keep[:, None, 0:P].to_broadcast([P, H1, P]), ALU.mult))
                dve.wait_ge(act_step, 3 + H1)
                link(dve.tensor_scalar(small[:, 13:14], small[:, 12:13], 1.0, None, ALU.add))
                link(dve.reciprocal(small[:, 14:15], small[:, 13:14]))
                dve.wait_ge(loaded["act"], n_act)
                link(dve.tensor_scalar(cosg[:], consts["cosq"][:], small[:, 14:15], None, ALU.mult))
                link(dve.tensor_scalar(sing[:], consts["sinq"][:], small[:, 14:15], None, ALU.mult))

            @block.tensor
            def _(pe):
                pe.wait_ge(loaded["tables"], 16 * len(early))
                pe.wait_ge(pool_step, 1)
                pe.wait_ge(step, 3)
                pe.matmul(psum[0][:, 0:2], consts["ones"][:], small[:, 16:18], start=True, stop=True).then_inc(pe_step, 1)

        def transposed(x, t, c):
            return x[:, t, c * P:(c + 1) * P]

        x_of = lambda s: st[s]["xz"][:, :, 1:T + 1]

        def pe_transposes(pe, s, name, src):
            b = st[s]["bk"].claim(pe, name)
            for c in range(NC):
                for t in range(NT):
                    last = pe.transpose(b[:, c * T + t * P:c * T + (t + 1) * P], transposed(src, t, c), ident[:])
            last.then_inc(st[s]["bk"].filled(name), 1)

        def pe_features(pe, s, name, w, col, x):
            b = st[s]["bk"].claim(pe, name)
            for m in range(NC):
                for c in range(NC):
                    last = pe.matmul(b[:, m * T:(m + 1) * T], w[:, c, col + m * P:col + (m + 1) * P], x[:, c, :],
                                     start=c == 0, stop=c == NC - 1)
            last.then_inc(st[s]["bk"].filled(name), 1)

        def pe_tokens(pe, s, name, w, col, x, chunks=NC):
            b = st[s]["bk"].claim(pe, name)
            for t in range(NT):
                for c in range(chunks):
                    last = pe.matmul(b[:, t * D:(t + 1) * D], x[:, c, t * P:(t + 1) * P], w[:, c, col:col + D],
                                     start=c == 0, stop=c == chunks - 1)
            last.then_inc(st[s]["bk"].filled(name), 1)

        def act_weights_high(act, s, key, names, highs, before=0):
            bk, e = st[s]["bk"], st[s][key]["e"]
            high, split = sem(f"{key}_weights_high{s}"), sem(f"{key}_weights_split{s}")

            def make_high(i):
                bk.await_emptied(act, names[i])
                act.copy(highs[i], e[:, i % 2]).then_inc(high, 1)

            for i, name in enumerate(names):
                b = bk.await_filled(act, name)
                if before + i >= 2:
                    act.wait_ge(split, before + i - 1)
                act.activation(e[:, i % 2], b[:], ACT.Exp).then_inc(bk.emptied(name), 1)
                if i:
                    make_high(i - 1)
            make_high(len(names) - 1)

        def dve_weights_low(dve, s, key, highs, lows, before=0):
            e = st[s][key]["e"]
            for i in range(len(highs)):
                dve.wait_ge(sem(f"{key}_weights_high{s}"), before + i + 1)
                dve.tensor_tensor(lows[i], e[:, i % 2], highs[i], ALU.subtract)\
                    .then_inc(sem(f"{key}_weights_split{s}"), 1)

        def nystrom_weights(n, part):
            return [n["e1"][:, part, 2 * i:2 * i + 2, :].rearrange("p a t -> p (a t)") for i in range(4)] + \
                   [n["e3"][:, part * NT + t, c, :] for t in range(NT) for c in range(NC)]

        def pe_nystrom(pe, s):
            v, bk = st[s], st[s]["bk"]
            n, x = v["n"], x_of(s)
            pe.wait_ge(sem(f"input_turned{s}"), 16)
            pe.wait_ge(sem("load_nystrom"), 16)
            pe_features(pe, s, "n_q", W["qkv"], 0, x)
            pe_features(pe, s, "n_k", W["qkv"], D, x)
            pe_tokens(pe, s, "n_v", W["qkv"], 2 * D, x)
            yield 1
            pe.wait_ge(sem(f"n_landmarks{s}"), 1)
            b = bk.claim(pe, "n_sim2")
            for p in range(PAIRS):
                c, h = p // 4, 2 * (p % 4)
                last = pe.matmul(b[:, p * M:(p + 1) * M], n["qlm"][:, c, h:h + 2, :], n["kl"][:, c, :], start=True, stop=True)
            last.then_inc(bk.filled("n_sim2"), 1)
            pe.wait_ge(sem(f"n_half{s}"), 4)
            for t in range(NT):
                for c in range(NC):
                    b = bk.claim(pe, f"n_max1_{t}{c}")
                    pe.matmul(b[:], n["qb"][:, c, t * P:(t + 1) * P], n["klmb"][:, c, :, :], start=True, stop=True)\
                        .then_inc(bk.filled(f"n_max1_{t}{c}"), 1)
            for i in range(4):
                b = bk.claim(pe, f"n_max3_{i}")
                for j in range(2):
                    p = 2 * i + j
                    c, h = p // 4, 2 * (p % 4)
                    last = pe.matmul(b[:, j * T:(j + 1) * T], n["qlmb"][:, c, h:h + 2, :], n["kb"][:, c, :], start=True, stop=True)
                last.then_inc(bk.filled(f"n_max3_{i}"), 1)
            yield 2
            pe.wait_ge(sem(f"n_neg{s}"), 1)
            b = bk.claim(pe, "n_negT")
            bb = b[:, 0:3 * P // 2].bitcast(BF16)
            for i in range(3):
                last = pe.transpose(bb[:, i * P:(i + 1) * P], n["neg"][:, i, :], identb[:])
            last.then_inc(bk.filled("n_negT"), 1)
            yield 3
            bk.await_emptied(pe, "n_negT")
            bk.await_emptied(pe, "n_k")
            for i in range(4):
                b = bk.claim(pe, f"n_s1_{i}")
                for j in range(2):
                    p = 2 * i + j
                    c, h = p // 4, 2 * (p % 4)
                    pe.matmul(b[:, j * T:(j + 1) * T], n["klm"][:, c, h:h + 2, :], n["q"][:, c, :], start=True, stop=False)
                    last = pe.matmul(b[:, j * T:(j + 1) * T], selp[:, p, :], n["negT"][:, 0:2, :], start=False, stop=True)
                last.then_inc(bk.filled(f"n_s1_{i}"), 1)
            for t in range(NT):
                for c in range(NC):
                    name = f"n_s3_{t}{c}"
                    b = bk.claim(pe, name)
                    pe.matmul(b[:], n["k"][:, c, t * P:(t + 1) * P], n["qlm"][:, c, :, :], start=True, stop=False)
                    for j in range(4):
                        last = pe.matmul(b[:, j * P:(j + 1) * P], sel16[:, 4 * c + j, :], n["negT"][:, 2, :],
                                         start=False, stop=j == 3)
                    last.then_inc(bk.filled(name), 1)
            yield 4
            pe.wait_ge(sem(f"n_diagonal_a{s}"), 1)
            for g in range(2):
                b = bk.claim(pe, f"n_aT_{g}")
                for p in range(4):
                    last = pe.transpose(b[:, p * P:(p + 1) * P], n["ad"][:, 4 * g + p, :], ident[:])
                last.then_inc(bk.filled(f"n_aT_{g}"), 1)
            b = bk.claim(pe, "n_y")
            pe.wait_ge(sem(f"n_values{s}"), 2)
            pe.wait_ge(sem(f"n_weights_split{s}"), 8)
            for p in range(PAIRS):
                terms = [(t, *term) for t in range(NT) for term in TERMS]
                for j, (t, w, x) in enumerate(terms):
                    last = pe.matmul(b[:, p * 2 * VW:(p + 1) * 2 * VW],
                                     n["e3"][:, w * NT + t, p // 4, (p % 4) * P:(p % 4 + 1) * P],
                                     n["v"][:, x * NT + t, 2 * p:2 * p + 2, :], start=j == 0, stop=j == len(terms) - 1)
            last.then_inc(bk.filled("n_y"), 1)
            yield 5

            def products(name, g, lhs, rhs, width):
                b = bk.claim(pe, f"{name}_{g}")
                for p in range(4):
                    last = pe.matmul(b[:, p * width:(p + 1) * width], lhs[:, 4 * g + p, :], rhs[:, 4 * g + p, :],
                                     start=True, stop=True)
                last.then_inc(bk.filled(f"{name}_{g}"), 1)

            for g in range(2):
                bk.await_emptied(pe, f"n_aT_{g}")
                products("n_k0", g, n["aT"], n["a"], M)
                products("n_kT0", g, n["ad"], n["aT"], P)
            for i in range(PINV_ITERS - 1):
                yield 6 + 3 * i
                for g in range(2):
                    bk.await_emptied(pe, f"n_k{i}_{g}")
                    bk.await_emptied(pe, f"n_kT{i}_{g}")
                    products(f"n_p{i}", g, n["kkT"], n["t1"], M)
                yield 7 + 3 * i
                for g in range(2):
                    bk.await_emptied(pe, f"n_p{i}_{g}")
                    products(f"n_t{i}", g, n["t2"], n["kkT"], P)
                yield 8 + 3 * i
                for g in range(2):
                    bk.await_emptied(pe, f"n_t{i}_{g}")
                    pe.wait_ge(sem(f"n_diagonal_k{s}"), 2 * i + g + 1)
                    products(f"n_kT{i + 1}", g, n["kk"], n["t3"], P)
                    if i == 0:
                        bk.await_emptied(pe, "n_y")
                    if i < PINV_ITERS - 2:
                        products(f"n_k{i + 1}", g, n["t3"], n["kz"], M + DH0)
                    else:
                        products(f"n_k{i + 1}", g, n["t3"], n["z"], DH0)
            yield 21
            for g in range(2):
                bk.await_emptied(pe, f"n_kT{PINV_ITERS - 1}_{g}")
                bk.await_emptied(pe, f"n_k{PINV_ITERS - 1}_{g}")
            for j in range(4):
                if j:
                    yield 21 + j
                    bk.await_emptied(pe, f"n_w{j - 1}")
                b = bk.claim(pe, f"n_w{j}")
                for p in range(PAIRS):
                    last = pe.matmul(b[:, p * DH0:(p + 1) * DH0], (n["kkT"] if j < 3 else n["aT"])[:, p, :],
                                     (n["z"] if j == 0 else n["z2"])[:, p, :], start=True, stop=True)
                last.then_inc(bk.filled(f"n_w{j}"), 1)
            yield 25
            bk.await_emptied(pe, "n_w3")
            for t in range(NT):
                b = bk.claim(pe, f"n_o{t}")
                for p in range(PAIRS):
                    for j, (w, x) in enumerate(TERMS):
                        last = pe.matmul(b[:, p * 2 * VW:(p + 1) * 2 * VW], n["e1"][:, w, p, t * P:(t + 1) * P],
                                         n["g"][:, x, p, :], start=j == 0, stop=j == len(TERMS) - 1)
                last.then_inc(bk.filled(f"n_o{t}"), 1)
            yield 26
            bk.await_emptied(pe, "n_o0")
            bk.await_emptied(pe, "n_o1")
            pe_transposes(pe, s, "n_oT", n["o"])
            yield 27
            bk.await_emptied(pe, "n_oT")
            pe_tokens(pe, s, "n_out", W["out"], 0, n["oT"])
            yield 28
            pe_norm(pe, s, "0", "n_xT")

        def dve_nystrom(dve, s, link):
            v, bk = st[s], st[s]["bk"]
            n = v["n"]
            b = bk.await_filled(dve, "n_q")
            for m in range(NC):
                last = dve.tensor_scalar(n["q"][:, m, :], b[:, m * T:(m + 1) * T], bias["q0"][:, m:m + 1],
                                         1.0 / np.sqrt(DH0), ALU.add, ALU.mult)
            last.then_inc(bk.emptied("n_q"), 1)
            bk.await_emptied(dve, "n_q")
            dve.tensor_reduce(n["qs"][:], n["q"][:].rearrange("p c (m l) -> p c m l", l=LM), axis=AX.X, op=ALU.add)
            bk.await_emptied(dve, "n_k")
            link(dve.tensor_reduce(n["ks"][:], n["k"][:].rearrange("p c (m l) -> p c m l", l=LM), axis=AX.X, op=ALU.add))
            for c in range(NC):
                m = hmask[:, HC:2 * HC, None].to_broadcast([P, HC, M])
                dve.tensor_tensor(n["qlm"][:, c], n["qs"][:, c, None, :].to_broadcast([P, HC, M]), m, ALU.mult)
                dve.tensor_tensor(n["klm"][:, c], n["ks"][:, c, None, :].to_broadcast([P, HC, M]), m, ALU.mult)
            dve.tensor_scalar(n["kl"][:], n["ks"][:], 1.0 / LM, None, ALU.mult).then_inc(sem(f"n_landmarks{s}"), 1)
            b = bk.await_filled(dve, "n_v")
            dve.tensor_tensor(n["v32"], b[:].rearrange("p (t d) -> p t d", t=NT),
                              rows["v0"][:, None, :].to_broadcast([P, NT, D]), ALU.add).then_inc(bk.emptied("n_v"), 1)
            yield 1
            b = bk.await_filled(dve, "n_sim2")
            b3 = b[:].rearrange("p (a m) -> p a m", m=M)
            link(dve.tensor_reduce(n["mx2"][:], b3, axis=AX.X, op=ALU.max))
            dve.tensor_tensor(n["a"][:], b3, n["mx2"][:, :, None].to_broadcast([P, PAIRS, M]), ALU.subtract)\
                .then_inc(bk.emptied("n_sim2"), 1)
            for t in range(NT):
                for c in range(NC):
                    b = bk.await_filled(dve, f"n_max1_{t}{c}")
                    dve.tensor_reduce(n["mx1"][:, t, c * HC:(c + 1) * HC], b[:].rearrange("p (h m) -> p h m", m=M),
                                      axis=AX.X, op=ALU.max).then_inc(bk.emptied(f"n_max1_{t}{c}"), 1)
            for i in range(4):
                b = bk.await_filled(dve, f"n_max3_{i}")
                dve.tensor_reduce(n["mx3"][:, 2 * i:2 * i + 2], b[:].rearrange("p (a t) -> p a t", t=T),
                                  axis=AX.X, op=ALU.max).then_inc(bk.emptied(f"n_max3_{i}"), 1)
            bk.await_emptied(dve, "n_max1_11")
            bk.await_emptied(dve, "n_max3_3")
            dve.wait_ge(sem(f"n_zeros{s}"), 1)
            dve.tensor_scalar(n["neg"][:, 0:2, 0:H0], n["mx1"][:], -1.0, None, ALU.mult)
            dve.tensor_scalar(n["neg"][:, 2, 0:PAIRS], n["mx3"][:], -1.0, None, ALU.mult).then_inc(sem(f"n_neg{s}"), 1)
            yield 2
            dve.wait_ge(sem(f"n_exp2{s}"), 1)
            link(dve.tensor_reduce(n["sum2"][:], n["a"][:], axis=AX.X, op=ALU.add))
            link(dve.reciprocal(n["rs2"][:], n["sum2"][:]))
            dve.tensor_tensor(n["a"][:], n["a"][:], n["rs2"][:, :, None].to_broadcast([P, PAIRS, M]), ALU.mult)\
                .then_inc(sem(f"n_a{s}"), 1)
            yield 3
            dve_weights_low(dve, s, "n", nystrom_weights(n, HIGH), nystrom_weights(n, LOW))
            yield 4
            b = bk.await_filled(dve, "n_y")
            y = b[:, 0:PAIRS * 2 * VW].rearrange("p (a w) -> p a w", w=2 * VW)
            for u in range(2):
                last = dve.reciprocal(n["ry"][u * M:(u + 1) * M, :], y[u * M:(u + 1) * M, :, u * VW + DH0])
            link(last)
            for u in range(2):
                r = slice(u * M, (u + 1) * M)
                last = dve.tensor_tensor(n["z"][r], y[r, :, u * VW:u * VW + DH0],
                                         n["ry"][r, :, None].to_broadcast([M, PAIRS, DH0]), ALU.mult)
            last.then_inc(bk.emptied("n_y"), 1)
            eye = consts["eye"][:, None, :].to_broadcast([P, 4, M])
            eye325 = consts["eye325"][:, None, :].to_broadcast([P, 4, P])

            def part(b, width, lo, hi):
                return b[:, 0:4 * width].rearrange("p (a m) -> p a m", m=width)[:, :, lo:hi]

            for i in range(PINV_ITERS):
                yield 5 + 3 * i
                for g in range(2):
                    q = slice(4 * g, 4 * g + 4)
                    b = bk.await_filled(dve, f"n_k{i}_{g}")
                    if i == PINV_ITERS - 1:
                        dve.tensor_copy(n["z"][:, q], part(b, DH0, 0, DH0)).then_inc(bk.emptied(f"n_k{i}_{g}"), 1)
                        continue
                    w = M + DH0 if i else M
                    dve.tensor_copy(n["kz"][:, q, 0:w], part(b, w, 0, w))
                    dve.scalar_tensor_tensor(n["t1"][:, q], eye, 7.0, part(b, w, 0, M), ALU.mult, ALU.subtract)\
                        .then_inc(bk.emptied(f"n_k{i}_{g}"), 1)
                if i == PINV_ITERS - 1:
                    break
                yield 6 + 3 * i
                for g in range(2):
                    q = slice(4 * g, 4 * g + 4)
                    b = bk.await_filled(dve, f"n_p{i}_{g}")
                    if i == 0:
                        dve.wait_ge(sem(f"n_cleared{s}"), 2)
                    for u in (0, M):
                        last = dve.scalar_tensor_tensor(n["t2"][u:u + M, q, u:u + M], eye[u:u + M], 15.0,
                                                        part(b, M, 0, M)[u:u + M], ALU.mult, ALU.subtract)
                    last.then_inc(bk.emptied(f"n_p{i}_{g}"), 1)
                yield 7 + 3 * i
                for g in range(2):
                    q = slice(4 * g, 4 * g + 4)
                    b = bk.await_filled(dve, f"n_t{i}_{g}")
                    dve.scalar_tensor_tensor(n["t3"][:, q], part(b, P, 0, P), -0.25, eye325, ALU.mult, ALU.add)\
                        .then_inc(bk.emptied(f"n_t{i}_{g}"), 1)
            for j in range(4):
                yield 21 + j
                b = bk.await_filled(dve, f"n_w{j}")
                w = b[:, 0:PAIRS * DH0].rearrange("p (a d) -> p a d", d=DH0)
                if j < 3:
                    dve.scalar_tensor_tensor(n["z2"][:], n["z"][:], (7.0, 15.0, 13.0)[j], w, ALU.mult, ALU.subtract)\
                        .then_inc(bk.emptied(f"n_w{j}"), 1)
                else:
                    dve.wait_ge(sem(f"n_vones{s}"), 1)
                    own = [(slice(u * M, (u + 1) * M), slice(u * VW, u * VW + DH0)) for u in range(2)]
                    for r, cols in own:
                        last = dve.tensor_scalar(n["g"][r, HIGH, :, cols], w[r], 0.25, None, ALU.mult)
                    link(last)
                    for r, cols in own:
                        last = dve.scalar_tensor_tensor(n["g"][r, LOW, :, cols], w[r], 0.25, n["g"][r, HIGH, :, cols],
                                                        ALU.mult, ALU.subtract)
                    last.then_inc(bk.emptied(f"n_w{j}"), 1)
            yield 25
            for t in range(NT):
                b = bk.await_filled(dve, f"n_o{t}")
                o = b[:, 0:H0 * VW].rearrange("p (h w) -> p h w", w=VW)
                link(dve.reciprocal(n["ro"][:, t, :], o[:, :, DH0]))
                dve.tensor_tensor(n["o"][:, t].rearrange("p (h d) -> p h d", h=H0), o[:, :, 0:DH0],
                                  n["ro"][:, t, :, None].to_broadcast([P, H0, DH0]), ALU.mult)\
                    .then_inc(bk.emptied(f"n_o{t}"), 1)
            yield 27
            dve_residual_norm(dve, s, link, "n_out", "0")

        def act_nystrom(act, s):
            v, bk = st[s], st[s]["bk"]
            n = v["n"]
            b = bk.await_filled(act, "n_k")
            for m in range(NC):
                last = act.activation(n["k"][:, m, :], b[:, m * T:(m + 1) * T], ACT.Identity, bias=bias["k0"][:, m:m + 1])
            last.then_inc(bk.emptied("n_k"), 1)
            bk.await_emptied(act, "n_q")
            act.copy(n["qb"][:], n["q"][:]).then_inc(sem(f"n_half{s}"), 1)
            bk.await_emptied(act, "n_k")
            act.copy(n["kb"][:], n["k"][:]).then_inc(sem(f"n_half{s}"), 1)
            act.wait_ge(sem(f"n_landmarks{s}"), 1)
            act.copy(n["klmb"][:], n["klm"][:]).then_inc(sem(f"n_half{s}"), 1)
            act.copy(n["qlmb"][:], n["qlm"][:]).then_inc(sem(f"n_half{s}"), 1)
            yield 1
            bk.await_emptied(act, "n_sim2")
            act.activation(n["a"][:], n["a"][:], ACT.Exp).then_inc(sem(f"n_exp2{s}"), 1)
            yield 2
            b = bk.await_filled(act, "n_negT")
            act.copy(n["negT"][:].rearrange("p a b -> p (a b)"), b[:, 0:3 * P // 2].bitcast(BF16))\
                .then_inc(bk.emptied("n_negT"), 1)
            yield 3
            act.wait_ge(sem(f"n_values{s}"), 2)
            act_weights_high(act, s, "n", [f"n_s1_{i}" for i in range(4)] +
                             [f"n_s3_{t}{c}" for t in range(NT) for c in range(NC)], nystrom_weights(n, HIGH))
            yield 4
            for g in range(2):
                b = bk.await_filled(act, f"n_aT_{g}")
                act.copy(n["aT"][:, 4 * g:4 * g + 4], b[:].rearrange("p (a m) -> p a m", m=P))\
                    .then_inc(bk.emptied(f"n_aT_{g}"), 1)
            for i in range(PINV_ITERS):
                yield 5 + 3 * i
                for g in range(2):
                    b = bk.await_filled(act, f"n_kT{i}_{g}")
                    act.copy(n["kkT"][:, 4 * g:4 * g + 4], b[:].rearrange("p (a m) -> p a m", m=P))\
                        .then_inc(bk.emptied(f"n_kT{i}_{g}"), 1)
                if i < PINV_ITERS - 1:
                    yield 6 + 3 * i
                    for g in range(2):
                        q = slice(4 * g, 4 * g + 4)
                        bk.await_emptied(act, f"n_k{i}_{g}")
                        if i == 0:
                            act.wait_ge(sem(f"n_cleared{s}"), 1)
                        for u in (0, M):
                            last = act.copy(n["kk"][u:u + M, q, u:u + M], n["kz"][u:u + M, q, 0:M])
                        last.then_inc(sem(f"n_diagonal_k{s}"), 1)
            yield 26
            b = bk.await_filled(act, "n_oT")
            act.copy(n["oT"][:].rearrange("p c t -> p (c t)"), b[:]).then_inc(bk.emptied("n_oT"), 1)
            yield 28
            act_norm(act, s, "n_xT")

        def pool_nystrom(pool, s):
            v, bk = st[s], st[s]["bk"]
            n = v["n"]
            pool.wait_ge(sem(f"input{s}"), 16)
            pool.memset(n["neg"][:], 0.0).then_inc(sem(f"n_zeros{s}"), 1)
            pool.tensor_tensor(out=v["res"][:], in0=v["x"][:], in1=rows["o0"][:, None, :].to_broadcast([P, NT, D]),
                               op=ALU.add).then_inc(sem(f"res{s}"), 1)
            pool.memset(n["v"][:, 0:NT, :, DH0], 1.0)
            pool.memset(n["v"][:, NT:2 * NT, :, DH0], 0.0)
            pool.memset(n["g"][:], 0.0).then_inc(sem(f"n_gz{s}"), 1)
            pool.wait_ge(sem(f"n_gz{s}"), 1)
            pool.memset(n["g"][0:M, HIGH, :, DH0], 1.0)
            pool.memset(n["g"][M:P, HIGH, :, VW + DH0], 1.0).then_inc(sem(f"n_vones{s}"), 1)
            pool.wait_ge(sem(f"n_vones{s}"), 1)
            bk.await_emptied(pool, "n_v")
            v32 = n["v32"].rearrange("p t (h d) -> p t h d", h=H0)
            pool.tensor_copy(n["v"][:, 0:NT, :, 0:DH0], v32).then_inc(sem(f"n_values{s}"), 1)
            pool.wait_ge(sem(f"n_values{s}"), 1)
            pool.tensor_tensor(out=n["v"][:, NT:2 * NT, :, 0:DH0], in0=v32, in1=n["v"][:, 0:NT, :, 0:DH0],
                               op=ALU.subtract).then_inc(sem(f"n_values{s}"), 1)
            yield 2
            bk.await_done(pool, "n_max3_3")
            pool.wait_ge(sem(f"n_a{s}"), 1)
            pool.tensor_tensor(out=n["ad"].rearrange("p a (u m) -> p a u m", u=2),
                               in0=n["a"][:, :, None, :].to_broadcast([P, PAIRS, 2, M]),
                               in1=consts["halves"][:, None, :, None].to_broadcast([P, PAIRS, 2, M]), op=ALU.mult)\
                .then_inc(sem(f"n_diagonal_a{s}"), 1)
            yield 4
            bk.await_done(pool, "n_s3_11")
            pool.memset(n["kk"], 0.0).then_inc(sem(f"n_cleared{s}"), 1)
            bk.await_done(pool, "n_y")
            pool.memset(n["t2"], 0.0).then_inc(sem(f"n_cleared{s}"), 1)
            yield 27
            pool_norm(pool, s, "0")

        def dve_norm(dve, s, link, key, src, dst):
            v = st[s]
            for t in range(NT):
                last = dve.bn_stats(v["st"][:, t, :], src[:, t, :])
            link(last)
            for t in range(NT):
                last = dve.bn_aggr(v["mv"][:, t, :], v["st"][:, t, :])
            link(last)
            dve.tensor_scalar(v["ve"][:], v["mv"][:, :, 1], EPS, None, ALU.add).then_inc(sem(f"variance{key}_{s}"), 1)
            dve.wait_ge(sem(f"rstd{key}_{s}"), 1)
            for t in range(NT):
                last = dve.tensor_scalar(dst[:, t, :], src[:, t, :], v["mv"][:, t, 0:1], v["rstd"][:, t:t + 1],
                                         ALU.subtract, ALU.mult)
            last.then_inc(sem(f"x{key}_{s}"), 1)

        def dve_residual_norm(dve, s, link, name, key):
            v, bk = st[s], st[s]["bk"]
            b = bk.await_filled(dve, name)
            dve.wait_ge(sem(f"res{s}"), 1 + int(key))
            dve.tensor_tensor(v["y"][:].rearrange("p t d -> p (t d)"), b[:], v["res"][:].rearrange("p t d -> p (t d)"),
                              ALU.add).then_inc(bk.emptied(name), 1)
            bk.await_emptied(dve, name)
            dve_norm(dve, s, link, key, v["y"], v["x"])

        def pool_norm(pool, s, key):
            v = st[s]
            pool.wait_ge(sem(f"variance{key}_{s}"), 1)
            pool.tensor_tensor(out=v["rstd"][:], in0=v["ve"][:], in1=NEGH[:], op=ALU.pow)\
                .then_inc(sem(f"rstd{key}_{s}"), 1)

        def pe_norm(pe, s, key, name):
            pe.wait_ge(sem(f"x{key}_{s}"), 1)
            pe_transposes(pe, s, name, st[s]["x"])

        def act_norm(act, s, name):
            v, bk = st[s], st[s]["bk"]
            b = bk.await_filled(act, name)
            act.copy(x_of(s), b[:].rearrange("p (c t) -> p c t", c=NC)).then_inc(bk.emptied(name), 1)

        def dilated_weights(n, part):
            return [n["p0"][:, part, 2 * i:2 * i + 2, :].rearrange("p h t -> p (h t)") for i in range(4)] + \
                   [n["p1"][:, part, 4 * i:4 * i + 4, :].rearrange("p h t -> p (h t)") for i in range(2)]

        def pe_dilated(pe, s):
            v, bk = st[s], st[s]["bk"]
            n, x = v["d"], x_of(s)
            yield 100
            bk.await_emptied(pe, "n_xT")
            pe.wait_ge(sem("load_rest"), 16)
            pe.wait_ge(sem(f"context{s}"), 16)
            pe_features(pe, s, "d_q", W["dq"], 0, x)
            pe_features(pe, s, "d_k", W["dk"], 0, v["ctx"])
            pe_tokens(pe, s, "d_v", W["dv"], 0, v["ctx"])
            for c in range(NC):
                yield 110 + 10 * c
                pe.wait_ge(sem(f"d_keys_half{s}"), 1)
                pe.wait_ge(sem(f"d_queries_high{s}"), 1 + c)
                for i in range(6):
                    t, heads, keys = (0, range(4 * i, 4 * i + 4), P) if i < 2 else (1, range(2 * i - 4, 2 * i - 2), T)
                    b = bk.claim(pe, f"d_m{c}_{i}")
                    for j, h in enumerate(heads):
                        pe.matmul(b[:, j * keys:(j + 1) * keys], n["qmb"][:, h, t * P:(t + 1) * P], n["kb"][:, c, 0:keys],
                                  start=True, stop=False)
                        last = pe.matmul(b[:, (j + 1) * keys - P:(j + 1) * keys], identb[:], consts["above"][:],
                                         start=False, stop=True)
                    last.then_inc(bk.filled(f"d_m{c}_{i}"), 1)
                yield 111 + 10 * c
                pe.wait_ge(sem(f"d_neg{s}"), 1 + c)
                b = bk.claim(pe, f"d_negT{c}")
                bb = b[:, 0:P].bitcast(BF16)
                for t in range(NT):
                    last = pe.transpose(bb[:, t * P:(t + 1) * P], n["neg"][:, t, :], identb[:])
                last.then_inc(bk.filled(f"d_negT{c}"), 1)
                yield 112 + 10 * c
                pe.wait_ge(sem(f"d_queries_low{s}"), 1 + c)
                bk.await_emptied(pe, f"d_negT{c}")
                pe.wait_ge(sem(f"d_klow{s}"), 1)
                for i in range(6):
                    b = bk.claim(pe, f"d_s{c}_{i}")
                    k, h, heads, keys, queries = (0, 2 * i, 2, slice(0, P), slice(0, T)) if i < 4 else \
                        (1, 4 * (i - 4), 4, slice(P, T), slice(P, T))
                    for j, (kp, qp) in enumerate(TERMS):
                        pe.matmul(b[:], n[("kb", "kl")[kp]][:, c, keys], n[("qmb", "qml")[qp]][:, h:h + heads, queries],
                                  start=j == 0, stop=False)
                    width = T - k * P
                    for j in range(heads):
                        pe.matmul(b[:, j * width:(j + 1) * width], sel16[:, c * HC + h + j, :], n["negT"][:, k:NT, :],
                                  start=False, stop=False)
                        last = pe.matmul(b[:, j * width:j * width + P], identb[:], consts["below"][:], start=False,
                                         stop=j == heads - 1)
                    last.then_inc(bk.filled(f"d_s{c}_{i}"), 1)
                yield 113 + 10 * c
                pe.wait_ge(sem(f"d_values{s}"), 3)
                pe.wait_ge(sem(f"d_weights_split{s}"), 6 * (c + 1))
                for t in range(NT):
                    b = bk.claim(pe, f"d_o{c}_{t}")
                    for h in range(HC):
                        out = b[:, h * BR * VW:(h + 1) * BR * VW]
                        terms = [(k, *term) for k in range(t + 1) for term in TERMS]
                        for j, (k, w, x) in enumerate(terms):
                            weights = n["p1"][:, w, h, :] if k else n["p0"][:, w, h, t * P:(t + 1) * P]
                            last = pe.matmul(out, weights, n["v"][:, x * NT + k, c * HC + h, :],
                                             start=j == 0, stop=j == len(terms) - 1)
                    last.then_inc(bk.filled(f"d_o{c}_{t}"), 1)
            yield 131
            pe.wait_ge(sem(f"d_o{s}"), 1)
            pe_transposes(pe, s, "d_oT", n["o"])
            yield 132
            bk.await_emptied(pe, "d_oT")
            pe_tokens(pe, s, "d_out", W["do"], 0, n["oT"])
            yield 133
            pe_norm(pe, s, "1", "d_xT")

        def dve_dilated(dve, s, link):
            v, bk = st[s], st[s]["bk"]
            n = v["d"]
            yield 100
            b = bk.await_filled(dve, "d_q")
            for m in range(NC):
                last = dve.tensor_scalar(n["q"][:, m, :], b[:, m * T:(m + 1) * T], bias["dq"][:, m:m + 1],
                                         float(DH0) ** -0.5, ALU.add, ALU.mult)
            last.then_inc(bk.emptied("d_q"), 1)
            b = bk.await_filled(dve, "d_v")
            dve.tensor_tensor(n["v32"], b[:].rearrange("p (t d) -> p t d", t=NT),
                              rows["dv"][:, None, :].to_broadcast([P, NT, D]), ALU.add).then_inc(bk.emptied("d_v"), 1)
            for c in range(NC):
                yield 110 + 10 * c
                if c:
                    bk.await_done(dve, f"d_s{c - 1}_5")
                else:
                    bk.await_emptied(dve, "d_q")
                    link(dve.tensor_copy(n["qh"], n["q"][:]))
                dve.tensor_tensor(n["qmb"][:], n["qh"][:, c, None, :].to_broadcast([P, HC, T]),
                                  hmask[:, 0:HC, None].to_broadcast([P, HC, T]), ALU.mult)\
                    .then_inc(sem(f"d_queries_high{s}"), 1)
                if c == 0:
                    dve.tensor_tensor(n["ql"], n["q"][:], n["qh"], ALU.subtract).then_inc(sem(f"d_low{s}"), 1)
                    dve.wait_ge(sem(f"d_keys_half{s}"), 1)
                    dve.tensor_tensor(n["kl"], n["k"][:], n["kb"][:], ALU.subtract).then_inc(sem(f"d_klow{s}"), 1)
                for i in range(6):
                    b = bk.await_filled(dve, f"d_m{c}_{i}")
                    t, h, k = (0, 4 * i, 4) if i < 2 else (1, 2 * i - 4, 2)
                    dve.tensor_reduce(n["mx"][:, t, c * HC + h:c * HC + h + k], b[:].rearrange("p (h k) -> p h k", h=k),
                                      axis=AX.X, op=ALU.max).then_inc(bk.emptied(f"d_m{c}_{i}"), 1)
                for i in (3, 4, 5):
                    bk.await_emptied(dve, f"d_m{c}_{i}")
                dve.wait_ge(sem(f"d_v{s}"), 1)
                if c:
                    bk.await_done(dve, f"d_negT{c - 1}")
                dve.tensor_scalar(n["neg"][:, :, c * HC:(c + 1) * HC], n["mx"][:, :, c * HC:(c + 1) * HC], -1.0, None,
                                  ALU.mult).then_inc(sem(f"d_neg{s}"), 1)
                yield 112 + 10 * c
                dve_weights_low(dve, s, "d", dilated_weights(n, HIGH), dilated_weights(n, LOW), 6 * c)
            yield 130
            for c in range(NC):
                for t in range(NT):
                    bk.await_emptied(dve, f"d_o{c}_{t}")
            dve.tensor_scalar(n["s"][:].rearrange("p t h b -> p (t h b)"),
                              n["n"][:].rearrange("p t h b w -> p (t h b) w")[:, :, DH0], TINY, None, ALU.max)\
                .then_inc(sem(f"d_sum{s}"), 1)
            valid = consts["valid"][:].rearrange("p (h b) -> p h b", b=BR)[:, None].to_broadcast([P, NT, H0, BR])
            allh = [P, NT * H0, BR]

            def flat(key):
                return n[key][:].rearrange("p t h b -> p (t h) b")

            lm = n["lm"][:].rearrange("p t h -> p (t h)")
            rz = n["rz"][:].rearrange("p t h -> p (t h)")
            dve.wait_ge(sem(f"d_sum{s}"), 1)
            dve.reciprocal(n["rc"][:], n["s"][:])
            dve.wait_ge(sem(f"d_sum{s}"), 2)
            for t in range(NT):
                last = dve.tensor_tensor(n["ls"][:, t], n["ls"][:, t], n["neg"][:, t, 0:H0, None].to_broadcast([P, H0, BR]),
                                         ALU.subtract)
            link(last)
            link(dve.scalar_tensor_tensor(n["isz"][:], n["ls"][:], 0.0, valid, ALU.not_equal, ALU.mult))
            link(dve.tensor_tensor(n["w"][:], n["isz"][:], n["s"][:], ALU.mult))
            link(dve.tensor_scalar(n["w"][:], n["w"][:], SMALLEST, None, ALU.add))
            link(dve.tensor_reduce(lm, flat("w"), axis=AX.X, op=ALU.add))
            dve.reciprocal(rz, lm)
            link(dve.tensor_tensor(n["w"][:], n["w"][:], n["rc"][:], ALU.mult))
            link(dve.tensor_tensor(flat("w"), flat("w"), rz[:, :, None].to_broadcast(allh), ALU.mult))
            for t in range(NT):
                r = n["n"][:, t].rearrange("p h b w -> p (h b) w")[:, :, 0:DH0]
                last = dve.tensor_tensor(r, r, n["w"][:, t].rearrange("p h b -> p (h b)")[:, :, None]
                                         .to_broadcast([P, H0 * BR, DH0]), ALU.mult)
            link(last)
            for t in range(NT):
                last = dve.tensor_reduce(n["o"][:, t].rearrange("p (h d) -> p h d", h=H0),
                                         n["n"][:, t].rearrange("p h b w -> p h w b")[:, :, 0:DH0, :], axis=AX.X, op=ALU.add)
            last.then_inc(sem(f"d_o{s}"), 1)
            yield 132
            dve_residual_norm(dve, s, link, "d_out", "1")

        def act_dilated(act, s):
            v, bk = st[s], st[s]["bk"]
            n = v["d"]
            yield 100
            b = bk.await_filled(act, "d_k")
            for m in range(NC):
                last = act.activation(n["k"][:, m, :], b[:, m * T:(m + 1) * T], ACT.Identity, bias=bias["dk"][:, m:m + 1])
            last.then_inc(bk.emptied("d_k"), 1)
            bk.await_emptied(act, "d_k")
            act.copy(n["kb"][:], n["k"][:]).then_inc(sem(f"d_keys_half{s}"), 1)
            bk.await_emptied(act, "d_v")
            act.copy(n["v"].rearrange("p t h (b w) -> p t h b w", b=BR)[:, 0:NT, :, 0, 0:DH0],
                     n["v32"].rearrange("p t (h d) -> p t h d", h=H0)).then_inc(sem(f"d_values{s}"), 1)
            for c in range(NC):
                yield 111 + 10 * c
                b = bk.await_filled(act, f"d_negT{c}")
                act.copy(n["negT"][:].rearrange("p a b -> p (a b)"), b[:, 0:P].bitcast(BF16))\
                    .then_inc(bk.emptied(f"d_negT{c}"), 1)
                yield 112 + 10 * c
                if c:
                    bk.await_done(act, f"d_o{c - 1}_1")
                act.wait_ge(sem(f"d_values{s}"), 2)
                act_weights_high(act, s, "d", [f"d_s{c}_{i}" for i in range(6)], dilated_weights(n, HIGH), 6 * c)
                yield 113 + 10 * c
                for t in range(NT):
                    b = bk.await_filled(act, f"d_o{c}_{t}")
                    act.copy(n["n"][:, t, c * HC:(c + 1) * HC].rearrange("p h b w -> p (h b w)"), b[:, 0:HC * BR * VW])\
                        .then_inc(bk.emptied(f"d_o{c}_{t}"), 1)
            yield 130
            act.wait_ge(sem(f"d_sum{s}"), 1)
            act.activation(n["ls"][:], n["s"][:], ACT.Ln).then_inc(sem(f"d_sum{s}"), 1)
            yield 131
            b = bk.await_filled(act, "d_oT")
            act.copy(n["oT"][:].rearrange("p c t -> p (c t)"), b[:]).then_inc(bk.emptied("d_oT"), 1)
            yield 133
            act_norm(act, s, "d_xT")

        def pool_dilated(pool, s):
            v, bk = st[s], st[s]["bk"]
            n = v["d"]
            yield 100
            pool.wait_ge(sem(f"x0_{s}"), 1)
            pool.tensor_tensor(out=v["res"][:], in0=v["x"][:], in1=rows["do"][:, None, :].to_broadcast([P, NT, D]),
                               op=ALU.add).then_inc(sem(f"res{s}"), 1)
            pool.memset(n["neg"][:], 0.0).then_inc(sem(f"d_v{s}"), 1)
            v4 = n["v"].rearrange("p t h (b w) -> p t h b w", b=BR)
            v32 = n["v32"].rearrange("p t (h d) -> p t h d", h=H0)
            pool.memset(v4[:, 0:NT, :, 0, DH0], 1.0)
            pool.memset(v4[:, NT:2 * NT, :, 0, DH0], 0.0)
            pool.wait_ge(sem(f"d_values{s}"), 1)
            pool.tensor_tensor(out=v4[:, NT:2 * NT, :, 0, 0:DH0], in0=v32, in1=v4[:, 0:NT, :, 0, 0:DH0],
                               op=ALU.subtract).then_inc(sem(f"d_values{s}"), 1)
            for c in range(NC):
                yield 110 + 10 * c
                if c:
                    bk.await_done(pool, f"d_s{c - 1}_5")
                pool.wait_ge(sem(f"d_low{s}"), 1)
                pool.tensor_tensor(out=n["qml"][:], in0=n["ql"][:, c, None, :].to_broadcast([P, HC, T]),
                                   in1=hmask[:, 0:HC, None].to_broadcast([P, HC, T]), op=ALU.mult)\
                    .then_inc(sem(f"d_queries_low{s}"), 1)
                if c == 0:
                    yield 111
                    pool.wait_ge(sem(f"d_values{s}"), 2)
                    valid = consts["valid"][:].rearrange("p (h b) -> p h b", b=BR)
                    for br in range(1, BR):
                        last = pool.tensor_tensor(out=v4[:, :, :, br, :], in0=v4[:, :, :, 0, :],
                                                  in1=valid[:, None, :, br, None].to_broadcast([P, 2 * NT, H0, VW]), op=ALU.mult)
                    last.then_inc(sem(f"d_values{s}"), 1)
            yield 132
            pool_norm(pool, s, "1")

        def pe_ffn(pe, s):
            v, bk = st[s], st[s]["bk"]
            n, x = v["f"], x_of(s)
            yield 200
            bk.await_emptied(pe, "d_xT")
            for i in range(FC // 2):
                b = bk.claim(pe, f"f_h{i}")
                for j in range(2):
                    f = 2 * i + j
                    for c in range(NC):
                        last = pe.matmul(b[:, j * T:(j + 1) * T], W["ff1"][:, c, f * P:(f + 1) * P], x[:, c, :],
                                         start=c == 0, stop=c == NC - 1)
                last.then_inc(bk.filled(f"f_h{i}"), 1)
            yield 201
            for i in range(FC // 2):
                bk.await_emptied(pe, f"f_h{i}")
            pe_tokens(pe, s, "f_out", w2, 0, n["h"], FC)
            yield 202
            pe_norm(pe, s, "2", "f_xT")

        def act_ffn(act, s):
            v, bk = st[s], st[s]["bk"]
            n = v["f"]
            yield 200
            for i in range(FC // 2):
                b = bk.await_filled(act, f"f_h{i}")
                for j in range(2):
                    f = 2 * i + j
                    last = act.activation(n["h"][:, f, :], b[:, j * T:(j + 1) * T], ACT.Gelu, bias=bias["ff1"][:, f:f + 1])
                last.then_inc(bk.emptied(f"f_h{i}"), 1)
            yield 202
            act_norm(act, s, "f_xT")

        def dve_ffn(dve, s, link):
            yield 201
            dve_residual_norm(dve, s, link, "f_out", "2")

        def pool_ffn(pool, s):
            v = st[s]
            yield 200
            pool.wait_ge(sem(f"x1_{s}"), 1)
            pool.tensor_tensor(out=v["res"][:], in0=v["x"][:], in1=rows["ff2"][:, None, :].to_broadcast([P, NT, D]),
                               op=ALU.add).then_inc(sem(f"res{s}"), 1)
            yield 201
            pool_norm(pool, s, "2")

        def pe_memory(pe, s):
            v, bk = st[s], st[s]["bk"]
            n, xz, x = v["r"], v["xz"], x_of(s)
            yield 300
            bk.await_emptied(pe, "f_xT")
            pe_tokens(pe, s, "r_v", W["mw"], 0, x)
            for i in range(4):
                r = slice(HD1 * (i % 2), HD1 * (i % 2 + 1))
                b = bk.claim(pe, f"r_s{i}")
                for c in range(NC):
                    if i < 2:
                        last = pe.matmul(b[:, c * T:(c + 1) * T], xz[r, c, 0:P], xz[r, c, 1:T + 1], start=True, stop=True)
                    else:
                        last = pe.matmul(b[:, c * P:(c + 1) * P], xz[r, c, P:T], xz[r, c, P + 1:T + 1], start=True, stop=True)
                last.then_inc(bk.filled(f"r_s{i}"), 1)
            yield 301
            for name in ("r_v", "r_s0", "r_s1", "r_s2", "r_s3"):
                bk.await_emptied(pe, name)
            b = bk.claim(pe, "r_r")
            for h in range(H1):
                r, c = slice(HD1 * (h % 2), HD1 * (h % 2 + 1)), h // 2
                pe.matmul(b[r, c * T:(c + 1) * T], n["v"][:, 0, h * HD1:(h + 1) * HD1], n["s0"][:, h, :],
                          start=True, stop=False)
                last = pe.matmul(b[r, c * T + P:(c + 1) * T], n["v"][:, 1, h * HD1:(h + 1) * HD1], n["s1"][:, h, :],
                                 start=False, stop=True)
            last.then_inc(bk.filled("r_r"), 1)
            yield 302
            bk.await_emptied(pe, "r_r")
            pe_tokens(pe, s, "r_out", W["mr"], 0, n["r"])
            yield 303
            pe_norm(pe, s, "3", "r_xT")

        def act_memory(act, s):
            v, bk = st[s], st[s]["bk"]
            n = v["r"]
            yield 300
            b = bk.await_filled(act, "r_v")
            act.copy(n["v"][:].rearrange("p t d -> p (t d)"), b[:]).then_inc(bk.emptied("r_v"), 1)
            yield 301
            b = bk.await_filled(act, "r_r")
            act.copy(n["r"][:].rearrange("p c t -> p (c t)"), b[:]).then_inc(bk.emptied("r_r"), 1)
            yield 303
            act_norm(act, s, "r_xT")

        def dve_memory(dve, s, link):
            v, bk = st[s], st[s]["bk"]
            n = v["r"]
            yield 300
            for i in range(4):
                b = bk.await_filled(dve, f"r_s{i}")
                out, table, t = (n["s0"], dec0, T) if i < 2 else (n["s1"], dec1, P)
                dve.tensor_tensor(out[:, i % 2::2, :], b[:, 0:NC * t].rearrange("p (h t) -> p h t", t=t),
                                  table[:, i % 2::2, :], ALU.mult).then_inc(bk.emptied(f"r_s{i}"), 1)
            yield 302
            dve_residual_norm(dve, s, link, "r_out", "3")

        def pool_memory(pool, s):
            v = st[s]
            yield 300
            pool.wait_ge(sem(f"x2_{s}"), 1)
            pool.tensor_tensor(out=v["res"][:], in0=v["x"][:], in1=v["x"][:], op=ALU.add).then_inc(sem(f"res{s}"), 1)
            yield 302
            pool_norm(pool, s, "3")

        ROPES = (("ka", "ctx", "cosk", "sink"), ("kt", "ctx", "cosk", "sink"),
                 ("qa", "x", "cosq", "sinq"), ("qt", "x", "cosg", "sing"))
        tables = {"cosg": cosg, "sing": sing, **{k: consts[k] for k in ("cosk", "sink", "cosq", "sinq")}}

        def pe_gated(pe, s):
            v, bk = st[s], st[s]["bk"]
            n, x = v["g"], x_of(s)
            yield 400
            bk.await_emptied(pe, "r_xT")
            for key, src, _, _ in ROPES:
                pe_features(pe, s, "g_" + key, W[key], 0, x if src == "x" else v["ctx"])
            pe_tokens(pe, s, "g_va", W["va"], 0, v["ctx"])
            pe_tokens(pe, s, "g_vt", W["vt"], 0, v["ctx"])
            yield 401
            pe.wait_ge(sem(f"g_high{s}"), len(ROPES))
            for h in range(H2):
                r, c = slice(HD2 * (h % 4), HD2 * (h % 4 + 1)), h // 4
                for t in range(NT):
                    b = bk.claim(pe, f"g_m{h}_{t}")
                    for i in range(2):
                        last = pe.matmul(b[:, i * T:(i + 1) * T], n["hl"][r, HIGH, 2 + i, c * T + t * P:c * T + (t + 1) * P],
                                         n["hl"][r, HIGH, i, c * T:(c + 1) * T], start=True, stop=True)
                    last.then_inc(bk.filled(f"g_m{h}_{t}"), 1)
            yield 402
            pe.wait_ge(sem(f"g_neg{s}"), 1)
            b = bk.claim(pe, "g_negT")
            bb = b[:, 0:P].bitcast(BF16)
            for t in range(NT):
                last = pe.transpose(bb[0:H2, t * P:(t + 1) * P], n["neg"][:, t, :], identb[:])
            last.then_inc(bk.filled("g_negT"), 1)

            def values(h):
                for i in range(2):
                    pe.wait_ge(sem(f"g_split{i}_{s}"), h + 1)
                for t in range(NT):
                    terms = [(k, w, x) for k in range(KT2) for w, x in ((HIGH, HIGH), (HIGH, LOW), (LOW, HIGH))]
                    for j, (k, w, x) in enumerate(terms):
                        last = pe.matmul(o[t][:, h * VW2:(h + 1) * VW2], n["p"][:, 2 * (h % 2) + w, k, t * P:(t + 1) * P],
                                         n["v"][:, x, k, h, :], start=j == 0, stop=j == len(terms) - 1)
                    if h == H2 - 1:
                        last.then_inc(bk.filled(f"g_o{t}"), 1)
                if h < H2 - 2:
                    last.then_inc(sem(f"g_weights_used{s}"), 1)

            for h in range(H2):
                yield 410 + h
                if h == 0:
                    pe.wait_ge(sem(f"g_stacked{s}"), 16 * STACKED)
                    pe.wait_ge(sem(f"g_values{s}"), 2)
                    o = [bk.claim(pe, f"g_o{t}") for t in range(NT)]
                for i in range(2):
                    b = bk.claim(pe, f"g_s{h}_{i}")
                    for j in range(NT):
                        last = pe.matmul(b[:, j * T:(j + 1) * T], n["stack"][0:STACK, i, h, j * P:(j + 1) * P],
                                         n["stack"][0:STACK, 2 + i, h, :], start=True, stop=True)
                    last.then_inc(bk.filled(f"g_s{h}_{i}"), 1)
                if h:
                    values(h - 1)
            yield 410 + H2
            values(H2 - 1)
            yield 419
            for t in range(NT):
                bk.await_emptied(pe, f"g_o{t}")
            pe_transposes(pe, s, "g_oT", n["o"])
            yield 420
            bk.await_emptied(pe, "g_oT")
            pe_tokens(pe, s, "g_out", W["go"], 0, n["oT"])
            yield 421
            pe.wait_ge(sem(f"x4_{s}"), 1)
            pe_transposes(pe, s, "g_nT", n["n"])
            yield 422
            bk.await_emptied(pe, "g_nT")
            pe_tokens(pe, s, "g_ffn", W["gf"], 0, n["nT"])

        def dve_gated(dve, s, link):
            v, bk = st[s], st[s]["bk"]
            n = v["g"]
            yield 400
            for i, (key, _, _, sin) in enumerate(ROPES):
                bk.await_emptied(dve, "g_" + key)
                rot = n["rot"][:, i % 2]
                link(dve.stream_shuffle(rot.rearrange("p c t -> p (c t)"), n["feat"][:, i % 2].rearrange("p c t -> p (c t)"),
                                        [j ^ 1 for j in range(32)]))
                link(dve.tensor_tensor(rot, rot, tables[sin][:, None, :].to_broadcast([P, NC, T]), ALU.mult))
                dve.wait_ge(sem(f"g_cos{s}"), i + 1)
                dve.tensor_tensor(n["sum"][:, i % 2], n["sum"][:, i % 2], rot, ALU.add).then_inc(sem(f"g_sum{s}"), 1)
            for i, k in enumerate(("va", "vt")):
                b = bk.await_filled(dve, "g_" + k)
                dve.tensor_tensor(n["v32"][:, 2 * i:2 * i + 2, :], b[:].rearrange("p (t d) -> p t d", t=NT),
                                  rows[k][:, None, :].to_broadcast([P, NT, D]), ALU.add).then_inc(bk.emptied("g_" + k), 1)
            yield 401
            for h in range(H2):
                for t in range(NT):
                    b = bk.await_filled(dve, f"g_m{h}_{t}")
                    dve.tensor_reduce(n["mx"][:, t, h:h + 1], b[:], axis=AX.X, op=ALU.max)\
                        .then_inc(bk.emptied(f"g_m{h}_{t}"), 1)
            for h in (H2 - 2, H2 - 1):
                for t in range(NT):
                    bk.await_emptied(dve, f"g_m{h}_{t}")
            dve.tensor_scalar(n["neg"][:], n["mx"][:], -1.0, None, ALU.mult).then_inc(sem(f"g_neg{s}"), 1)
            for h in range(H2):
                yield 410 + h
                w = n["p"][:, 2 * (h % 2):2 * (h % 2) + 2]
                bk.await_emptied(dve, f"g_s{h}_1")
                if h >= 2:
                    dve.wait_ge(sem(f"g_weights_used{s}"), h - 1)
                dve.tensor_copy(w[:, HIGH, 2:4, :], n["e"][:, 1]).then_inc(sem(f"g_high_second{s}"), 1)
                dve.wait_ge(sem(f"g_high_second{s}"), h + 1)
                dve.tensor_tensor(w[:, LOW, 2:4, :], n["e"][:, 1], w[:, HIGH, 2:4, :], ALU.subtract)\
                    .then_inc(sem(f"g_split1_{s}"), 1)
            yield 418
            for t in range(NT):
                b = bk.await_filled(dve, f"g_o{t}")
                o = b[:, 0:H2 * VW2].rearrange("p (h w) -> p h w", w=VW2)
                link(dve.reciprocal(n["ro"][:, t, :], o[:, :, HD2]))
                dve.tensor_tensor(n["o"][:, t].rearrange("p (h d) -> p h d", h=H2), o[:, :, 0:HD2],
                                  n["ro"][:, t, :, None].to_broadcast([P, H2, HD2]), ALU.mult)\
                    .then_inc(bk.emptied(f"g_o{t}"), 1)
            yield 420
            b = bk.await_filled(dve, "g_out")
            dve.wait_ge(sem(f"res{s}"), 5)
            dve.tensor_tensor(n["u"][:].rearrange("p t d -> p (t d)"), b[:], v["res"][:].rearrange("p t d -> p (t d)"),
                              ALU.add).then_inc(bk.emptied("g_out"), 1)
            bk.await_emptied(dve, "g_out")
            dve_norm(dve, s, link, "4", n["u"], n["n"])
            yield 422
            b = bk.await_filled(dve, "g_ffn")
            dve.tensor_tensor(n["f"][:], b[:].rearrange("p (t d) -> p t d", t=NT),
                              rows["gf"][:, None, :].to_broadcast([P, NT, D]), ALU.add).then_inc(bk.emptied("g_ffn"), 1)
            bk.await_emptied(dve, "g_ffn")
            link(dve.scalar_tensor_tensor(v["y"][:], n["f"][:], 0.0, v["x"][:], ALU.max, ALU.add))
            dve_norm(dve, s, link, "5", v["y"], v["y"])

        def act_gated(act, s):
            v, bk = st[s], st[s]["bk"]
            n = v["g"]
            yield 400

            def high(i):
                act.wait_ge(sem(f"g_sum{s}"), i + 1)
                act.copy(n["hl"][:, HIGH, i], n["sum"][:, i % 2].rearrange("p c t -> p (c t)"))\
                    .then_inc(sem(f"g_high{s}"), 1)

            for i, (key, _, _, _) in enumerate(ROPES):
                b = bk.await_filled(act, "g_" + key)
                if i >= 2:
                    act.wait_ge(sem(f"g_sum{s}"), i - 1)
                for m in range(NC):
                    last = act.activation(n["feat"][:, i % 2, m, :], b[:, m * T:(m + 1) * T], ACT.Identity,
                                          bias=bias[key][:, m:m + 1])
                last.then_inc(bk.emptied("g_" + key), 1)
                if i:
                    high(i - 1)
            high(len(ROPES) - 1)
            yield 401
            bk.await_emptied(act, "g_va")
            bk.await_emptied(act, "g_vt")
            act.copy(n["v"][:, HIGH, :, :, 0:HD2], n["v32"].rearrange("p k (h d) -> p k h d", h=H2))\
                .then_inc(sem(f"g_values{s}"), 1)
            yield 402
            b = bk.await_filled(act, "g_negT")
            act.copy(n["negT"][0:H2].rearrange("p a b -> p (a b)"), b[0:H2, 0:P].bitcast(BF16))\
                .then_inc(bk.emptied("g_negT"), 1)
            for h in range(H2):
                yield 410 + h
                if h == 0:
                    act.wait_ge(sem(f"g_values{s}"), 2)
                for i in range(2):
                    b = bk.await_filled(act, f"g_s{h}_{i}")
                    if h:
                        act.wait_ge(sem(f"g_split{i}_{s}"), h)
                    act.activation(n["e"][:, i], b[:].rearrange("p (k t) -> p k t", t=T), ACT.Exp)\
                        .then_inc(bk.emptied(f"g_s{h}_{i}"), 1)
                bk.await_emptied(act, f"g_s{h}_0")
                if h >= 2:
                    act.wait_ge(sem(f"g_weights_used{s}"), h - 1)
                act.copy(n["p"][:, 2 * (h % 2) + HIGH, 0:2, :], n["e"][:, 0]).then_inc(sem(f"g_high_first{s}"), 1)
            yield 419
            b = bk.await_filled(act, "g_oT")
            act.copy(n["oT"][:].rearrange("p c t -> p (c t)"), b[:]).then_inc(bk.emptied("g_oT"), 1)
            yield 421
            b = bk.await_filled(act, "g_nT")
            for c in range(NC):
                last = act.activation(n["nT"][:, c, :], b[:, c * T:(c + 1) * T], ACT.Identity,
                                      bias=bias["beta"][:, c:c + 1], scale=bias["gamma"][:, c:c + 1])
            last.then_inc(bk.emptied("g_nT"), 1)

        def pool_gated(pool, s):
            v, bk = st[s], st[s]["bk"]
            n = v["g"]
            yield 400
            pool.wait_ge(sem(f"x3_{s}"), 1)
            pool.tensor_tensor(out=v["res"][:], in0=v["x"][:], in1=rows["go"][:, None, :].to_broadcast([P, NT, D]),
                               op=ALU.add).then_inc(sem(f"res{s}"), 1)

            def low(i):
                pool.wait_ge(sem(f"g_high{s}"), i + 1)
                pool.tensor_tensor(out=n["hl"][:, LOW, i], in0=n["sum"][:, i % 2].rearrange("p c t -> p (c t)"),
                                   in1=n["hl"][:, HIGH, i], op=ALU.subtract).then_inc(sem(f"g_low{s}"), 1)

            for i, (key, _, cos, _) in enumerate(ROPES):
                bk.await_emptied(pool, "g_" + key)
                if i >= 2:
                    pool.wait_ge(sem(f"g_low{s}"), i - 1)
                pool.tensor_tensor(out=n["sum"][:, i % 2], in0=n["feat"][:, i % 2],
                                   in1=tables[cos][:, None, :].to_broadcast([P, NC, T]), op=ALU.mult)\
                    .then_inc(sem(f"g_cos{s}"), 1)
                if i:
                    low(i - 1)
            low(len(ROPES) - 1)
            yield 401
            v32 = n["v32"].rearrange("p k (h d) -> p k h d", h=H2)
            pool.memset(n["v"][:, HIGH, :, :, HD2], 1.0)
            pool.memset(n["v"][:, LOW, :, :, HD2], 0.0)
            pool.wait_ge(sem(f"g_values{s}"), 1)
            pool.tensor_tensor(out=n["v"][:, LOW, :, :, 0:HD2], in0=v32, in1=n["v"][:, HIGH, :, :, 0:HD2],
                               op=ALU.subtract).then_inc(sem(f"g_values{s}"), 1)
            for h in range(H2):
                yield 410 + h
                w = n["p"][:, 2 * (h % 2):2 * (h % 2) + 2]
                pool.wait_ge(sem(f"g_high_first{s}"), h + 1)
                pool.tensor_tensor(out=w[:, LOW, 0:2, :], in0=n["e"][:, 0], in1=w[:, HIGH, 0:2, :], op=ALU.subtract)\
                    .then_inc(sem(f"g_split0_{s}"), 1)
            yield 420
            pool_norm(pool, s, "4")
            yield 422
            pool_norm(pool, s, "5")

        STACKED = 1 + 2 * 3 * 4 + 2

        def sp_stack(sp, s):
            n = st[s]["g"]
            done = sem(f"g_stacked{s}")
            yield 400
            sp.wait_ge(sem(f"x3_{s}"), 1)
            sp.dma_start(n["stack"][STACK - 1:STACK, 0:2].rearrange("p i h t -> p (i h t)"),
                         a["C_onesb"][0:2 * H2 * T // P, :].rearrange("(o a) b -> o (a b)", o=1)).then_inc(done, 16)
            for i, parts in ((0, (HIGH, HIGH, LOW)), (2, (HIGH, LOW, HIGH))):
                yield 400 + i / 4
                sp.wait_ge(sem(f"g_low{s}"), i + 2)
                for g in range(4):
                    for row, part in enumerate(parts):
                        heads = n["stack"][row * HD2:(row + 1) * HD2, i:i + 2].rearrange("p i (c g) t -> p i c g t", g=4)
                        sp.dma_start(heads[:, :, :, g, :], n["hl"][g * HD2:(g + 1) * HD2, part, i:i + 2, :]
                                     .rearrange("p i (c t) -> p i c t", c=NC)).then_inc(done, 16)
            yield 402
            bk = st[s]["bk"]
            bk.await_emptied(sp, "g_negT")
            for i in (2, 3):
                sp.dma_start(n["stack"][STACK - 1:STACK, i], n["negT"][0:H2].rearrange("p a b -> p (a b)")).then_inc(done, 16)

        PIECE = 512
        pieces = []
        for which in range(E // (BATCH // STREAMS)):
            for name, width in (("1", HF), ("3", HF), ("2", D)):
                deep = D * HF // width // P
                step_c = max(1, PIECE // width)
                for c in range(0, deep, step_c):
                    for col in range(0, width, PIECE):
                        pieces.append((which, name, slice(c, c + step_c), slice(col, min(width, col + PIECE))))
        spread = [5 + 16 * j / len(pieces) for j in range(len(pieces))]

        def piece_of(array, turn, which, c, cols):
            return array[bass.ds(turn * (len(pieces) // 12) + which, 1)].rearrange("o (c p) n -> p (o c) n", p=P)[:, c, cols]

        def sp_weights(sp, turn):
            for j in range(len(pieces) + 2):
                yield spread[min(j, len(pieces) - 1)]
                if j < len(pieces):
                    which, name, c, cols = pieces[j]
                    if j >= 2:
                        sp.wait_ge(sem("e_low"), j - 1)
                    sp.dma_start(e_whole[:, j % 2].rearrange("p (c n) -> p c n", c=c.stop - c.start),
                                 piece_of(a["E" + name], turn, which, c, cols)).then_inc(sem(f"e_whole{j % 2}"), 16)
                if j >= 2:
                    which, name, c, cols = pieces[j - 2]
                    sp.wait_ge(sem("e_low"), j - 1)
                    for part in range(2):
                        sp.dma_start(piece_of(a["S" + name][part], turn, which, c, cols),
                                     e_parts[:, j % 2, part].rearrange("p (c n) -> p c n", c=c.stop - c.start))\
                            .then_inc(sem(f"e_parts_stored{j % 2}"), 16)

        def act_weights(act):
            for j in range(len(pieces)):
                yield spread[j]
                act.wait_ge(sem(f"e_whole{j % 2}"), 16 * (j // 2 + 1))
                if j >= 2:
                    act.wait_ge(sem(f"e_parts_stored{j % 2}"), 32 * (j // 2))
                act.copy(e_parts[:, j % 2, HIGH], e_whole[:, j % 2]).then_inc(sem("e_high"), 1)

        def pool_weights(pool):
            for j in range(len(pieces)):
                yield spread[j]
                pool.wait_ge(sem("e_high"), j + 1)
                pool.tensor_tensor(out=e_parts[:, j % 2, LOW], in0=e_whole[:, j % 2], in1=e_parts[:, j % 2, HIGH],
                                   op=ALU.subtract).then_inc(sem("e_low"), 1)

        LAYERS = (("nystrom", 0), ("dilated", 1), ("ffn", 2), ("memory", 3), ("gated", 4))[:stop]
        parts = {"pe": (pe_nystrom, pe_dilated, pe_ffn, pe_memory, pe_gated),
                 "dve": (dve_nystrom, dve_dilated, dve_ffn, dve_memory, dve_gated),
                 "act": (act_nystrom, act_dilated, act_ffn, act_memory, act_gated),
                 "pool": (pool_nystrom, pool_dilated, pool_ffn, pool_memory, pool_gated)}

        def interleaved(programs):
            due = [[0, s, g] for s, g in enumerate(programs)]
            while due:
                due.sort(key=lambda d: (d[0], d[1]))
                try:
                    stage = next(due[0][2])
                    assert stage >= due[0][0]
                    due[0][0] = stage
                except StopIteration:
                    due.pop(0)

        def chain(fns, *args):
            for f in fns[:stop]:
                yield from f(*args)

        final = "x" if stop < 5 else "y"
        key = str(stop - 1) if stop < 5 else "5"
        with nc.Fori(0, BATCH // STREAMS) as turn:
            with nc.Block() as block:
                @block.sync
                def _(sp):
                    for s in range(STREAMS):
                        tok = (turn * STREAMS + s) * T
                        sp.dma_start(x_of(s), a["xT"][:, bass.ds(tok, T)].rearrange("(c p) t -> p c t", p=P))\
                            .then_inc(sem(f"input_turned{s}"), 16)
                    for s in range(STREAMS):
                        tok = (turn * STREAMS + s) * T
                        sp.dma_start(st[s]["x"][:], a["x"][bass.ds(tok, T), :].rearrange("(t p) d -> p t d", p=P))\
                            .then_inc(sem(f"input{s}"), 16)
                    for s in range(STREAMS):
                        tok = (turn * STREAMS + s) * T
                        sp.dma_start(st[s]["ctx"][:], a["ctxT"][:, bass.ds(tok, T)].rearrange("(c p) t -> p c t", p=P))\
                            .then_inc(sem(f"context{s}"), 16)
                    if stop > 4:
                        share = ROOMS * SLOTS // (BATCH // STREAMS)
                        sp.dma_start(a["slots"][bass.ds(turn * share, share), :].rearrange("(n p) d -> p n d", p=P),
                                     zeros[:, None, :].to_broadcast([P, share // P, D])).then_inc(sem("cleared"), 16)
                        interleaved([sp_stack(sp, s) for s in range(STREAMS)] + [sp_weights(sp, turn)])
                        for i in range(2):
                            sp.wait_ge(sem(f"e_parts_stored{i}"), 32 * (len(pieces) // 2))
                    for s in range(STREAMS):
                        sp.wait_ge(sem(f"x{key}_{s}"), 1)
                        tok = (turn * STREAMS + s) * T
                        sp.dma_start(a["y"][bass.ds(tok, T), :].rearrange("(t p) d -> p t d", p=P), st[s][final][:])\
                            .then_inc(sem(f"stored{s}"), 16)
                    for s in range(STREAMS):
                        sp.wait_ge(sem(f"stored{s}"), 16)
                    if stop > 4:
                        sp.wait_ge(sem("cleared"), 16)

                @block.tensor
                def _(pe):
                    interleaved([chain(parts["pe"], pe, s) for s in range(STREAMS)])

                @block.vector
                def _(dve):
                    links = 0
                    dve_link = sem("dve_link")

                    def link(ins):
                        nonlocal links
                        links += 1
                        ins.then_inc(dve_link, 1)
                        dve.wait_ge(dve_link, links)

                    interleaved([chain(parts["dve"], dve, s, link) for s in range(STREAMS)])

                @block.scalar
                def _(act):
                    interleaved([chain(parts["act"], act, s) for s in range(STREAMS)]
                                + [act_weights(act)] * (stop > 4))

                @block.gpsimd
                def _(pool):
                    interleaved([chain(parts["pool"], pool, s) for s in range(STREAMS)]
                                + [pool_weights(pool)] * (stop > 4))
            counters = [x for x in sems.values() if x.name[:4] != "load" and x.name[:5] != "setup"]

            def clear(engine, share):
                for x in counters[share::5]:
                    engine.sem_clear(x)

            with nc.Block() as block:
                @block.sync
                def _(sp):
                    clear(sp, 0)

                @block.tensor
                def _(pe):
                    clear(pe, 1)

                @block.vector
                def _(dve):
                    clear(dve, 2)

                @block.scalar
                def _(act):
                    clear(act, 3)

                @block.gpsimd
                def _(pool):
                    clear(pool, 4)

        with nc.Block() as block:
            @block.sync
            def _(sp):
                for x in sems.values():
                    if x.name[:4] == "load" or x.name[:5] == "setup":
                        sp.sem_clear(x)


TOK = BATCH * T
TT = TOK // P
TOPK = 2
SLOTS = 256
SHIFT = 8
TILES = (TOK * TOPK + E * (SLOTS - 1)) // SLOTS
ROOMS = TILES + TILES % 2
TURNS = TILES // 2
ST = SLOTS // P


def experts_kernel(nc, a):
    ctx = ExitStack()
    with ctx:
        def sb(name, shape, dt=F32):
            return ctx.enter_context(nc.sbuf_tensor(name, shape, dt))

        def sem(name):
            return ctx.enter_context(nc.semaphore(name))

        I32 = mybir.dt.int32
        U32 = mybir.dt.uint32
        x = sb("m_x", [P, TT, D])
        xs = sb("m_xs", [P, TOPK, TT, D])
        xT = sb("m_xT", [P, NC, TOK])
        wg = sb("m_wg", [P, NC, E])
        bg = sb("m_bg", [P, E])
        ident = sb("m_ident", [P, P])
        tri = sb("m_tri", [P, P], BF16)
        ones = sb("m_ones", [P, P], BF16)
        eids = sb("m_eids", [P, E])
        jids = sb("m_jids", [P, TILES])
        lg = sb("m_lg", [P, TT, E])
        top = sb("m_top", [P, TT, E])
        topi = sb("m_topi", [P, TT, E], U32)
        topf = sb("m_topf", [P, TT, TOPK])
        wts = sb("m_wts", [P, TOPK, TT])
        tmp = sb("m_tmp", [P, 4, TT])
        hit = sb("m_hit", [P, TOPK, TT, E])
        sel = sb("m_sel", [P, TT, E])
        selb = sb("m_selb", [P, TT, E], BF16)
        cum = sb("m_cum", [P, 2, TT, E])
        pre = sb("m_pre", [P, TT, E])
        cnt = sb("m_cnt", [P, 8, E])
        cnti = sb("m_cnti", [P, 2, E], I32)
        posf = sb("m_posf", [P, TOPK, TT])
        posi = sb("m_posi", [P, TOPK, TT], U32)
        tile_e = sb("m_tile_e", [P, TILES, E])
        tef = sb("m_tef", [P, TILES])
        tei = sb("m_tei", [P, TILES], I32)

        bank = [ctx.enter_context(nc.psum_tensor(f"m_bank{i}", [P, 512], F32)) for i in range(8)]
        loaded, routed, step, soft = sem("m_loaded"), sem("m_routed"), sem("m_step"), sem("m_soft")
        pe_done, act_done = sem("m_pe"), sem("m_act")
        scaled, positions, sent = sem("m_scaled"), sem("m_positions"), sem("m_sent")

        loads = [(x[:], a["x5"].rearrange("(t p) d -> p t d", p=P)),
                 (wg[:], a["Wg"].rearrange("(c p) e -> p c e", p=P)), (bg[:], a["R_bg"]),
                 (ident[:], a["C_ident"]), (tri[:], a["C_tri"]), (ones[:], a["C_onesb"]),
                 (eids[:], a["C_eids"]), (jids[:], a["C_jids"])]

        w1 = [sb(f"e_w1_{i}", [P, 2, NC, HF], BF16) for i in range(2)]
        w3 = [sb(f"e_w3_{i}", [P, 2, NC, HF], BF16) for i in range(2)]
        w2 = [xT[:, i, :].bitcast(BF16).rearrange("p (b f d) -> p b f d", b=2, d=D) for i in range(2)]
        xe = [sb(f"e_x{i}", [P, ST, D]) for i in range(2)]
        xeT = [sb(f"e_xT{i}", [P, 2, NC, SLOTS], BF16) for i in range(2)]
        h32 = [sb(f"e_h32_{i}", [P, SLOTS]) for i in range(4)]
        h = [sb(f"e_h{i}", [P, 2, HF // P, SLOTS], BF16) for i in range(2)]
        silu = [sb(f"e_silu{i}", [P, SLOTS]) for i in range(4)]
        yo = [sb(f"e_y{i}", [P, ST, D]) for i in range(2)]
        wl = [sem(f"e_weights13_{i}") for i in range(2)]
        w2l = [sem(f"e_weights2_{i}") for i in range(2)]
        xl = [sem(f"e_rows{i}") for i in range(2)]
        tf = [sem(f"e_turned{i}") for i in range(2)]
        th = [sem(f"e_turned_high{i}") for i in range(2)]
        te = [sem(f"e_turned_low{i}") for i in range(2)]
        hf = [sem(f"e_hidden{i}") for i in range(4)]
        sd = [sem(f"e_silu{i}") for i in range(4)]
        hr = [sem(f"e_gated{i}") for i in range(4)]
        hh = [sem(f"e_hidden_high{i}") for i in range(4)]
        hl = [sem(f"e_hidden_low{i}") for i in range(4)]
        yf = [sem(f"e_answer{i}") for i in range(2)]
        ye = [sem(f"e_answer_sbuf{i}") for i in range(2)]
        ys = [sem(f"e_stored{i}") for i in range(2)]
        FE = HF // P

        with nc.Block() as block:
            @block.sync
            def _(sp):
                for dst, src in loads:
                    sp.dma_start(dst, src).then_inc(loaded, 16)

            @block.tensor
            def _(pe):
                pe.wait_ge(loaded, 16 * len(loads))
                for t in range(TT):
                    if t >= 4:
                        pe.wait_ge(act_done, t - 3)
                    for c in range(NC):
                        last = pe.transpose(bank[t % 4][:, c * P:(c + 1) * P], x[:, t, c * P:(c + 1) * P], ident[:])
                    last.then_inc(pe_done, 1)
                pe.wait_ge(act_done, TT)
                for t in range(TT):
                    for c in range(NC):
                        last = pe.matmul(bank[4][:, t * E:(t + 1) * E], xT[:, c, t * P:(t + 1) * P], wg[:, c, :],
                                         start=c == 0, stop=c == NC - 1)
                last.then_inc(pe_done, 1)
                pe.wait_ge(routed, 1)
                pe.matmul(bank[5][:, 0:TT * E], tri[:], selb[:].rearrange("p t e -> p (t e)"), start=True, stop=True)
                pe.matmul(bank[6][:, 0:TT * E], ones[:], selb[:].rearrange("p t e -> p (t e)"), start=True, stop=True)\
                    .then_inc(pe_done, 1)

            @block.scalar
            def _(act):
                for t in range(TT):
                    act.wait_ge(pe_done, t + 1)
                    act.copy(xT[:, :, t * P:(t + 1) * P], bank[t % 4][:, 0:D].rearrange("p (c t) -> p c t", c=NC))\
                        .then_inc(act_done, 1)
                act.wait_ge(soft, 1)
                act.activation(tmp[:, 1, :], tmp[:, 0, :], ACT.Exp).then_inc(soft, 1)

            @block.vector
            def _(dve):
                n = 0

                def link(ins):
                    nonlocal n
                    n += 1
                    ins.then_inc(step, 1)
                    dve.wait_ge(step, n)

                dve.wait_ge(pe_done, TT + 1)
                link(dve.tensor_tensor(lg[:], bank[4][:, 0:TT * E].rearrange("p (t e) -> p t e", e=E),
                                       bg[:, None, :].to_broadcast([P, TT, E]), ALU.add))
                for t in range(TT):
                    last = dve.max(top[:, t, :], lg[:, t, :])
                link(last)
                for t in range(TT):
                    last = dve.max_index(topi[:, t, :], top[:, t, :], lg[:, t, :])
                link(last)
                dve.tensor_tensor(tmp[:, 0, :], top[:, :, 1], top[:, :, 0], ALU.subtract).then_inc(soft, 1)
                link(dve.tensor_copy(topf[:], topi[:, :, 0:TOPK]))
                for k in range(TOPK):
                    last = dve.tensor_tensor(hit[:, k], topf[:, :, k, None].to_broadcast([P, TT, E]),
                                             eids[:, None, :].to_broadcast([P, TT, E]), ALU.is_equal)
                link(last)
                link(dve.tensor_tensor(sel[:], hit[:, 0], hit[:, 1], ALU.add))
                dve.tensor_copy(selb[:], sel[:]).then_inc(routed, 1)
                dve.wait_ge(soft, 2)
                link(dve.tensor_scalar(tmp[:, 2, :], tmp[:, 1, :], 1.0, None, ALU.add))
                link(dve.reciprocal(wts[:, 0, :], tmp[:, 2, :]))
                link(dve.tensor_tensor(wts[:, 1, :], tmp[:, 1, :], wts[:, 0, :], ALU.mult))
                for k in range(TOPK):
                    for t in range(TT):
                        last = dve.tensor_scalar(xs[:, k, t, :], x[:, t, :], wts[:, k, t:t + 1], None, ALU.mult)
                last.then_inc(scaled, 1)
                dve.wait_ge(pe_done, TT + 2)
                link(dve.tensor_copy(cum[:, 0], bank[6][:, 0:TT * E].rearrange("p (t e) -> p t e", e=E)))
                at, d = 0, 1
                while d < TT:
                    dve.tensor_copy(cum[:, 1 - at, 0:d], cum[:, at, 0:d])
                    link(dve.tensor_tensor(cum[:, 1 - at, d:TT], cum[:, at, d:TT], cum[:, at, 0:TT - d], ALU.add))
                    at, d = 1 - at, 2 * d
                total = cum[:, at, TT - 1, :]
                link(dve.tensor_tensor(pre[:], cum[:, at], bank[6][:, 0:TT * E].rearrange("p (t e) -> p t e", e=E),
                                       ALU.subtract))
                link(dve.tensor_tensor(pre[:], pre[:], bank[5][:, 0:TT * E].rearrange("p (t e) -> p t e", e=E), ALU.add))
                link(dve.tensor_scalar(cnt[:, 0, :], total, float(SLOTS - 1), None, ALU.add))
                link(dve.tensor_copy(cnti[:, 0, :], cnt[:, 0, :]))
                link(dve.tensor_scalar(cnti[:, 1, :], cnti[:, 0, :], SHIFT, None, ALU.arith_shift_right))
                link(dve.tensor_copy(cnt[:, 1, :], cnti[:, 1, :]))
                k, d = 2, 1
                link(dve.tensor_copy(cnt[:, 2, :], cnt[:, 1, :]))
                while d < E:
                    dve.tensor_copy(cnt[:, k + 1, 0:d], cnt[:, k, 0:d])
                    link(dve.tensor_tensor(cnt[:, k + 1, d:E], cnt[:, k, d:E], cnt[:, k, 0:E - d], ALU.add))
                    k, d = k + 1, 2 * d
                link(dve.tensor_tensor(cnt[:, 6, :], cnt[:, k, :], cnt[:, 1, :], ALU.subtract))
                link(dve.tensor_scalar(cnt[:, 7, :], cnt[:, 6, :], float(SLOTS), None, ALU.mult))
                link(dve.tensor_tensor(pre[:], pre[:], cnt[:, 7, None, :].to_broadcast([P, TT, E]), ALU.add))
                for j in range(TOPK):
                    last = dve.tensor_tensor(hit[:, j], hit[:, j], pre[:], ALU.mult)
                link(last)
                link(dve.tensor_reduce(posf[:].rearrange("p k t -> p (k t)"), hit[:].rearrange("p k t e -> p (k t) e"),
                                       axis=AX.X, op=ALU.add))
                link(dve.tensor_tensor(tile_e[:], jids[:, :, None].to_broadcast([P, TILES, E]),
                                       cnt[:, k, None, :].to_broadcast([P, TILES, E]), ALU.is_ge))
                link(dve.tensor_reduce(tef[:], tile_e[:], axis=AX.X, op=ALU.add))
                link(dve.tensor_scalar(tef[:], tef[:], float(E - 1), None, ALU.min))
                dve.tensor_copy(tei[:], tef[:])
                dve.tensor_copy(posi[:], posf[:]).then_inc(positions, 1)

            @block.gpsimd
            def _(pool):
                for i in range(2):
                    pool.memset(yo[i][:], 0.0).then_inc(yf[i], 1)
                    pool.memset(xeT[i][:], 0.0).then_inc(te[i], 1)
                    pool.memset(h[i][:, 0], 0.0).then_inc(ye[i], 1)
                    pool.memset(h[i][:, 1], 0.0).then_inc(ys[i], 16)
                for i in range(4):
                    pool.memset(silu[i][:], 0.0).then_inc(hr[i], 1)
                    pool.memset(h32[i][:], 0.0).then_inc(hl[i], 4)

        with nc.Block() as block:
            @block.gpsimd
            def _(pool):
                pool.wait_ge(scaled, 1)
                pool.wait_ge(positions, 1)
                for k in range(TOPK):
                    for t in range(TT):
                        pool.indirect_dma_start(out=a["slots"], out_offset=bass.IndirectOffsetOnAxis(posi[:, k, t:t + 1], 0),
                                                in_=xs[:, k, t, :], in_offset=None).then_inc(sent, 16)
                pool.wait_ge(sent, 16 * TOPK * TT)

            @block.sync
            def _(sp):
                def turn(i, tiles):
                    expert = [sp.value_load(tei[0:1, bass.ds(i * 2 + u, 1)], min_val=0, max_val=E - 1) for u in tiles]

                    def weights(dst, src, u, loaded):
                        for part in range(2):
                            sp.dma_start(dst[u][:, part], src[part][bass.ds(expert[u], 1)]
                                         .rearrange("o (c p) n -> p (o c) n", p=P)).then_inc(loaded[u], 16)

                    for u in tiles:
                        sp.wait_ge(hl[3], i * 4 + 2 * u + 2)
                        weights(w1, a["S1"], u, wl)
                        weights(w3, a["S3"], u, wl)
                        sp.wait_ge(te[u], i + 1)
                        sp.wait_ge(sent, 16 * TOPK * TT)
                        sp.dma_start(xe[u][:], a["slots"][bass.ds((i * 2 + u) * SLOTS, SLOTS), :]
                                     .rearrange("(t p) d -> p t d", p=P)).then_inc(xl[u], 16)
                    for u in tiles:
                        sp.wait_ge(yf[u], i + 1)
                        weights(w2, a["S2"], u, w2l)

                with sp.Fori(0, TURNS) as i:
                    turn(i, range(2))
                if TILES % 2:
                    turn(TURNS, range(1))

            @block.tensor
            def _(pe):
                def turn(i, tiles):
                    for u in tiles:
                        pe.wait_ge(xl[u], i * 16 + 16)
                        pe.wait_ge(te[u], i + 1)
                        for c in range(NC):
                            for t in range(ST):
                                last = pe.transpose(bank[4 + u][:, c * SLOTS + t * P:c * SLOTS + (t + 1) * P],
                                                    xe[u][:, t, c * P:(c + 1) * P], ident[:])
                        last.then_inc(tf[u], 1)
                    for u in tiles:
                        pe.wait_ge(te[u], i + 2)
                        pe.wait_ge(wl[u], i * 64 + 64)
                        for f in range(FE):
                            b = f % 4
                            pe.wait_ge(hr[b], i * 4 + 2 * u + f // 4 + 1)
                            for col, w in ((0, w1[u]), (SLOTS, w3[u])):
                                terms = [(c, *term) for c in range(NC) for term in TERMS]
                                for j, (c, wp, xp) in enumerate(terms):
                                    last = pe.matmul(bank[b][:, col:col + SLOTS], w[:, wp, c, f * P:(f + 1) * P],
                                                     xeT[u][:, xp, c, :], start=j == 0, stop=j == len(terms) - 1)
                            last.then_inc(hf[b], 1)
                    for u in tiles:
                        pe.wait_ge(ye[u], i + 1)
                        for b in range(4):
                            pe.wait_ge(hl[b], i * 4 + 2 * u + 6)
                        pe.wait_ge(w2l[u], i * 32 + 32)
                        for t in range(ST):
                            terms = [(f, *term) for f in range(FE) for term in TERMS]
                            for j, (f, hp, wp) in enumerate(terms):
                                last = pe.matmul(bank[6 + u][:, t * D:(t + 1) * D], h[u][:, hp, f, t * P:(t + 1) * P],
                                                 w2[u][:, wp, f, :], start=j == 0, stop=j == len(terms) - 1)
                        last.then_inc(yf[u], 1)

                with pe.Fori(0, TURNS) as i:
                    turn(i, range(2))
                if TILES % 2:
                    turn(TURNS, range(1))

            @block.scalar
            def _(act):
                def turn(i, tiles):
                    for u in tiles:
                        act.wait_ge(tf[u], i + 1)
                        act.copy(xeT[u][:, HIGH].rearrange("p c s -> p (c s)"), bank[4 + u][:]).then_inc(th[u], 1)

                    def high(u, f):
                        b = f % 4
                        act.wait_ge(hr[b], i * 4 + 2 * u + f // 4 + 2)
                        act.copy(h[u][:, HIGH, f, :], h32[b][:]).then_inc(hh[b], 1)

                    for u in tiles:
                        for f in range(FE):
                            b = f % 4
                            act.wait_ge(hf[b], i * 4 + 2 * u + f // 4 + 1)
                            act.activation(silu[b][:], bank[b][:, 0:SLOTS], ACT.Silu).then_inc(sd[b], 1)
                            if f:
                                high(u, f - 1)
                        high(u, FE - 1)
                    for u in tiles:
                        act.wait_ge(yf[u], i + 2)
                        act.wait_ge(ys[u], i * 16 + 16)
                        act.copy(yo[u][:].rearrange("p t d -> p (t d)"), bank[6 + u][:]).then_inc(ye[u], 1)
                        act.wait_ge(ye[u], i + 2)
                        act.dma_start(a["back"][bass.ds((i * 2 + u) * SLOTS, SLOTS), :].rearrange("(t p) d -> p t d", p=P),
                                      yo[u][:]).then_inc(ys[u], 16)

                with act.Fori(0, TURNS) as i:
                    turn(i, range(2))
                if TILES % 2:
                    turn(TURNS, range(1))
                for u in range(2):
                    act.wait_ge(ys[u], 16 * ((TILES + 1 - u) // 2) + 16)

            @block.vector
            def _(dve):
                def turn(i, tiles):
                    for u in tiles:
                        dve.wait_ge(th[u], i + 1)
                        dve.tensor_tensor(xeT[u][:, LOW].rearrange("p c s -> p (c s)"), bank[4 + u][:],
                                          xeT[u][:, HIGH].rearrange("p c s -> p (c s)"), ALU.subtract).then_inc(te[u], 1)

                    def low(u, f):
                        b = f % 4
                        dve.wait_ge(hh[b], i * 4 + 2 * u + f // 4 + 1)
                        dve.tensor_tensor(h[u][:, LOW, f, :], h32[b][:], h[u][:, HIGH, f, :], ALU.subtract)\
                            .then_inc(hl[b], 1)

                    for u in tiles:
                        for f in range(FE):
                            b = f % 4
                            dve.wait_ge(sd[b], i * 4 + 2 * u + f // 4 + 1)
                            dve.tensor_tensor(h32[b][:], bank[b][:, SLOTS:2 * SLOTS], silu[b][:], ALU.mult)\
                                .then_inc(hr[b], 1)
                            if f:
                                low(u, f - 1)
                        low(u, FE - 1)

                with dve.Fori(0, TURNS) as i:
                    turn(i, range(2))
                if TILES % 2:
                    turn(TURNS, range(1))

        QUARTERS = 4
        q = TT // QUARTERS
        fetched = [sem(f"m_fetched{i}") for i in range(QUARTERS)]
        summed, normed = sem("m_summed"), sem("m_normed")
        halved = sem("m_half")
        vend, ready, out_done = sem("m_variance"), sem("m_rstd"), sem("m_out")
        stt, mv, ve, rstd, half = (sb("m_st", [P, TT, 6]), sb("m_mv", [P, TT, 2]), sb("m_ve", [P, TT]),
                                   sb("m_rstd", [P, TT]), sb("m_halves", [P, TT]))
        with nc.Block() as block:
            @block.gpsimd
            def _(pool):
                pool.memset(half[:], -0.5).then_inc(halved, 1)
                pool.wait_ge(halved, 1)
                for i in range(QUARTERS + 1):
                    if i < QUARTERS:
                        for t in range(i * q, (i + 1) * q):
                            for k in range(TOPK):
                                pool.indirect_dma_start(out=xs[:, k, t, :], out_offset=None, in_=a["back"],
                                                        in_offset=bass.IndirectOffsetOnAxis(posi[:, k, t:t + 1], 0))\
                                    .then_inc(fetched[i], 16)
                    if i:
                        r = slice((i - 1) * q, i * q)
                        pool.wait_ge(vend, i)
                        pool.tensor_tensor(out=rstd[:, r], in0=ve[:, r], in1=half[:, r], op=ALU.pow).then_inc(ready, 1)

            @block.vector
            def _(dve):
                n = 0

                def link(ins):
                    nonlocal n
                    n += 1
                    ins.then_inc(summed, 1)
                    dve.wait_ge(summed, n)

                def normalize(i):
                    dve.wait_ge(ready, i + 1)
                    for t in range(i * q, (i + 1) * q):
                        dve.tensor_scalar(xs[:, 0, t, :], xs[:, 0, t, :], mv[:, t, 0:1], rstd[:, t:t + 1],
                                          ALU.subtract, ALU.mult).then_inc(normed, 1)

                for i in range(QUARTERS):
                    r = slice(i * q, (i + 1) * q)
                    dve.wait_ge(fetched[i], 16 * TOPK * q)
                    link(dve.tensor_tensor(xs[:, 0, r], xs[:, 0, r], xs[:, 1, r], ALU.add))
                    link(dve.scalar_tensor_tensor(xs[:, 0, r], x[:, r], 2.0, xs[:, 0, r], ALU.mult, ALU.add))
                    for t in range(i * q, (i + 1) * q):
                        last = dve.bn_stats(stt[:, t, :], xs[:, 0, t, :])
                    link(last)
                    for t in range(i * q, (i + 1) * q):
                        last = dve.bn_aggr(mv[:, t, :], stt[:, t, :])
                    link(last)
                    dve.tensor_scalar(ve[:, r], mv[:, r, 1], EPS, None, ALU.add).then_inc(vend, 1)
                    if i:
                        normalize(i - 1)
                normalize(QUARTERS - 1)

            @block.sync
            def _(sp):
                for i in range(QUARTERS):
                    sp.wait_ge(normed, (i + 1) * q)
                    sp.dma_start(a["y"][i * q * P:(i + 1) * q * P, :].rearrange("(t p) d -> p t d", p=P),
                                 xs[:, 0, i * q:(i + 1) * q, :]).then_inc(out_done, 16)
                sp.wait_ge(out_done, 16 * QUARTERS)


def lay_out(i):
    f = lambda n: np.asarray(i[n])
    e = 3
    cols = lambda b: np.ascontiguousarray(b.reshape(-1, P).T)
    rep = lambda b: np.ascontiguousarray(np.broadcast_to(b.reshape(1, -1), (P, b.size)))
    a = {}
    x, c = f("x").reshape(-1, D), f("ctx_1024").reshape(-1, D)
    a["x"], a["xT"], a["ctxT"] = x, x.T, c.T
    g = lambda n: f("L1_xattn_" + n)[e]
    a["W_qkv"], a["W_out"] = f("L0_attn_Wqkv"), f("L0_attn_Wout")
    for n in "qkvo":
        a["W_d" + n] = f("L0_xattn_W" + n).T
    a["W_ff1"], a["W_ff2"] = f("L0_ffn_W1").T, f("L0_ffn_W2").T
    a["W_mw"], a["W_mr"] = f("L1_attn_W_write").T, f("L1_attn_W_read").T
    for n in ("qa", "ka", "qt", "kt"):
        a["W_" + n], a["B_" + n] = g("W_" + n).T, cols(g("b_" + n))
    a["W_va"], a["W_vt"], a["W_go"], a["W_gf"] = g("W_va").T, g("W_vt").T, g("W_o").T, g("W_ffn").T
    bq = f("L0_attn_bqkv")
    a["B_q0"], a["B_k0"], a["R_v0"] = cols(bq[:D]), cols(bq[D:2 * D]), rep(bq[2 * D:])
    a["R_o0"] = rep(f("L0_attn_bout"))
    a["B_dq"], a["B_dk"], a["R_dv"], a["R_do"] = (cols(f("L0_xattn_bq")), cols(f("L0_xattn_bk")),
                                                  rep(f("L0_xattn_bv")), rep(f("L0_xattn_bo")))
    a["B_ff1"], a["R_ff2"] = cols(f("L0_ffn_b1")), rep(f("L0_ffn_b2"))
    a["B_decay"], a["B_alpha"] = rep(f("L1_attn_decay")), rep(f("L1_attn_log_alpha"))
    a["R_va"], a["R_vt"], a["R_go"], a["R_gf"] = rep(g("b_va")), rep(g("b_vt")), rep(g("b_o")), rep(g("b_ffn"))
    a["B_gamma"], a["B_beta"] = cols(g("gamma")), cols(g("beta"))
    a["B_gate"] = rep(f("L1_xattn_gating_factor")[e:e + 1])
    a["Wg"], a["R_bg"] = f("L1_ffn_Wg"), rep(f("L1_ffn_bg"))
    a["E1"], a["E2"], a["E3"] = f("L1_ffn_W1"), f("L1_ffn_W2"), f("L1_ffn_W3")
    for group, names in GROUPS.items():
        a["W_" + group] = np.concatenate([a.pop("W_" + n) for n in names], 1)
    a["B"] = np.concatenate([a.pop("B_" + n) for n in COLUMNS], 1)
    a["R"] = np.concatenate([a.pop("R_" + n) for n in ROWS], 1)
    tables = shape_constants()
    for group, names in constant_groups(tables).items():
        a["C_" + group] = np.concatenate([tables[n] for n in names], 1)
    for n in ("ident",) + ROUTING:
        a["C_" + n] = tables[n]
    return {n: np.ascontiguousarray(t) for n, t in a.items()}


def build(nc, a, y):
    tokens = nc.dram_tensor("tokens", (TOK, D), F32, kind="Internal").ap()
    slots = nc.dram_tensor("slots", (ROOMS * SLOTS, D), F32, kind="Internal").ap()
    back = nc.dram_tensor("back", (TILES * SLOTS, D), F32, kind="Internal").ap()
    a = {**a, **{f"S{i}": [nc.dram_tensor(f"parts{i}_{part}", a[f"E{i}"].shape, BF16, kind="Internal").ap()
                           for part in range(2)] for i in (1, 2, 3)}}
    layers_kernel(nc, {**a, "y": tokens, "slots": slots}, 5)
    experts_kernel(nc, {**a, "x5": tokens, "slots": slots, "back": back, "y": y})


def kernel(**inputs):
    import concourse.bacc as _bacc
    from concourse.bass_utils import run_bass_kernel_spmd as _run

    nc = _bacc.Bacc("TRN2", target_bir_lowering=False, num_devices=1)
    arrays = lay_out(inputs)
    args = {n: nc.dram_tensor(n, t.shape, mybir.dt.from_np(t.dtype), kind="ExternalInput").ap()
            for n, t in arrays.items()}
    y = nc.dram_tensor("y_out", (TOK, D), F32, kind="ExternalOutput").ap()
    build(nc, args, y)
    r = _run(nc, [arrays], core_ids=[0])
    return r.results[0]["y_out"].reshape(BATCH, T, D)
```
